# Optimizing a Trainium2 kernel written in Bass

```python
import numpy as np
import jax
import jax.numpy as jnp

def _softmax(x, axis=-1):
    return jax.nn.softmax(x, axis=axis)

def _gelu(x):
    return jax.nn.gelu(x, approximate=True)

def _silu(x):
    return jax.nn.silu(x)

def _sigmoid(x):
    return jax.nn.sigmoid(x)

def _layernorm(x, axis=-1, eps=1e-05):
    m = jnp.mean(x, axis=axis, keepdims=True)
    v = jnp.var(x, axis=axis, keepdims=True)
    return (x - m) / jnp.sqrt(v + eps)

def _scatter_add(tgt, idx, src, axis=0):
    return tgt.at[idx].add(src)

def _segment_sum(src, seg, n):
    return jax.ops.segment_sum(src, seg, n)
kernel_name = 'mk_flamingo_gated_d1_seqx_r4_91ec28'

def setup_inputs(seed: int=0):
    np.random.seed(seed)
    _w = jnp.asarray

    def _rec_inputs():
        import jax
        import jax.numpy as jnp
        _rk = jax.random.key(seed)
        x = 2.818e-05 + 1 * jax.random.normal(jax.random.fold_in(_rk, 1), (4, 512, 512), jnp.float32)
        _lenS = 512 - jax.random.randint(jax.random.fold_in(_rk, 7), (4,), 0, max(1, 512 // 4) + 1, jnp.int32)
        _lenS2 = 512 - jax.random.randint(jax.random.fold_in(_rk, 8), (4,), 0, max(1, 512 // 4) + 1, jnp.int32)
        _ctx_1024P = jax.random.normal(jax.random.fold_in(_rk, 11), (4, 16, 256), jnp.float32)
        _ctx_1024c = jax.random.dirichlet(jax.random.fold_in(_rk, 511), 0.3 * jnp.ones((16,), jnp.float32), (4, 512))
        _ctx_1024t = jnp.einsum('bsk,bkd->bsd', _ctx_1024c, _ctx_1024P)
        _ctx_1024t = _ctx_1024t * jax.lax.rsqrt(jnp.mean(jnp.square(_ctx_1024t)) + 1e-12) * 0.953939
        ctx_1024 = 7.22013e-05 + 1.00017 * (_ctx_1024t + 0.3 * jax.random.normal(jax.random.fold_in(_rk, 611), (4, 512, 256), jnp.float32))
        _g = jax.random.normal(jax.random.fold_in(_rk, 9001), (2, 1), jnp.float32)
        _g = jnp.sign(_g) * jnp.maximum(jnp.abs(_g), 1.0) + (_g == 0) * 1.0
        g_xattn = _g[0]
        g_ffn = _g[1]
        return (x, ctx_1024, g_xattn, g_ffn)
    x, ctx_1024, g_xattn, g_ffn = _rec_inputs()

    def _L0_xattn_setup():
        import jax, jax.numpy as jnp
        import numpy as np
        B_, L_, D_MODEL = (4, 512, 256)
        D_STATE, D_CONV, EXPAND = (16, 4, 2)
        D_INNER = EXPAND * D_MODEL
        DT_RANK = (D_MODEL + 15) // 16

        def silu(x):
            return x * jax.nn.sigmoid(x)
        key = jax.random.key(seed)
        ks = jax.random.split(key, 10)
        f32 = jnp.float32
        hidden_states = jax.random.normal(ks[0], (B_, L_, D_MODEL), dtype=f32)
        z = jax.random.normal(ks[1], (B_, D_INNER, L_), dtype=f32)
        in_proj_w = jax.random.normal(ks[2], (D_INNER, D_MODEL), dtype=f32) * 0.02
        conv_w = jax.random.normal(ks[3], (D_INNER, 1, D_CONV), dtype=f32) * 0.1
        conv_b = jax.random.normal(ks[4], (D_INNER,), dtype=f32) * 0.02
        x_proj_w = jax.random.normal(ks[5], (DT_RANK + 2 * D_STATE, D_INNER), dtype=f32) * 0.02
        dt_proj_w = jax.random.uniform(ks[6], (D_INNER, DT_RANK), dtype=f32, minval=-DT_RANK ** (-0.5), maxval=DT_RANK ** (-0.5))
        dt = jnp.exp(jax.random.uniform(ks[7], (D_INNER,), dtype=f32, minval=np.log(0.001), maxval=np.log(0.1)))
        dt_proj_b = jnp.log(jnp.expm1(dt))
        A_log = jnp.log(jnp.broadcast_to(jnp.arange(1, D_STATE + 1, dtype=f32), (D_INNER, D_STATE)))
        D = jnp.ones((D_INNER,), f32)
        return {'hidden_states': hidden_states, 'z': z, 'in_proj_w': in_proj_w, 'conv_w': conv_w, 'conv_b': conv_b, 'x_proj_w': x_proj_w, 'dt_proj_w': dt_proj_w, 'dt_proj_b': dt_proj_b, 'A_log': A_log, 'D': D}
    _L0_xattn_all = _L0_xattn_setup()
    _L0_xattn_in = {k: v for k, v in _L0_xattn_all.items() if k in ('in_proj_w', 'conv_w', 'conv_b', 'x_proj_w', 'dt_proj_w', 'dt_proj_b', 'A_log', 'D')}
    del _L0_xattn_all

    def _L0_ffn_setup():
        import jax, jax.numpy as jnp
        import numpy as np
        H = 512
        I = 352
        E = 16
        K = 2
        SI = I * 2

        def _swiglu(gu, inter):
            g, u = (gu[..., :inter], gu[..., inter:])
            return jax.nn.silu(g) * u
        key = jax.random.key(seed)
        ks = jax.random.split(key, 6)
        s = 0.02
        hidden_states = jax.random.normal(ks[0], (1, 256, H), dtype=jnp.float32)
        gate_w = jax.random.normal(ks[1], (E, H), dtype=jnp.float32) * s
        w_gate_up = jax.random.normal(ks[2], (E, H, 2 * I), dtype=jnp.float32) * s
        w_down = jax.random.normal(ks[3], (E, I, H), dtype=jnp.float32) * s
        shared_gate_up = jax.random.normal(ks[4], (H, 2 * SI), dtype=jnp.float32) * s
        shared_down = jax.random.normal(ks[5], (SI, H), dtype=jnp.float32) * s
        return {'hidden_states': hidden_states, 'gate_w': gate_w, 'w_gate_up': w_gate_up, 'w_down': w_down, 'shared_gate_up': shared_gate_up, 'shared_down': shared_down}
    _L0_ffn_all = _L0_ffn_setup()
    _L0_ffn_in = {k: v for k, v in _L0_ffn_all.items() if k in ('gate_w', 'w_gate_up', 'w_down', 'shared_gate_up', 'shared_down')}
    del _L0_ffn_all
    return {'x': x, 'ctx_1024': ctx_1024, 'g_xattn': g_xattn, 'g_ffn': g_ffn, 'L0_xattn_in_proj_w': _L0_xattn_in['in_proj_w'], 'L0_xattn_conv_w': _L0_xattn_in['conv_w'], 'L0_xattn_conv_b': _L0_xattn_in['conv_b'], 'L0_xattn_x_proj_w': _L0_xattn_in['x_proj_w'], 'L0_xattn_dt_proj_w': _L0_xattn_in['dt_proj_w'], 'L0_xattn_dt_proj_b': _L0_xattn_in['dt_proj_b'], 'L0_xattn_A_log': _L0_xattn_in['A_log'], 'L0_xattn_D': _L0_xattn_in['D'], 'L0_ffn_gate_w': _L0_ffn_in['gate_w'], 'L0_ffn_w_gate_up': _L0_ffn_in['w_gate_up'], 'L0_ffn_w_down': _L0_ffn_in['w_down'], 'L0_ffn_shared_gate_up': _L0_ffn_in['shared_gate_up'], 'L0_ffn_shared_down': _L0_ffn_in['shared_down']}

def reference(x, ctx_1024, g_xattn, g_ffn, L0_xattn_in_proj_w, L0_xattn_conv_w, L0_xattn_conv_b, L0_xattn_x_proj_w, L0_xattn_dt_proj_w, L0_xattn_dt_proj_b, L0_xattn_A_log, L0_xattn_D, L0_ffn_gate_w, L0_ffn_w_gate_up, L0_ffn_w_down, L0_ffn_shared_gate_up, L0_ffn_shared_down):
    import jax
    import jax.numpy as jnp

    def _L0_xattn_ref(hidden_states, z, in_proj_w, conv_w, conv_b, x_proj_w, dt_proj_w, dt_proj_b, A_log, D):
        import jax, jax.numpy as jnp
        import numpy as np
        B_, L_, D_MODEL = (4, 512, 256)
        D_STATE, D_CONV, EXPAND = (16, 4, 2)
        D_INNER = EXPAND * D_MODEL
        DT_RANK = (D_MODEL + 15) // 16

        def silu(x):
            return x * jax.nn.sigmoid(x)
        Bsz, L, _ = hidden_states.shape
        d_inner, _, d_conv = conv_w.shape
        dt_rank = dt_proj_w.shape[1]
        d_state = A_log.shape[1]
        x = jnp.einsum('bld,ed->bel', hidden_states, in_proj_w)
        xc = jax.lax.conv_general_dilated(x, conv_w, window_strides=(1,), padding=[(d_conv - 1, 0)], feature_group_count=d_inner, dimension_numbers=('NCH', 'OIH', 'NCH'))
        x = silu(xc + conv_b[None, :, None])
        x_dbl = jnp.einsum('bdl,ed->bel', x, x_proj_w)
        dt_low, Bm, Cm = jnp.split(x_dbl, [dt_rank, dt_rank + d_state], axis=1)
        dt = jnp.einsum('brl,dr->bdl', dt_low, dt_proj_w)
        dt = jax.nn.softplus(dt + dt_proj_b[None, :, None])
        A = -jnp.exp(A_log)
        dt_t = jnp.moveaxis(dt, -1, 0)
        B_t = jnp.moveaxis(Bm, -1, 0)
        C_t = jnp.moveaxis(Cm, -1, 0)
        u_t = jnp.moveaxis(x, -1, 0)

        def step(state, inp):
            d, b, c, u = inp
            dA = jnp.exp(d[..., None] * A)
            state = state * dA + (d * u)[..., None] * b[:, None, :]
            y = jnp.einsum('bdn,bn->bd', state, c)
            return (state, y)
        state0 = jnp.zeros((Bsz, d_inner, d_state), x.dtype)
        _, ys = jax.lax.scan(step, state0, (dt_t, B_t, C_t, u_t))
        y = jnp.moveaxis(ys, 0, 2)
        y = y + D[None, :, None] * x
        y = y * silu(z)
        return jnp.swapaxes(y, 1, 2)

    def _L0_ffn_ref(hidden_states, gate_w, w_gate_up, w_down, shared_gate_up, shared_down):
        import jax, jax.numpy as jnp
        import numpy as np
        H = 512
        I = 352
        E = 16
        K = 2
        SI = I * 2

        def _swiglu(gu, inter):
            g, u = (gu[..., :inter], gu[..., inter:])
            return jax.nn.silu(g) * u
        orig_shape = hidden_states.shape
        x = hidden_states.reshape(-1, H)
        logits = jnp.einsum('th,eh->te', x, gate_w)
        scores = jax.nn.softmax(logits, axis=-1)
        topk_w, topk_idx = jax.lax.top_k(scores, K)
        combine = jnp.sum(jax.nn.one_hot(topk_idx, E, dtype=x.dtype) * topk_w[..., None], axis=1)
        gu = jnp.einsum('th,ehj->etj', x, w_gate_up)
        h = _swiglu(gu, I)
        y = jnp.einsum('eti,eih,te->th', h, w_down, combine)
        gu_s = x @ shared_gate_up
        y = y + _swiglu(gu_s, SI) @ shared_down
        return y.reshape(orig_shape)
    x = x + jnp.tanh(g_xattn[0]) * _L0_xattn_ref(ctx_1024, _layernorm(x, axis=-1), L0_xattn_in_proj_w, L0_xattn_conv_w, L0_xattn_conv_b, L0_xattn_x_proj_w, L0_xattn_dt_proj_w, L0_xattn_dt_proj_b, L0_xattn_A_log, L0_xattn_D)
    x = x + jnp.tanh(g_ffn[0]) * _L0_ffn_ref(_layernorm(x, axis=-1), L0_ffn_gate_w, L0_ffn_w_gate_up, L0_ffn_w_down, L0_ffn_shared_gate_up, L0_ffn_shared_down)
    return x

_drawn_inputs = setup_inputs


def setup_inputs(seed=0):
    import zlib

    import numpy as np

    out = dict(_drawn_inputs(seed))
    spreads = {'L0_xattn_D': (1.0, 0.2)}
    factors = {}
    for name, (base, spread) in spreads.items():
        noise = np.random.default_rng([zlib.crc32(name.encode()), seed]).standard_normal(out[name].shape)
        drawn = base * np.exp(spread * noise) if base else spread * noise
        out[name] = jnp.asarray(drawn.astype(out[name].dtype))
    for name, factor in factors.items():
        out[name] = (out[name] * factor).astype(out[name].dtype)
    return out
```

```python
from contextlib import ExitStack

import concourse.bass as bass
from concourse import mybir

F32 = mybir.dt.float32
F32R = mybir.dt.float32r
BF16 = mybir.dt.bfloat16
I32 = mybir.dt.int32
U32 = mybir.dt.uint32
ALU = mybir.AluOpType
ACT = mybir.ActivationFunctionType
AX = mybir.AxisListType

P = 128
EPS = 1e-5


def flamingo_block(nc, x, ctx_in, g_xattn, g_ffn, in_proj_w, conv_w, conv_b, x_proj_w, dt_proj_w,
                   dt_proj_b, A_log, D_in, gate_w, w_gate_up, w_down, shared_gate_up, shared_down, out):
    NB, L, D = x.shape
    DM = ctx_in.shape[2]
    NS = A_log.shape[1]
    RK = dt_proj_w.shape[1]
    XR = RK + 2 * NS
    TAPS = conv_w.shape[2]
    ND, NL, NK = D // P, L // P, DM // P
    H = D
    NE = gate_w.shape[0]
    INTER = w_down.shape[1]
    assert L == D and ND == NL == 4 and NK == 2 and NS == 16 and RK == 16 and TAPS == 4
    assert shared_down.shape[0] == 2 * INTER
    T = NB * L
    NT = T // P
    KH = H // P
    IPAD = 3 * P
    ILAST = INTER - 2 * P
    SLOTS = 2 * T // P + NE
    NDK = NE + 3
    ITEMS = NS * ND
    NB1 = NT // 2

    xn_rows = nc.dram_tensor("xn_rows", [T, H], F32).ap()
    slot_in = nc.dram_tensor("slot_in", [SLOTS * P, H], F32).ap()
    slot_out = nc.dram_tensor("slot_out", [SLOTS * P, H], F32).ap()
    c_rows = nc.dram_tensor("c_rows", [NB, NS, L], F32).ap()

    with ExitStack() as top:
        def sem(name):
            return top.enter_context(nc.semaphore(name))

        def sb_in(stack, name, shape, dt=F32):
            return stack.enter_context(nc.sbuf_tensor(name, shape, dt))

        def ps_in(stack, name, shape, dt=F32):
            return stack.enter_context(nc.psum_tensor(name, shape, dt))

        x_tok = sb_in(top, "x_tok", [P, NT, H])
        ident = sb_in(top, "ident", [P, P])
        tg = sb_in(top, "tg", [P, 2])
        gate_raw = sb_in(top, "gate_raw", [NE, H])

        p1 = ExitStack()
        s1 = lambda name, shape, dt=F32: sb_in(p1, name, shape, dt)
        ctx_cur = s1("ctx_cur", [P, NL, DM])
        ctxT = s1("ctxT", [P, NK, L])
        win_raw = s1("win_raw", [P, ND, DM])
        winT = s1("winT", [P, NK, D])
        xp_raw = s1("xp_raw", [XR, D])
        xpT = s1("xpT", [P, ND, XR])
        dp_raw = s1("dp_raw", [P, ND, RK])
        dpT = s1("dpT", [RK, D])
        cw = s1("cw", [P, ND, TAPS])
        cb = s1("cb", [P, ND])
        db = s1("db", [P, ND])
        Dv = s1("Dv", [P, ND])
        Aneg = s1("Aneg", [P, ND, NS])
        xs = s1("xs", [P, 2, ND, L])
        dts = s1("dts", [P, 2, ND, L])
        duT = s1("duT", [P, 2, NL, D])
        BT = s1("BT", [P, 2, NL, XR])
        xdbl = s1("xdbl", [XR, L])
        du = s1("du", [P, 2, L])
        sp_a = s1("sp_a", [P, L])
        sp_r = s1("sp_r", [P, L])
        sp_u = s1("sp_u", [P, L])
        sp_l = s1("sp_l", [P, L])
        sp_t = s1("sp_t", [P, L])
        zs = s1("zs", [P, 2, ND, L])
        y3 = s1("y3", [P, ND, L])
        dbuT = s1("dbuT", [P, 2, NL, D])
        dA = s1("dA", [P, ND, L])
        hst = s1("hst", [P, ND, L])
        prod = s1("prod", [P, ND, L])
        cbc = s1("cbc", [P, 2, L])
        zb16 = s1("zb16", [P, P], BF16)
        zmov = s1("zmov", [P, L], BF16)
        ztile = s1("ztile", [P, H])
        st1 = s1("st1", [P, ND, 6])
        mv1 = s1("mv1", [P, ND, 2])
        rs1 = s1("rs1", [P, 4, ND])
        st2 = s1("st2", [P, NL, 6])
        mv2 = s1("mv2", [P, NL, 2])
        rs2 = s1("rs2", [P, 4, NL])
        q1 = ExitStack()
        y_ps = [ps_in(q1, f"y_ps{j}", [P, L]) for j in range(ND)]
        dbu_ps = [ps_in(q1, f"dbu_ps{k}", [P, L]) for k in range(2)]
        mp = [ps_in(q1, f"mp{k}", [P, L]) for k in range(2)]
        q1.close()
        p1.close()

        p2 = ExitStack()
        s2 = lambda name, shape, dt=F32: sb_in(p2, name, shape, dt)
        wgu_h = s2("wgu_h", [P, 3, KH, 2 * INTER], F32R)
        wgu_l = s2("wgu_l", [P, 3, KH, 2 * INTER], F32R)
        wd_h = s2("wd_h", [P, 3, 3, H], F32R)
        wd_l = s2("wd_l", [P, 3, 3, H], F32R)
        raw_gu = s2("raw_gu", [P, KH, 2 * INTER])
        raw_d = s2("raw_d", [P, 3, H])
        xin = s2("xin", [P, 2, H])
        xh = s2("xh", [P, 2, KH, P], F32R)
        xl = s2("xl", [P, 2, KH, P], F32R)
        sg = s2("sg", [P, 2, INTER])
        hbuf = s2("hbuf", [P, 2, IPAD])
        hh = s2("hh", [P, 2, 3, P], F32R)
        hl = s2("hl", [P, 2, 3, P], F32R)
        yout = s2("yout", [P, 2, H])
        gbuf = s2("gbuf", [P, 4, H])
        gw_h = s2("gw_h", [P, KH, NE], F32R)
        gw_l = s2("gw_l", [P, KH, NE], F32R)
        lg = s2("lg", [P, NT, NE])
        top8 = s2("top8", [P, NT, 8])
        idx8 = s2("idx8", [P, NT, 8], U32)
        e12 = s2("e12", [P, 2, NT])
        iota_e = s2("iota_e", [P, NE])
        oh = s2("oh", [P, 2, NT, NE])
        msum = s2("msum", [P, NT, NE], BF16)
        upper = s2("upper", [P, P], BF16)
        ones = s2("ones", [P, P], BF16)
        onesf = s2("onesf", [P, NT * NE])
        cnt = s2("cnt", [P, NE, NT])
        cinc = s2("cinc", [P, NE, NT])
        cexc = s2("cexc", [P, NE, NT])
        ce = s2("ce", [P, 6, NE])
        cei = s2("cei", [P, 2, NE], I32)
        zpos = s2("zpos", [P, NT, NE])
        ztmp = s2("ztmp", [P, NT, NE])
        posf = s2("posf", [P, 2, NT])
        posi = s2("posi", [P, 2, NT], I32)
        ex = s2("ex", [P, NT, NE])
        esum = s2("esum", [P, NT])
        wts = s2("wts", [P, 2, NT])
        iota_s = s2("iota_s", [1, SLOTS])
        iota_k = s2("iota_k", [1, NDK])
        yflat = yout[0:1].rearrange("p k c -> p (k c)")
        scmp = yflat[:, 0:SLOTS * NE].rearrange("p (s e) -> p s e", s=SLOTS)
        skcmp = yflat[:, 0:NDK * SLOTS].rearrange("p (k s) -> p k s", k=NDK)
        se = s2("se", [1, SLOTS + 1])
        schg = s2("schg", [1, SLOTS])
        srank = s2("srank", [1, SLOTS])
        dk = s2("dk", [1, NDK])
        chg_i = s2("chg_i", [1, SLOTS], I32)
        rank_i = s2("rank_i", [1, SLOTS], I32)
        dk_i = s2("dk_i", [1, NDK], I32)
        q2 = ExitStack()
        psT = ps_in(q2, "psT", [P, KH, P])
        psG = [ps_in(q2, f"psG{k}", [P, 512]) for k in range(2)]
        psU = [ps_in(q2, f"psU{k}", [P, 512]) for k in range(2)]
        psHT = ps_in(q2, "psHT", [P, 4, P])
        psY = [ps_in(q2, f"psY{k}", [P, H]) for k in range(2)]
        q2.close()
        p2.close()

        wait_carrier = sem("wait_carrier")
        consts_in = sem("consts_in")
        x_in = sem("x_in")
        ctx_loaded = sem("ctx_loaded")
        ident_made = sem("ident_made")
        consts_made = sem("consts_made")
        wt_full = sem("wt_full")
        wt_read = sem("wt_read")
        a_exp = sem("a_exp")
        a_ready = sem("a_ready")
        tg_ready = sem("tg_ready")
        zeroed = sem("zeroed")
        misc_full = [sem("misc_full0"), sem("misc_full1")]
        misc_read = [sem("misc_read0"), sem("misc_read1")]
        post_full = [sem("post_full0"), sem("post_full1")]
        post_read = [sem("post_read0"), sem("post_read1")]
        conv_tap = sem("conv_tap")
        ln1_var = sem("ln1_var")
        ln1_act = sem("ln1_act")
        ln1_dve = sem("ln1_dve")
        z_ready = sem("z_ready")
        silu_done = sem("silu_done")
        c_stored = sem("c_stored")
        c_loaded = [sem("c_loaded0"), sem("c_loaded1")]
        sp_abs = sem("sp_abs")
        sp_exp = sem("sp_exp")
        sp_ln = sem("sp_ln")
        sp_dve = sem("sp_dve")
        du_ready = sem("du_ready")
        dbut_ready = sem("dbut_ready")
        da_ready = sem("da_ready")
        dbu_ready = sem("dbu_ready")
        scanned = sem("scanned")
        prod_ready = sem("prod_ready")
        prod_used = sem("prod_used")
        y_done = sem("y_done")
        y_taken = sem("y_taken")
        y3_ready = sem("y3_ready")
        x1_ready = sem("x1_ready")
        ln2_var = sem("ln2_var")
        ln2_act = sem("ln2_act")
        ln2_dve = sem("ln2_dve")
        xn_ready = sem("xn_ready")
        xn_stored = sem("xn_stored")
        raw_loaded = sem("raw_loaded")
        w_hi = sem("w_hi")
        w_split = sem("w_split")
        xin_ready = [sem("xin_ready0"), sem("xin_ready1")]
        xT_done = sem("xT_done")
        xh_ready = sem("xh_ready")
        xl_ready = sem("xl_ready")
        g_done = sem("g_done")
        gu_done = sem("gu_done")
        sg_ready = sem("sg_ready")
        h_ready = sem("h_ready")
        hT_done = sem("hT_done")
        hh_ready = sem("hh_ready")
        hl_ready = sem("hl_ready")
        y_full = sem("y_full")
        y_read = sem("y_read")
        y_stored = [sem("y_stored0"), sem("y_stored1")]
        lg_ready = sem("lg_ready")
        gw_full = sem("gw_full")
        gw_hi = sem("gw_hi")
        gw_ready = sem("gw_ready")
        rt_top = sem("rt_top")
        rt_shift = sem("rt_shift")
        cnt_read = sem("cnt_read")
        p2_consts = sem("p2_consts")
        rt = sem("rt")
        rt_mask = sem("rt_mask")
        rt_count = sem("rt_count")
        rt_act = sem("rt_act")
        pos_ready = sem("pos_ready")
        table_ready = sem("table_ready")
        g_loaded = [sem(f"g_loaded{k}") for k in range(4)]
        scat = [sem(f"scat{k}") for k in range(4)]
        gathered = [sem("gathered0"), sem("gathered1")]
        f_first = sem("f_first")
        f_done = sem("f_done")
        out_stored = sem("out_stored")

        block = top.enter_context(nc.Block())

        def mbase(bp):
            return bp * 8

        NCONST = 11

        @block.sync
        def _(sp):
            def load_ctx(bp):
                sp.dma_start(ctx_cur[:], ctx_in[bass.ds(bp, 1)].rearrange("a (t p) c -> p (a t) c", p=P)
                             ).then_inc(ctx_loaded, 16)

            for dst, src in (
                (win_raw[:], in_proj_w.rearrange("(j p) c -> p j c", p=P)),
                (xp_raw[:], x_proj_w),
                (dp_raw[:], dt_proj_w.rearrange("(j p) r -> p j r", p=P)),
                (cw[:], conv_w.rearrange("(j p) a k -> p j (a k)", p=P)),
                (Aneg[:], A_log.rearrange("(j p) n -> p j n", p=P)),
                (gate_raw[:], gate_w),
            ):
                sp.dma_start(dst, src).then_inc(consts_in, 16)
            with nc.allow_non_contiguous_dma(reason="four short columns"):
                for dst, src in ((cb, conv_b), (db, dt_proj_b), (Dv, D_in)):
                    sp.dma_start(dst[:], src.rearrange("(j p) -> p j", p=P)).then_inc(consts_in, 16)
            sp.dma_start(tg[:, 0:1], g_xattn.partition_broadcast(P)).then_inc(consts_in, 16)
            sp.dma_start(tg[:, 1:2], g_ffn.partition_broadcast(P)).then_inc(consts_in, 16)
            sp.dma_start(x_tok[:, 0:NL, :], x[0].rearrange("(t p) c -> p t c", p=P)).then_inc(x_in, 16)
            sp.dma_start(x_tok[:, NL:, :], x[1:].rearrange("b (t p) c -> p (b t) c", p=P)).then_inc(x_in, 16)
            load_ctx(0)
            sp.wait_ge(consts_made, 3)
            sp.dma_start(slot_in.rearrange("(s p) c -> p s c", p=P),
                         ztile[:].unsqueeze(1).broadcast_to([P, SLOTS, H])).then_inc(zeroed, 16)

            def store_c(bp):
                sp.wait_ge(misc_read[0], mbase(bp) + 5)
                sp.dma_start(c_rows[bass.ds(bp, 1)].rearrange("a n l -> n (a l)"),
                             xdbl[RK + NS:XR, :]).then_inc(c_stored, 16)

            def load_c(b, n):
                if n == 0:
                    sp.wait_ge(c_stored, 16 * (b + 1))
                sp.wait_ge(prod_ready, (b * NS + n) * ND)
                src = c_rows[bass.ds(b, 1), n, :].rearrange("a l -> (a l)").partition_broadcast(P)
                sp.dma_start(cbc[:, n % 2, :], src).then_inc(c_loaded[n % 2], 16)

            def store_xn(b):
                sp.wait_ge(xn_ready, NL * (b + 1))
                sp.dma_start(xn_rows[bass.ds(b * L, L), :].rearrange("(t p) c -> p t c", p=P),
                             y3[:]).then_inc(xn_stored, 16)

            store_c(0)
            load_c(0, 0)
            load_c(0, 1)
            with sp.Fori(0, NB - 1) as b:
                sp.wait_ge(misc_full[1], mbase(b) + 1)
                load_ctx(b + 1)
                for n in range(2, NS):
                    load_c(b, n)
                    if n == 13:
                        store_c(b + 1)
                load_c(b + 1, 0)
                load_c(b + 1, 1)
                store_xn(b)
            for n in range(2, NS):
                load_c(NB - 1, n)
            store_xn(NB - 1)

            def load_shared(half):
                g0 = half * INTER
                gu = shared_gate_up.rearrange("(k p) c -> p k c", p=P)
                sp.dma_start(raw_gu[:, :, 0:INTER], gu[:, :, g0:g0 + INTER]).then_inc(raw_loaded, 16)
                sp.dma_start(raw_gu[:, :, INTER:], gu[:, :, g0 + 2 * INTER:g0 + 3 * INTER]).then_inc(raw_loaded, 16)
                sp.dma_start(raw_d[:, 0:2, :], shared_down[g0:g0 + 2 * P, :].rearrange("(k p) c -> p k c", p=P)
                             ).then_inc(raw_loaded, 16)
                sp.dma_start(raw_d[0:ILAST, 2, :], shared_down[g0 + 2 * P:g0 + INTER, :]).then_inc(raw_loaded, 16)

            def load_expert(e, cond=None):
                gu = w_gate_up[bass.ds(e, 1)].rearrange("a (k p) c -> p (a k) c", p=P)
                dn = w_down[bass.ds(e, 1)].rearrange("a i c -> (a i) c")
                for dst, src in ((raw_gu[:, 0:2, :], gu[:, 0:2, :]), (raw_gu[:, 2:4, :], gu[:, 2:4, :]),
                                 (raw_d[:, 0:2, :], dn[0:2 * P, :].rearrange("(k p) c -> p k c", p=P)),
                                 (raw_d[0:ILAST, 2, :], dn[2 * P:INTER, :])):
                    sp.dma_start(dst, src, cond=cond).then_inc(raw_loaded, 16)

            def load_tile(src, q, qq, wait=True):
                if wait:
                    sp.wait_ge(xT_done, q - 1)
                sp.dma_start(xin[:, qq % 2, :], src).then_inc(xin_ready[qq % 2], 16)

            def tile_rows(rows, t):
                return rows[bass.ds(t * P, P), :]

            sp.wait_ge(xn_stored, 16 * NB)
            load_shared(0)
            load_tile(tile_rows(xn_rows, 0), 0, 0, wait=False)
            load_tile(tile_rows(xn_rows, 1), 1, 1, wait=False)
            load_tile(tile_rows(xn_rows, 2), 2, 2)
            load_tile(tile_rows(xn_rows, 3), 3, 3)
            sp.wait_ge(w_split, 1)
            load_shared(1)
            with sp.Fori(2, NT // 2) as m:
                for k in range(2):
                    load_tile(tile_rows(xn_rows, m * 2 + k), m * 2 + k, k)
            with sp.Fori(0, NB1 // 2) as m:
                for k in range(2):
                    load_tile(tile_rows(xn_rows, m * 2 + k), m * 2 + k + NT, k)
            Q0 = NT + NB1
            sp.wait_ge(table_ready, 3)
            sp.wait_ge(w_split, 2)
            e0 = sp.value_load(dk_i[0:1, 0:1], min_val=0, max_val=NE - 1)
            load_expert(e0)
            for k in range(4):
                sp.wait_ge(scat[k], 32 * (NT // 4))
            load_tile(tile_rows(slot_in, 0), Q0, 0)
            load_tile(tile_rows(slot_in, 1), Q0 + 1, 1)
            sp.wait_ge(w_split, 3)
            e1 = sp.value_load(dk_i[0:1, 1:2], min_val=0, max_val=NE - 1)
            load_expert(e1)

            def prefetch_expert(r):
                rank = sp.value_load(rank_i[0:1, bass.ds(r, 1)], min_val=0, max_val=NE)
                chg = sp.value_load(chg_i[0:1, bass.ds(r, 1)], min_val=0, max_val=1)
                e = sp.value_load(dk_i[0:1, bass.ds(rank + 2, 1)], min_val=0, max_val=NE - 1)
                sp.wait_ge(w_split, rank + 4)
                load_expert(e, cond=chg)

            with sp.Fori(0, SLOTS // 2 - 1) as m:
                for k in range(2):
                    r = m * 2 + k
                    load_tile(tile_rows(slot_in, r + 2), Q0 + r + 2, k)
                    prefetch_expert(r)
            for r in range(SLOTS - 2, SLOTS):
                load_tile(tile_rows(xn_rows, r + 2 - SLOTS + NB1), Q0 + r + 2, r % 2)
                prefetch_expert(r)
            Q1 = Q0 + SLOTS
            with sp.Fori(1, (NT - NB1) // 2) as m:
                for k in range(2):
                    load_tile(tile_rows(xn_rows, m * 2 + k + NB1), m * 2 + k + Q1, k)
            out_t = out.rearrange("b (t p) c -> p (b t) c", p=P)
            with sp.Fori(0, NB1) as m:
                for k in range(2):
                    t = m + k * NB1
                    sp.wait_ge(f_done, m * 2 + k + 1)
                    sp.dma_start(out_t[:, bass.ds(t, 1), :], x_tok[:, bass.ds(t, 1), :]).then_inc(out_stored, 16)
            sp.wait_ge(out_stored, 16 * NT)
            sp.wait_ge(raw_loaded, 64 * (4 + SLOTS))

        @block.gpsimd
        def _(pool):
            pool.memset(ident[:], 0.0).then_inc(ident_made, 1)
            pool.wait_ge(ident_made, 1)
            pool.affine_select(out=ident[:], in_=ident[:], compare_op=ALU.not_equal, fill=1.0, base=0,
                               pattern=[[-1, P]], channel_multiplier=1).then_inc(ident_made, 1)
            pool.memset(zb16[:], 0.0).then_inc(consts_made, 1)
            pool.memset(zmov[:], 0.0).then_inc(consts_made, 1)
            pool.memset(ztile[:], 0.0).then_inc(consts_made, 1)
            pool.sem_inc(prod_ready, ND)

            def products(b, n):
                pool.wait_ge(c_loaded[n % 2], 16 * (b * (NS // 2) + n // 2 + 1))
                for j in range(ND):
                    i = b * ITEMS + n * ND + j
                    pool.wait_ge(scanned, i + 1 + ND)
                    pool.wait_ge(prod_used, i + 1)
                    pool.tensor_tensor(prod[:, j, :], hst[:, j, :], cbc[:, n % 2, :],
                                       ALU.mult).then_inc(prod_ready, 1)

            with pool.Fori(0, NB) as b:
                for n in range(NS):
                    products(b, n)

            pool.wait_ge(xn_stored, 16 * NB)
            pool.iota(iota_e[:], pattern=[[1, NE]], base=0, channel_multiplier=0,
                      allow_small_or_imprecise_dtypes=True).then_inc(p2_consts, 1)
            pool.iota(iota_s[:], pattern=[[1, SLOTS]], base=0, channel_multiplier=0,
                      allow_small_or_imprecise_dtypes=True).then_inc(p2_consts, 1)
            pool.iota(iota_k[:], pattern=[[1, NDK]], base=0, channel_multiplier=0,
                      allow_small_or_imprecise_dtypes=True).then_inc(p2_consts, 1)
            pool.memset(ones[:], 1.0).then_inc(p2_consts, 1)
            pool.memset(onesf[:], 1.0).then_inc(p2_consts, 1)
            pool.memset(upper[:], 1.0).then_inc(p2_consts, 1)
            pool.memset(hbuf[:], 0.0).then_inc(p2_consts, 1)
            pool.wait_ge(p2_consts, 7)
            pool.affine_select(out=upper[:], in_=upper[:], compare_op=ALU.is_gt, fill=0.0, base=0,
                               pattern=[[1, P]], channel_multiplier=-1).then_inc(p2_consts, 1)

            def load_g(t):
                k = t % 4
                if t >= 4:
                    pool.wait_ge(scat[k], 32 * (t // 4))
                pool.dma_start(gbuf[:, k, :], xn_rows[t * P:(t + 1) * P, :]).then_inc(g_loaded[k], 16)

            for t in range(4):
                load_g(t)
            pool.wait_ge(pos_ready, 1)
            pool.wait_ge(zeroed, 16)
            for t in range(NT):
                k = t % 4
                pool.wait_ge(g_loaded[k], 16 * (t // 4 + 1))
                for c in range(2):
                    pool.indirect_dma_start(
                        slot_in, bass.IndirectOffsetOnAxis(ap=posi[:, c, t:t + 1].bitcast(U32), axis=0),
                        gbuf[:, k, :], None).then_inc(scat[k], 16)
                if t + 4 < NT:
                    load_g(t + 4)

            Q0 = NT + NB1
            with pool.Fori(0, SLOTS // 2) as m:
                for k in range(2):
                    pool.wait_ge(y_read, Q0 + m * 2 + k + 1 + 2)
                    pool.dma_start(slot_out[bass.ds((m * 2 + k) * P, P), :],
                                   yout[:, k, :]).then_inc(y_stored[k], 16)
            pool.wait_ge(y_stored[0], 16 * (SLOTS // 2))
            pool.wait_ge(y_stored[1], 16 * (SLOTS // 2))
            for i in range(NT):
                t = (i % 2) * NB1 + i // 2
                if i >= 2:
                    pool.wait_ge(f_done, i - 1)
                else:
                    for k in (0, 1):
                        pool.wait_ge(scat[2 * i + k], 32 * (NT // 4))
                for c in range(2):
                    pool.indirect_dma_start(
                        gbuf[:, 2 * (i % 2) + c, :], None, slot_out,
                        bass.IndirectOffsetOnAxis(ap=posi[:, c, t:t + 1].bitcast(U32), axis=0),
                    ).then_inc(gathered[i % 2], 16)

        @block.tensor
        def _(pe):
            mm, tr = nc.tensor.matmul, nc.tensor.transpose
            pe.wait_ge(ident_made, 2)
            pe.wait_ge(consts_made, 3)
            pe.wait_ge(consts_in, 16 * NCONST)
            for k in range(NK):
                for j in range(ND):
                    last = tr(mp[k][:, j * P:(j + 1) * P], win_raw[:, j, k * P:(k + 1) * P], ident[:])
                last.then_inc(wt_full, 1)
            for j in range(ND):
                last = tr(dbu_ps[0][:, j * XR:(j + 1) * XR], xp_raw[:, j * P:(j + 1) * P], ident[0:XR, 0:XR])
            last.then_inc(wt_full, 1)
            for j in range(ND):
                last = tr(dbu_ps[1][0:RK, j * P:(j + 1) * P], dp_raw[:, j, :], ident[:])
            last.then_inc(wt_full, 1)
            pe.wait_ge(wt_read, 4)
            pe.sem_inc(dbu_ready, 2 * ND)
            pe.sem_inc(prod_used, ND)

            def ctx_transposes(bp):
                pe.wait_ge(ctx_loaded, 16 * (bp + 1))
                for k in range(NK):
                    pe.wait_ge(misc_read[k], mbase(bp) + 1)
                    for t in range(NL):
                        last = tr(mp[k][:, t * P:(t + 1) * P], ctx_cur[:, t, k * P:(k + 1) * P], ident[:])
                    last.then_inc(misc_full[k], 1)

            def in_proj(bp, j):
                u = 1 + j // 2
                pe.wait_ge(misc_read[j % 2], mbase(bp) + u + 1)
                if j == 0:
                    pe.wait_ge(misc_read[1], mbase(bp) + 2)
                for k in range(NK):
                    last = mm(mp[j % 2][:], winT[:, k, j * P:(j + 1) * P], ctxT[:, k, :],
                              start=k == 0, stop=k == NK - 1)
                last.then_inc(misc_full[j % 2], 1)

            def x_proj(bp):
                pe.wait_ge(misc_read[0], mbase(bp) + 4)
                pe.wait_ge(silu_done, bp + 1)
                for j in range(ND):
                    last = mm(mp[0][0:XR, :], xpT[:, j, :],
                              xs[:, bass.ds(bp % 2, 1), j, :].rearrange("p a l -> p (a l)"),
                              start=j == 0, stop=j == ND - 1)
                last.then_inc(misc_full[0], 1)

            def b_transposes(bp):
                pe.wait_ge(misc_read[0], mbase(bp) + 5)
                pe.wait_ge(misc_read[1], mbase(bp) + 4)
                pe.sem_inc(wait_carrier, 1)
                for t in range(NL):
                    last = tr(mp[1][:, t * XR:(t + 1) * XR], xdbl[:, t * P:(t + 1) * P], ident[0:XR, 0:XR])
                last.then_inc(misc_full[1], 1)

            def dt_proj(bp, j):
                pe.wait_ge(misc_read[0], mbase(bp) + 5 + j)
                mm(mp[0][:], dpT[:, j * P:(j + 1) * P], xdbl[0:RK, :], start=True,
                   stop=True).then_inc(misc_full[0], 1)

            def du_transposes(bp, j):
                pe.wait_ge(du_ready, bp * ND + j + 1)
                pe.wait_ge(misc_read[1], mbase(bp) + 5 + j)
                for t in range(NL):
                    last = tr(mp[1][:, t * P:(t + 1) * P], du[:, j % 2, t * P:(t + 1) * P], ident[:])
                last.then_inc(misc_full[1], 1)

            def step(b, n, j):
                i = b * ITEMS + n * ND + j
                if j == 0:
                    pe.wait_ge(dbut_ready, b * NS + n + 1)
                pe.wait_ge(scanned, i - 1 + ND)
                for t in range(NL):
                    last = tr(dbu_ps[j % 2][:, t * P:(t + 1) * P], dbuT[:, n % 2, t, j * P:(j + 1) * P], ident[:])
                last.then_inc(dbu_ready, 1)

            def open_y(b, j):
                pe.wait_ge(y_taken, b * ND + j + 1)
                mm(y_ps[j][:], zb16[:], zmov[:], start=True, stop=False)

            def close_y(b, j):
                mm(y_ps[j][:], zb16[:], zmov[:], start=False, stop=True).then_inc(y_done, 1)

            def add_y(b, n, j):
                i = b * ITEMS + n * ND + j
                pe.wait_ge(prod_ready, i + 1 + ND)
                mm(y_ps[j][:], ident[:], prod[:, j, :], start=False, stop=False).then_inc(prod_used, 1)

            def y_transposes(b, prepared):
                pe.wait_ge(y3_ready, (b + 1) * ND)
                for t in range(NL):
                    if t < 2:
                        pe.wait_ge(misc_read[t], mbase(prepared) + 1)
                    else:
                        pe.wait_ge(post_read[t % 2], b * 2 + 1)
                    for j in range(ND):
                        last = tr(mp[t % 2][:, j * P:(j + 1) * P], y3[:, j, t * P:(t + 1) * P], ident[:])
                    last.then_inc(post_full[t % 2], 1)

            def first_steps(b, before=None):
                for j in range(ND):
                    step(b, 0, j)
                    if before is not None:
                        add_y(before, NS - 1, j)
                        close_y(before, j)
                for j in range(ND):
                    step(b, 1, j)
                    open_y(b, j)
                    add_y(b, 0, j)

            def pieces(bp, n):
                if n == 2:
                    ctx_transposes(bp)
                elif 3 <= n < 7:
                    in_proj(bp, n - 3)
                elif n == 8:
                    x_proj(bp)
                elif n == 9:
                    b_transposes(bp)
                if 10 <= n < 14:
                    dt_proj(bp, n - 10)
                if 12 <= n < 16:
                    du_transposes(bp, n - 12)

            pe.wait_ge(misc_read[0], 1)
            for n in range(2, NS):
                pieces(0, n)
            first_steps(0)
            with pe.Fori(0, NB - 1) as b:
                for n in range(2, NS):
                    for j in range(ND):
                        step(b, n, j)
                        add_y(b, n - 1, j)
                    pieces(b + 1, n)
                first_steps(b + 1, before=b)
                y_transposes(b, b + 2)
            for n in range(2, NS):
                for j in range(ND):
                    step(NB - 1, n, j)
                    add_y(NB - 1, n - 1, j)
            for j in range(ND):
                add_y(NB - 1, NS - 1, j)
                close_y(NB - 1, j)
            y_transposes(NB - 1, NB)

            pe.wait_ge(xn_stored, 16 * NB)
            for k in range(KH):
                last = tr(psHT[:, k, 0:NE], gate_raw[:, k * P:(k + 1) * P], ident[0:NE, 0:NE])
            last.then_inc(gw_full, 1)

            def transpose_x(q, k):
                pe.wait_ge(xin_ready[k], 16 * ((q >> 1) + 1))
                pe.wait_ge(xl_ready, q + 1)
                for c in range(KH):
                    last = tr(psT[:, c, :], xin[:, k, c * P:(c + 1) * P], ident[:])
                last.then_inc(xT_done, 1)

            def half_product(ps, w0, k, buf):
                n = 0
                for c in range(KH):
                    for a, w in ((xh, wgu_h), (xh, wgu_l), (xl, wgu_h)):
                        last = mm(ps[:, 0:INTER], a[:, k, c, :], w_at(w, buf)[:, c, w0:w0 + INTER],
                                  start=n == 0, stop=n == 3 * KH - 1)
                        n += 1
                return last

            def w_at(w, buf):
                if isinstance(buf, int):
                    return w[:, buf]
                return w[:, bass.ds(buf, 1)].rearrange("p a k c -> p (a k) c")

            def transpose_h(q, k):
                pe.wait_ge(h_ready, q + 1 + 2)
                pe.wait_ge(hl_ready, q + 2)
                for c in range(3):
                    last = tr(psHT[:, c, :], hbuf[:, k, c * P:(c + 1) * P], ident[:])
                last.then_inc(hT_done, 1)

            def down(q, k, buf):
                pe.wait_ge(hl_ready, q + 1 + 2)
                pe.wait_ge(y_read, q + 1)
                n = 0
                for c in range(3):
                    rows = P if c < 2 else ILAST
                    for a, w in ((hh, wd_h), (hh, wd_l), (hl, wd_h)):
                        last = mm(psY[k][:], a[0:rows, k, c, :], w_at(w, buf)[0:rows, c, :],
                                  start=n == 0, stop=n == 8)
                        n += 1
                last.then_inc(y_full, 1)

            def slot(q, k, buf, prev_buf, router=False, first=False, last_slot=False):
                pe.wait_ge(xl_ready, q + 2)
                pe.wait_ge(h_ready, q + 1)
                half_product(psG[k], 0, k, buf).then_inc(g_done, 1)
                if router:
                    n = 0
                    for c in range(KH):
                        for a, w in ((xh, gw_h), (xh, gw_l), (xl, gw_h)):
                            mm(psG[k][:, INTER:INTER + NE], a[:, k, c, :], w[:, c, :],
                               start=n == 0, stop=n == 3 * KH - 1)
                            n += 1
                if not first:
                    transpose_h(q - 1, 1 - k)
                if not last_slot:
                    transpose_x(q + 1, 1 - k)
                half_product(psU[k], INTER, k, buf).then_inc(gu_done, 1)
                if not first:
                    down(q - 1, 1 - k, prev_buf)

            transpose_x(0, 0)
            pe.wait_ge(w_split, 1)
            pe.wait_ge(gw_ready, 1)
            slot(0, 0, 1, 1, router=True, first=True)
            slot(1, 1, 1, 1, router=True)
            with pe.Fori(1, NT // 2) as m:
                for k in range(2):
                    slot(m * 2 + k, k, 1, 1, router=True)
            pe.wait_ge(w_split, 2)
            slot(NT, 0, 2, 1)
            slot(NT + 1, 1, 2, 2)
            pe.wait_ge(rt_mask, 1)
            pe.wait_ge(hl_ready, NT + 1 + 2)
            counts = psHT[:].rearrange("p c n -> p (c n)")
            marks = msum[:].rearrange("p t e -> p (t e)")
            mm(counts[:, 0:NT * NE], upper[:], marks, start=True, stop=True)
            mm(counts[:, NT * NE:], ones[:], marks, start=True, stop=True).then_inc(rt_count, 1)
            pe.wait_ge(cnt_read, 1)
            with pe.Fori(1, NB1 // 2) as m:
                for k in range(2):
                    slot(m * 2 + k + NT, k, 2, 2)

            def routed_slot(r, k, first=False):
                pe.sem_inc(wait_carrier, 1)
                rank = pe.value_load(rank_i[0:1, bass.ds(r, 1)], min_val=0, max_val=NE)
                pe.wait_ge(w_split, rank + 3)
                if first:
                    slot(r + Q0, k, rank % 2, 2)
                else:
                    pe.sem_inc(wait_carrier, 1)
                    before = pe.value_load(rank_i[0:1, bass.ds(r - 1, 1)], min_val=0, max_val=NE)
                    slot(r + Q0, k, rank % 2, before % 2)

            Q0 = NT + NB1
            pe.wait_ge(table_ready, 3)
            routed_slot(0, 0, first=True)
            routed_slot(1, 1)
            with pe.Fori(1, SLOTS // 2) as m:
                for k in range(2):
                    routed_slot(m * 2 + k, k)
            Q1 = Q0 + SLOTS
            pe.sem_inc(wait_carrier, 1)
            before = pe.value_load(rank_i[0:1, SLOTS - 1:SLOTS], min_val=0, max_val=NE)
            slot(Q1, 0, 2, before % 2)
            slot(Q1 + 1, 1, 2, 2)
            with pe.Fori(1, (NT - NB1) // 2 - 1) as m:
                for k in range(2):
                    slot(m * 2 + k + Q1, k, 2, 2)
            QE = Q1 + NT - NB1
            slot(QE - 2, 0, 2, 2)
            slot(QE - 1, 1, 2, 2, last_slot=True)
            transpose_h(QE - 1, 1)
            down(QE - 1, 1, 2)

        @block.scalar
        def _(act):
            def par(buf, b):
                return buf[:, bass.ds(b % 2, 1)].rearrange("p a j l -> p (a j) l")

            act.wait_ge(consts_in, 16 * NCONST)
            nc.scalar.activation(Aneg[:], Aneg[:], ACT.Exp).then_inc(a_exp, 1)
            nc.scalar.activation(tg[:], tg[:], ACT.Tanh).then_inc(tg_ready, 1)
            act.wait_ge(a_exp, 1)
            nc.scalar.mul(Aneg[:], Aneg[:], -1.0).then_inc(a_ready, 1)
            act.wait_ge(a_ready, 1)
            nc.scalar.preload_act_table_set("natural_log_exp_and_others")

            def ln_seed(var, rs, ready, done, count):
                act.wait_ge(ready, count)
                nc.scalar.activation(rs[:, 1, :], rs[:, 0, :], ACT.Ln).then_inc(done, 1)
                act.wait_ge(done, count * 2 - 1)
                nc.scalar.activation(rs[:, 2, :], rs[:, 1, :], ACT.Exp, scale=-0.5).then_inc(done, 1)

            def silus(bp):
                act.wait_ge(conv_tap, (bp + 1) * ND * TAPS)
                act.wait_ge(z_ready, (bp + 1) * ND)
                for j in range(ND):
                    nc.scalar.activation(par(xs, bp)[:, j, :], par(xs, bp)[:, j, :], ACT.Silu)
                for j in range(ND):
                    last = nc.scalar.activation(par(zs, bp)[:, j, :], par(zs, bp)[:, j, :], ACT.Silu)
                last.then_inc(silu_done, 1)
                nc.scalar.preload_act_table_set("natural_log_exp_and_others")

            def softplus_parts(bp, j):
                if j > 0 or not isinstance(bp, int):
                    act.wait_ge(du_ready, bp * ND + j)
                act.wait_ge(misc_full[0], mbase(bp) + 5 + j)
                nc.scalar.activation(sp_a[:], mp[0][:], ACT.Abs, bias=db[:, j:j + 1]).then_inc(sp_abs, 1)
                act.wait_ge(sp_abs, bp * ND + j + 1)
                nc.scalar.activation(sp_u[:], sp_a[:], ACT.Exp, scale=-1.0).then_inc(sp_exp, 1)
                act.wait_ge(sp_exp, bp * ND + j + 1)
                nc.scalar.activation(sp_l[:], sp_u[:], ACT.Ln, bias=1.0).then_inc(sp_ln, 1)

            def du_to_time(bp, j):
                act.wait_ge(misc_full[1], mbase(bp) + 5 + j)
                nc.scalar.copy(par(duT, bp)[:, :, j * P:(j + 1) * P],
                               mp[1][:].rearrange("p (t d) -> p t d", t=NL)).then_inc(misc_read[1], 1)

            def step(b, n):
                if n == 0:
                    act.wait_ge(misc_read[1], mbase(b) + 9)
                    act.wait_ge(du_ready, (b + 1) * ND)
                act.wait_ge(dbu_ready, (b * NS + n + 1) * ND)
                for t in range(NL):
                    last = nc.scalar.activation(dbuT[:, n % 2, t, :], par(duT, b)[:, t, :], ACT.Copy,
                                                scale=par(BT, b)[:, t, RK + n:RK + n + 1])
                last.then_inc(dbut_ready, 1)
                for j in range(ND):
                    act.wait_ge(scanned, b * ITEMS + n * ND + j + 1)
                    act.sem_inc(wait_carrier, 1)
                    nc.scalar.activation(dA[:, j, :], par(dts, b)[:, j, :], ACT.Exp,
                                         scale=Aneg[:, j, n:n + 1]).then_inc(da_ready, 1)

            def pieces(bp, n):
                if n == 3:
                    ln_seed(mv1, rs1, ln1_var, ln1_act, bp + 1)
                elif n == 7:
                    silus(bp)
                if 12 <= n < 16:
                    du_to_time(bp, n - 12)
                if 10 <= n < 14:
                    softplus_parts(bp, n - 10)

            for n in range(2, NS):
                pieces(0, n)
            step(0, 0)
            step(0, 1)
            with act.Fori(0, NB - 1) as b:
                for n in range(2, NS):
                    step(b, n)
                    pieces(b + 1, n)
                step(b + 1, 0)
                step(b + 1, 1)
                ln_seed(mv2, rs2, ln2_var, ln2_act, b + 1)
            for n in range(2, NS):
                step(NB - 1, n)
            ln_seed(mv2, rs2, ln2_var, ln2_act, NB)

            act.wait_ge(xn_stored, 16 * NB)
            act.wait_ge(gw_full, 1)
            nc.scalar.copy(gw_h[:], psHT[:, :, 0:NE]).then_inc(gw_hi, 1)

            def split_hi(loaded, dst):
                act.wait_ge(raw_loaded, loaded)
                for c in range(KH):
                    nc.scalar.copy(dst(wgu_h)[:, c, :], raw_gu[:, c, :]).then_inc(w_hi, 1)
                for c in range(3):
                    rows = P if c < 2 else ILAST
                    nc.scalar.copy(dst(wd_h)[0:rows, c, :], raw_d[0:rows, c, :]).then_inc(w_hi, 1)

            def slot(q, k, first=False, last_slot=False):
                if not first:
                    act.wait_ge(hT_done, q)
                    nc.scalar.copy(hh[:, 1 - k, :, :], psHT[:, 0:3, :]).then_inc(hh_ready, 1)
                if not last_slot:
                    act.wait_ge(xT_done, q + 2)
                    nc.scalar.copy(xh[:, 1 - k, :, :], psT[:]).then_inc(xh_ready, 1)
                act.wait_ge(g_done, q + 1)
                nc.scalar.activation(sg[:, k, :], psG[k][:, 0:INTER], ACT.Silu).then_inc(sg_ready, 1)

            def static(buf):
                return lambda w: w[:, buf]

            split_hi(64, static(1))
            act.wait_ge(xT_done, 1)
            nc.scalar.copy(xh[:, 0, :, :], psT[:]).then_inc(xh_ready, 1)
            slot(0, 0, first=True)
            slot(1, 1)
            split_hi(128, static(2))
            with act.Fori(1, NT // 2) as m:
                for k in range(2):
                    slot(m * 2 + k, k)
            slot(NT, 0)
            slot(NT + 1, 1)
            act.wait_ge(rt_shift, 1)
            nc.scalar.activation(ex[:], ex[:], ACT.Exp).then_inc(rt_act, 1)
            with act.Fori(1, NB1 // 2) as m:
                for k in range(2):
                    slot(m * 2 + k + NT, k)
            split_hi(192, static(0))
            Q0 = NT + NB1
            act.wait_ge(table_ready, 3)

            def routed_slot(r, k):
                slot(r + Q0, k)
                chg = act.value_load(chg_i[0:1, bass.ds(r, 1)], min_val=0, max_val=1)
                rank = act.value_load(rank_i[0:1, bass.ds(r, 1)], min_val=0, max_val=NE)
                buf = (rank + 1) % 2
                with act.If(chg):
                    act.wait_ge(y_full, r + Q0)
                    split_hi(256 + 64 * r, lambda w: w[:, bass.ds(buf, 1)].rearrange("p a k c -> p (a k) c"))

            with act.Fori(0, SLOTS // 2) as m:
                for k in range(2):
                    routed_slot(m * 2 + k, k)
            Q1 = Q0 + SLOTS
            with act.Fori(0, (NT - NB1) // 2 - 1) as m:
                for k in range(2):
                    slot(m * 2 + k + Q1, k)
            QE = Q1 + NT - NB1
            slot(QE - 2, 0)
            slot(QE - 1, 1, last_slot=True)
            act.wait_ge(hT_done, QE)
            nc.scalar.copy(hh[:, 1, :, :], psHT[:, 0:3, :]).then_inc(hh_ready, 1)

        @block.vector
        def _(dve):
            V = nc.vector

            def par(buf, b):
                return buf[:, bass.ds(b % 2, 1)].rearrange("p a j l -> p (a j) l")

            dve.wait_ge(wt_full, 4)
            for k in range(NK):
                V.tensor_copy(winT[:, k, :], mp[k][:]).then_inc(wt_read, 1)
            V.tensor_copy(xpT[:].rearrange("p j e -> p (j e)"), dbu_ps[0][:, 0:ND * XR]).then_inc(wt_read, 1)
            V.tensor_copy(dpT[:], dbu_ps[1][0:RK, :]).then_inc(wt_read, 1)
            for k in range(2):
                dve.sem_inc(misc_read[k], 1)
            dve.sem_inc(scanned, ND)
            dve.sem_inc(y_taken, ND)
            dve.wait_ge(x_in, 32)
            dve.wait_ge(consts_in, 16 * NCONST)

            def tile_of(b, j):
                return x_tok[:, bass.ds(b * NL + j, 1), :].rearrange("p a c -> p (a c)")

            def ln_stats(b, st, mv, rs, steps, done):
                for j in range(NL):
                    V.bn_stats(st[:, j, :], tile_of(b, j)).then_inc(steps, 1)
                dve.wait_ge(steps, b * 11 + 4)
                dve.sem_inc(wait_carrier, 1)
                for j in range(NL):
                    V.bn_aggr(mv[:, j, :], st[:, j, :]).then_inc(steps, 1)
                dve.wait_ge(steps, b * 11 + 8)
                V.tensor_scalar(rs[:, 0, :], mv[:, :, 1], EPS, None, ALU.add).then_inc(done, 1)

            def ln_refine(b, rs, steps, acted):
                dve.wait_ge(acted, (b + 1) * 2)
                V.tensor_tensor(rs[:, 1, :], rs[:, 2, :], rs[:, 2, :], ALU.mult).then_inc(steps, 1)
                dve.wait_ge(steps, b * 11 + 9)
                V.scalar_tensor_tensor(rs[:, 3, :], rs[:, 1, :], -0.5, rs[:, 0, :], ALU.mult,
                                       ALU.mult).then_inc(steps, 1)
                dve.wait_ge(steps, b * 11 + 10)
                V.scalar_tensor_tensor(rs[:, 3, :], rs[:, 3, :], 1.5, rs[:, 2, :], ALU.add,
                                       ALU.mult).then_inc(steps, 1)
                dve.wait_ge(steps, b * 11 + 11)

            def z_normalise(bp):
                ln_refine(bp, rs1, ln1_dve, ln1_act)
                for j in range(ND):
                    V.tensor_scalar(par(zs, bp)[:, j, :], tile_of(bp, j), mv1[:, j, 0:1], rs1[:, 3, j:j + 1],
                                    ALU.subtract, ALU.mult).then_inc(z_ready, 1)

            def ctx_to_sbuf(bp):
                for k in range(NK):
                    dve.wait_ge(misc_full[k], mbase(bp) + 1)
                    V.tensor_copy(ctxT[:, k, :], mp[k][:]).then_inc(misc_read[k], 1)

            def conv(bp, j):
                k, u = j % 2, 1 + j // 2
                xj = par(xs, bp)[:, j, :]
                c0 = (bp * ND + j) * TAPS
                dve.wait_ge(misc_full[k], mbase(bp) + u + 1)
                V.tensor_scalar(xj, mp[k][:], cw[:, j, TAPS - 1:TAPS], cb[:, j:j + 1], ALU.mult,
                                ALU.add).then_inc(conv_tap, 1)
                for s in range(1, TAPS):
                    dve.wait_ge(conv_tap, c0 + s)
                    ins = V.scalar_tensor_tensor(xj[:, s:], mp[k][:, 0:L - s], cw[:, j, TAPS - 1 - s:TAPS - s],
                                                 xj[:, s:], ALU.mult, ALU.add)
                    ins.then_inc(conv_tap, 1)
                dve.wait_ge(conv_tap, c0 + TAPS)
                dve.sem_inc(misc_read[k], 1)

            def x_proj_to_sbuf(bp):
                if not (isinstance(bp, int) and bp == 0):
                    dve.wait_ge(c_stored, 16 * bp)
                dve.wait_ge(misc_full[0], mbase(bp) + 4)
                V.tensor_copy(xdbl[:], mp[0][0:XR, :]).then_inc(misc_read[0], 1)

            def b_to_sbuf(bp):
                dve.wait_ge(misc_full[1], mbase(bp) + 4)
                V.tensor_copy(par(BT, bp).rearrange("p t e -> p (t e)"),
                              mp[1][:, 0:NL * XR]).then_inc(misc_read[1], 1)

            def softplus_in(bp, j):
                dve.wait_ge(misc_full[0], mbase(bp) + 5 + j)
                dve.wait_ge(sp_abs, bp * ND + j + 1)
                V.tensor_scalar(sp_r[:], mp[0][:], db[:, j:j + 1], 0.0, ALU.add,
                                ALU.max).then_inc(misc_read[0], 1)

            def softplus_out(bp, j):
                c0 = (bp * ND + j) * 4
                dve.wait_ge(sp_ln, bp * ND + j + 1)
                V.tensor_scalar(sp_t[:], sp_u[:], 1.0, -1.0, ALU.add, ALU.add).then_inc(sp_dve, 1)
                dve.wait_ge(misc_read[0], mbase(bp) + 6 + j)
                V.tensor_tensor(sp_r[:], sp_r[:], sp_l[:], ALU.add).then_inc(sp_dve, 1)
                dve.wait_ge(sp_dve, c0 + 2)
                V.tensor_tensor(sp_t[:], sp_t[:], sp_u[:], ALU.subtract).then_inc(sp_dve, 1)
                dve.wait_ge(sp_dve, c0 + 3)
                V.tensor_tensor(par(dts, bp)[:, j, :], sp_r[:], sp_t[:], ALU.subtract).then_inc(sp_dve, 1)
                dve.wait_ge(sp_dve, c0 + 4)
                V.tensor_tensor(du[:, j % 2, :], par(dts, bp)[:, j, :], par(xs, bp)[:, j, :],
                                ALU.mult).then_inc(du_ready, 1)

            def scans(b, n):
                for j in range(ND):
                    i = b * ITEMS + n * ND + j
                    dve.wait_ge(da_ready, i + 1)
                    dve.wait_ge(dbu_ready, i + 1 + 2 * ND)
                    dve.wait_ge(prod_ready, i + 1)
                    V.tensor_tensor_scan(hst[:, j, :], dA[:, j, :], dbu_ps[j % 2][:], 0.0, ALU.mult,
                                         ALU.add).then_inc(scanned, 1)

            def gate_y(b):
                if not (isinstance(b, int) and b == 0):
                    dve.wait_ge(xn_stored, 16 * b)
                for j in range(ND):
                    dve.wait_ge(y_done, b * ND + j + 1)
                    V.scalar_tensor_tensor(y3[:, j, :], par(xs, b)[:, j, :], Dv[:, j:j + 1], y_ps[j][:],
                                           ALU.mult, ALU.add).then_inc(y_taken, 1)
                for j in range(ND):
                    dve.wait_ge(y_taken, b * ND + j + 1 + ND)
                    V.scalar_tensor_tensor(y3[:, j, :], y3[:, j, :], tg[:, 0:1], par(zs, b)[:, j, :],
                                           ALU.mult, ALU.mult).then_inc(y3_ready, 1)

            def residual(b):
                for t in range(NL):
                    dve.wait_ge(post_full[t % 2], b * 2 + t // 2 + 1)
                    V.tensor_tensor(tile_of(b, t), tile_of(b, t), mp[t % 2][:], ALU.add).then_inc(x1_ready, 1)
                    dve.wait_ge(x1_ready, b * NL + t + 1)
                    dve.sem_inc(post_read[t % 2], 1)
                ln_stats(b, st2, mv2, rs2, ln2_dve, ln2_var)

            def normalise_x1(b):
                ln_refine(b, rs2, ln2_dve, ln2_act)
                for t in range(NL):
                    V.tensor_scalar(y3[:, t, :], tile_of(b, t), mv2[:, t, 0:1], rs2[:, 3, t:t + 1],
                                    ALU.subtract, ALU.mult).then_inc(xn_ready, 1)

            def pieces(bp, n):
                if n == 2:
                    ctx_to_sbuf(bp)
                    ln_stats(bp, st1, mv1, rs1, ln1_dve, ln1_var)
                elif 3 <= n < 7:
                    conv(bp, n - 3)
                    if n == 4:
                        z_normalise(bp)
                elif n == 8:
                    x_proj_to_sbuf(bp)
                elif n == 9:
                    b_to_sbuf(bp)
                if 11 <= n < 15:
                    softplus_out(bp, n - 11)
                if 10 <= n < 14:
                    softplus_in(bp, n - 10)

            dve.wait_ge(a_ready, 1)
            dve.wait_ge(tg_ready, 1)
            for n in range(2, NS):
                pieces(0, n)
            scans(0, 0)
            scans(0, 1)
            with dve.Fori(0, NB - 1) as b:
                for n in range(2, NS):
                    scans(b, n)
                    pieces(b + 1, n)
                scans(b + 1, 0)
                gate_y(b)
                scans(b + 1, 1)
                residual(b)
                normalise_x1(b)
            for n in range(2, NS):
                scans(NB - 1, n)
            gate_y(NB - 1)
            residual(NB - 1)
            normalise_x1(NB - 1)

            dve.sem_inc(xl_ready, 1)
            dve.sem_inc(h_ready, 2)
            dve.sem_inc(hl_ready, 2)
            dve.sem_inc(y_read, 2)
            dve.wait_ge(xn_stored, 16 * NB)
            dve.wait_ge(p2_consts, 8)
            dve.wait_ge(gw_hi, 1)
            V.tensor_tensor(gw_l[:], psHT[:, :, 0:NE], gw_h[:].bitcast(F32), ALU.subtract).then_inc(gw_ready, 1)

            def split_lo(ordinal, dst):
                for c in range(KH):
                    dve.wait_ge(w_hi, ordinal * 7 + c + 1)
                    V.tensor_tensor(dst(wgu_l)[:, c, :], raw_gu[:, c, :], dst(wgu_h)[:, c, :].bitcast(F32),
                                    ALU.subtract)
                for c in range(3):
                    rows = P if c < 2 else ILAST
                    dve.wait_ge(w_hi, ordinal * 7 + KH + c + 1)
                    ins = V.tensor_tensor(dst(wd_l)[0:rows, c, :], raw_d[0:rows, c, :],
                                          dst(wd_h)[0:rows, c, :].bitcast(F32), ALU.subtract)
                ins.then_inc(w_split, 1)

            def static(buf):
                return lambda w: w[:, buf]

            def h_lo(q, k):
                dve.wait_ge(hT_done, q + 1)
                dve.wait_ge(hh_ready, q + 1)
                V.tensor_tensor(hl[:, k, :, :], psHT[:, 0:3, :], hh[:, k, :, :].bitcast(F32),
                                ALU.subtract).then_inc(hl_ready, 1)

            def x_lo(q, k):
                dve.wait_ge(xT_done, q + 1)
                dve.wait_ge(xh_ready, q + 1)
                V.tensor_tensor(xl[:, k, :, :], psT[:], xh[:, k, :, :].bitcast(F32),
                                ALU.subtract).then_inc(xl_ready, 1)

            def token_tile(t):
                return x_tok[:, bass.ds(t, 1), :].rearrange("p a c -> p (a c)")

            def result_to(q, k, kind, t):
                dve.wait_ge(y_full, q + 1)
                if kind == "shared":
                    ins = V.scalar_tensor_tensor(token_tile(t), psY[k][:], tg[:, 1:2], token_tile(t),
                                                 ALU.mult, ALU.add)
                else:
                    if not isinstance(t, int) or t >= 2:
                        dve.wait_ge(y_stored[k], 16 * (t >> 1))
                    ins = V.tensor_copy(yout[:, k, :], psY[k][:])
                ins.then_inc(y_read, 1)

            def slot(q, k, kind, t, router=False, first=False, last_slot=False):
                if not first:
                    h_lo(q - 1, 1 - k)
                if not last_slot:
                    x_lo(q + 1, 1 - k)
                dve.wait_ge(sg_ready, q + 1)
                dve.wait_ge(gu_done, q + 1)
                V.tensor_tensor(hbuf[:, k, 0:INTER], sg[:, k, :], psU[k][:, 0:INTER], ALU.mult
                                ).then_inc(h_ready, 1)
                if router:
                    V.tensor_copy(lg[:, bass.ds(q, 1), :].rearrange("p a e -> p (a e)"),
                                  psG[k][:, INTER:INTER + NE]).then_inc(lg_ready, 1)
                if not first:
                    result_to(q - 1, 1 - k, kind, t)

            steps = [0]

            def link(ins):
                steps[0] += 1
                ins.then_inc(rt, 1)
                dve.wait_ge(rt, steps[0])

            split_lo(0, static(1))
            x_lo(0, 0)
            slot(0, 0, "shared", 0, router=True, first=True)
            slot(1, 1, "shared", 0, router=True)
            split_lo(1, static(2))
            with dve.Fori(1, NT // 2) as m:
                for k in range(2):
                    slot(m * 2 + k, k, "shared", m * 2 + k - 1, router=True)
            slot(NT, 0, "shared", NT - 1)

            dve.wait_ge(lg_ready, NT)
            for t in range(NT):
                V.max(top8[:, t, :], lg[:, t, :]).then_inc(rt_top, 1)
            for t in range(NT):
                dve.wait_ge(rt_top, t + 1)
                V.max_index(idx8[:, t, :], top8[:, t, :], lg[:, t, :]).then_inc(rt_top, 1)
            dve.wait_ge(rt_top, 2 * NT)
            link(V.tensor_copy(e12[:], idx8[:, :, 0:2].rearrange("p t c -> p c t")))
            iota_b = iota_e[:].unsqueeze(1).broadcast_to([P, NT, NE])
            for c in range(2):
                ins = V.tensor_tensor(oh[:, c], iota_b, e12[:, c].unsqueeze(2).broadcast_to([P, NT, NE]),
                                      ALU.is_equal)
                link(ins)
            V.tensor_tensor(msum[:], oh[:, 0], oh[:, 1], ALU.add).then_inc(rt_mask, 1)
            V.tensor_tensor(ex[:], lg[:], top8[:, :, 0:1].broadcast_to([P, NT, NE]),
                            ALU.subtract).then_inc(rt_shift, 1)
            slot(NT + 1, 1, "shared", 0)
            dve.wait_ge(rt_count, 1)
            counts = psHT[:].rearrange("p c n -> p (c n)")
            link(V.tensor_copy(zpos[:].rearrange("p t e -> p (t e)"), counts[:, 0:NT * NE]))
            V.tensor_copy(cnt[:], counts[:, NT * NE:].rearrange("p (t e) -> p e t", t=NT)).then_inc(cnt_read, 1)
            dve.wait_ge(cnt_read, 1)
            flat = lambda a: a[:].rearrange("p e t -> p (e t)")
            link(V.tensor_tensor_scan(flat(cinc), onesf[:], flat(cnt), 0.0, ALU.mult, ALU.add))
            link(V.tensor_tensor(cexc[:], cinc[:], cnt[:], ALU.subtract))
            CE, TL, TE, ADJ, TMP = range(5)
            link(V.tensor_tensor(ce[:, CE], cinc[:, :, NT - 1], cexc[:, :, 0], ALU.subtract))
            link(V.tensor_scalar(cei[:, 0], ce[:, CE], float(P - 1), None, ALU.add))
            link(V.tensor_scalar(cei[:, 1], cei[:, 0], 7, None, ALU.logical_shift_right))
            link(V.tensor_copy(ce[:, TL], cei[:, 1]))
            link(V.tensor_tensor_scan(ce[:, TE], onesf[:, 0:NE], ce[:, TL], 0.0, ALU.mult, ALU.add))
            link(V.tensor_tensor(ce[:, TMP], ce[:, TE], ce[:, TL], ALU.subtract))
            link(V.scalar_tensor_tensor(ce[:, ADJ], ce[:, TMP], float(P), cexc[:, :, 0], ALU.mult,
                                        ALU.subtract))
            link(V.tensor_tensor(zpos[:], zpos[:], cexc[:].rearrange("p e t -> p t e"), ALU.add))
            link(V.tensor_tensor(zpos[:], zpos[:], ce[:, ADJ].unsqueeze(1).broadcast_to([P, NT, NE]), ALU.add))
            for c in range(2):
                link(V.tensor_tensor(ztmp[:], zpos[:], oh[:, c], ALU.mult))
                link(V.tensor_reduce(posf[:, c], ztmp[:], AX.X, ALU.add))
            V.tensor_copy(posi[:], posf[:]).then_inc(pos_ready, 1)
            link(V.memset(se[:, 0:1], -1.0))
            link(V.tensor_tensor(scmp, iota_s[:].unsqueeze(2).broadcast_to([1, SLOTS, NE]),
                                 ce[0:1, TE].unsqueeze(1).broadcast_to([1, SLOTS, NE]), ALU.is_ge))
            link(V.tensor_reduce(se[:, 1:], scmp, AX.X, ALU.add))
            link(V.tensor_scalar(se[:, 1:], se[:, 1:], float(NE - 1), None, ALU.min))
            link(V.tensor_tensor(schg[:], se[:, 1:], se[:, 0:SLOTS], ALU.not_equal))
            link(V.tensor_tensor_scan(srank[:], onesf[0:1, 0:SLOTS], schg[:], -1.0, ALU.mult, ALU.add))
            V.tensor_copy(chg_i[:], schg[:]).then_inc(table_ready, 1)
            V.tensor_copy(rank_i[:], srank[:]).then_inc(table_ready, 1)
            link(V.tensor_tensor(se[:, 1:], se[:, 1:], schg[:], ALU.mult))
            link(V.tensor_tensor(skcmp, iota_k[:].unsqueeze(2).broadcast_to([1, NDK, SLOTS]),
                                 srank[:].unsqueeze(1).broadcast_to([1, NDK, SLOTS]), ALU.is_equal))
            link(V.tensor_tensor(skcmp, skcmp, se[:, 1:].unsqueeze(1).broadcast_to([1, NDK, SLOTS]),
                                 ALU.mult))
            link(V.tensor_reduce(dk[:], skcmp, AX.X, ALU.add))
            V.tensor_copy(dk_i[:], dk[:]).then_inc(table_ready, 1)
            dve.wait_ge(rt_act, 1)
            link(V.tensor_reduce(esum[:], ex[:], AX.X, ALU.add))
            link(V.reciprocal(esum[:], esum[:]))
            link(V.tensor_scalar(esum[:], esum[:], tg[:, 1:2], None, ALU.mult))
            for c in range(2):
                link(V.tensor_tensor(ztmp[:], ex[:], oh[:, c], ALU.mult))
                link(V.tensor_reduce(wts[:, c], ztmp[:], AX.X, ALU.add))
                link(V.tensor_tensor(wts[:, c], wts[:, c], esum[:], ALU.mult))

            with dve.Fori(1, NB1 // 2) as m:
                for k in range(2):
                    slot(m * 2 + k + NT, k, "shared", m * 2 + k - 1)
            split_lo(2, static(0))
            Q0 = NT + NB1

            def routed_slot(r, k, kind="routed"):
                slot(r + Q0, k, kind, r - 1 if kind == "routed" else NB1 - 1)
                chg = dve.value_load(chg_i[0:1, bass.ds(r, 1)], min_val=0, max_val=1)
                rank = dve.value_load(rank_i[0:1, bass.ds(r, 1)], min_val=0, max_val=NE)
                buf = (rank + 1) % 2
                with dve.If(chg):
                    split_lo(rank + 3, lambda w: w[:, bass.ds(buf, 1)].rearrange("p a k c -> p (a k) c"))

            routed_slot(0, 0, "shared")
            routed_slot(1, 1)
            with dve.Fori(1, SLOTS // 2) as m:
                for k in range(2):
                    routed_slot(m * 2 + k, k)
            Q1 = Q0 + SLOTS

            def finish(i, t):
                k = i % 2 if isinstance(i, int) else i[1]
                i = i if isinstance(i, int) else i[0]
                dve.wait_ge(gathered[k], 32 * ((i >> 1) + 1))
                for c in range(2):
                    ins = V.scalar_tensor_tensor(token_tile(t), gbuf[:, 2 * k + c, :],
                                                 wts[:, c, bass.ds(t, 1)], token_tile(t), ALU.mult, ALU.add)
                    if c == 0:
                        ins.then_inc(f_first, 1)
                        dve.wait_ge(f_first, i + 1)
                ins.then_inc(f_done, 1)

            slot(Q1, 0, "routed", SLOTS - 1)
            slot(Q1 + 1, 1, "shared", NB1)
            with dve.Fori(1, (NT - NB1) // 2 - 1) as m:
                for k in range(2):
                    slot(m * 2 + k + Q1, k, "shared", m * 2 + k + NB1 - 1)
                    finish((m * 4 + 2 * k - 4, 0), m * 2 + k - 2)
                    finish((m * 4 + 2 * k - 3, 1), m * 2 + k - 2 + NB1)
            QE = Q1 + NT - NB1
            for k in range(2):
                slot(QE - 2 + k, k, "shared", NT - 3 + k, last_slot=k == 1)
                i = 2 * (NB1 - 4 + k)
                finish(i, NB1 - 4 + k)
                finish(i + 1, 2 * NB1 - 4 + k)
            h_lo(QE - 1, 1)
            result_to(QE - 1, 1, "shared", NT - 1)
            for i in range(2 * NB1 - 4, 2 * NB1):
                finish(i, (i % 2) * NB1 + i // 2)


_INS = ['x', 'ctx_1024', 'g_xattn', 'g_ffn', 'L0_xattn_in_proj_w', 'L0_xattn_conv_w', 'L0_xattn_conv_b',
        'L0_xattn_x_proj_w', 'L0_xattn_dt_proj_w', 'L0_xattn_dt_proj_b', 'L0_xattn_A_log', 'L0_xattn_D',
        'L0_ffn_gate_w', 'L0_ffn_w_gate_up', 'L0_ffn_w_down', 'L0_ffn_shared_gate_up', 'L0_ffn_shared_down']
_OUTS = [((4, 512, 512), 'float32')]


def kernel(**inputs):
    import numpy as _np
    import concourse.bacc as _bacc
    from concourse import mybir as _mybir
    from concourse.bass_utils import run_bass_kernel_spmd as _run

    nc = _bacc.Bacc("TRN2", target_bir_lowering=False, num_devices=1)
    arrays, args = {}, []
    for name in _INS:
        a = _np.ascontiguousarray(inputs[name])
        arrays[f"in_{name}_dram"] = a
        args.append(nc.dram_tensor(f"in_{name}_dram", a.shape, _mybir.dt.from_np(a.dtype), kind="ExternalInput").ap())
    for i, (shape, dtype) in enumerate(_OUTS):
        dt = _mybir.dt.from_np(_np.dtype(dtype))
        args.append(nc.dram_tensor(f"out_{i}_dram", shape, dt, kind="ExternalOutput").ap())
    flamingo_block(nc, *args)
    r = _run(nc, [arrays], core_ids=[0])
    return r.results[0]["out_0_dram"]
```

```python
from contextlib import ExitStack

import concourse.bass as bass
from concourse import mybir

F32 = mybir.dt.float32
F32R = mybir.dt.float32r
BF16 = mybir.dt.bfloat16
I32 = mybir.dt.int32
U32 = mybir.dt.uint32
ALU = mybir.AluOpType
ACT = mybir.ActivationFunctionType
AX = mybir.AxisListType

P = 128
EPS = 1e-5


def flamingo_block(nc, x, ctx_in, g_xattn, g_ffn, in_proj_w, conv_w, conv_b, x_proj_w, dt_proj_w,
                   dt_proj_b, A_log, D_in, gate_w, w_gate_up, w_down, shared_gate_up, shared_down, out):
    NB, L, D = x.shape
    DM = ctx_in.shape[2]
    NS = A_log.shape[1]
    RK = dt_proj_w.shape[1]
    XR = RK + 2 * NS
    TAPS = conv_w.shape[2]
    ND, NL, NK = D // P, L // P, DM // P
    H = D
    NE = gate_w.shape[0]
    INTER = w_down.shape[1]
    assert L == D and ND == NL == 4 and NK == 2 and NS == 16 and RK == 16 and TAPS == 4
    assert shared_down.shape[0] == 2 * INTER
    T = NB * L
    NT = T // P
    KH = H // P
    IPAD = 3 * P
    ILAST = INTER - 2 * P
    SLOTS = 2 * T // P + NE
    NDK = NE + 3
    ITEMS = NS * ND
    RING = 2 * ND
    ZROWS = SLOTS * P // (NB - 1)
    NB1 = NT // 2

    xn_rows = nc.dram_tensor("xn_rows", [T, H], F32).ap()
    slot_in = nc.dram_tensor("slot_in", [SLOTS * P, H], F32).ap()
    slot_out = nc.dram_tensor("slot_out", [SLOTS * P, H], F32).ap()
    c_rows = nc.dram_tensor("c_rows", [NB, NS, L], F32).ap()

    with ExitStack() as top:
        def sem(name):
            return top.enter_context(nc.semaphore(name))

        def sb_in(stack, name, shape, dt=F32):
            return stack.enter_context(nc.sbuf_tensor(name, shape, dt))

        def ps_in(stack, name, shape, dt=F32):
            return stack.enter_context(nc.psum_tensor(name, shape, dt))

        x_tok = sb_in(top, "x_tok", [P, NT, H])
        ident = sb_in(top, "ident", [P, P])
        tg = sb_in(top, "tg", [P, 2])
        gate_raw = sb_in(top, "gate_raw", [NE, H])
        st2 = sb_in(top, "st2", [P, NT, 6])
        mv2 = sb_in(top, "mv2", [P, NT, 2])
        rs2 = sb_in(top, "rs2", [P, 4, NT])

        p1 = ExitStack()
        s1 = lambda name, shape, dt=F32: sb_in(p1, name, shape, dt)
        ctx_cur = s1("ctx_cur", [P, NL, DM])
        ctxT = s1("ctxT", [P, NK, L])
        winT = s1("winT", [P, NK, D])
        xpT = s1("xpT", [P, ND, XR])
        dp_raw = s1("dp_raw", [P, ND, RK])
        dpT = s1("dpT", [RK, D])
        cw = s1("cw", [P, ND, TAPS])
        cb = s1("cb", [P, ND])
        db = s1("db", [P, ND])
        Dv = s1("Dv", [P, ND])
        Aneg = s1("Aneg", [P, ND, NS])
        xs = s1("xs", [P, 2, ND, L])
        dts = s1("dts", [P, 2, ND, L])
        duT = s1("duT", [P, 2, NL, D])
        BT = s1("BT", [P, 2, NL, XR])
        xdbl = s1("xdbl", [XR, L])
        du = s1("du", [P, 2, L])
        sp_t = s1("sp_t", [P, L])
        zs = s1("zs", [P, 2, ND, L])
        y3 = s1("y3", [P, ND, L])
        sp_a, sp_r, sp_u, sp_l = (y3[:, j, :] for j in range(ND))
        dbuT = s1("dbuT", [P, 2, NL, D])
        dA = s1("dA", [P, RING, L])
        win_raw = dA[:, 0:2, :].rearrange("p a (k c) -> p (a k) c", c=DM)
        xp_raw = dA[0:XR, 2, :]
        hst = s1("hst", [P, RING, L])
        prod = s1("prod", [P, RING, L])
        cbc = s1("cbc", [P, 2, L])
        zb16 = s1("zb16", [P, P], BF16)
        zmov = s1("zmov", [P, L], BF16)
        ztile = s1("ztile", [P, H])
        st1 = s1("st1", [P, ND, 6])
        mv1 = s1("mv1", [P, ND, 2])
        rs1 = s1("rs1", [P, 5, ND])
        q1 = ExitStack()
        y_ps = [ps_in(q1, f"y_ps{j}", [P, L]) for j in range(ND)]
        dbu_ps = [ps_in(q1, f"dbu_ps{k}", [P, L]) for k in range(2)]
        mp = [ps_in(q1, f"mp{k}", [P, L]) for k in range(2)]
        q1.close()
        p1.close()

        p2 = ExitStack()
        s2 = lambda name, shape, dt=F32: sb_in(p2, name, shape, dt)
        wgu_h = s2("wgu_h", [P, 3, KH, 2 * INTER], F32R)
        wgu_l = s2("wgu_l", [P, 3, KH, 2 * INTER], F32R)
        wd_h = s2("wd_h", [P, 3, 3, H], F32R)
        wd_l = s2("wd_l", [P, 3, 3, H], F32R)
        raw_gu = s2("raw_gu", [P, KH, 2 * INTER])
        raw_d = s2("raw_d", [P, 3, H])
        xin = s2("xin", [P, 2, H])
        xh = s2("xh", [P, 2, KH, P], F32R)
        xl = s2("xl", [P, 2, KH, P], F32R)
        sg = s2("sg", [P, 2, INTER])
        hbuf = s2("hbuf", [P, 2, IPAD])
        hh = s2("hh", [P, 2, 3, P], F32R)
        hl = s2("hl", [P, 2, 3, P], F32R)
        yout = s2("yout", [P, 2, H])
        gbuf = s2("gbuf", [P, 4, H])
        gw_h = s2("gw_h", [P, KH, NE], F32R)
        gw_l = s2("gw_l", [P, KH, NE], F32R)
        lg = s2("lg", [P, NT, NE])
        top8 = s2("top8", [P, NT, 8])
        idx8 = s2("idx8", [P, NT, 8], U32)
        e12 = s2("e12", [P, 2, NT])
        iota_e = s2("iota_e", [P, NE])
        oh = s2("oh", [P, 2, NT, NE])
        msum = s2("msum", [P, NT, NE], BF16)
        upper = s2("upper", [P, P], BF16)
        ones = s2("ones", [P, P], BF16)
        onesf = s2("onesf", [P, NT * NE])
        cnt = s2("cnt", [P, NE, NT])
        cinc = s2("cinc", [P, NE, NT])
        cexc = s2("cexc", [P, NE, NT])
        ce = s2("ce", [P, 6, NE])
        cei = s2("cei", [P, 2, NE], I32)
        zpos = s2("zpos", [P, NT, NE])
        ztmp = s2("ztmp", [P, NT, NE])
        posf = s2("posf", [P, 2, NT])
        posi = s2("posi", [P, 2, NT], I32)
        ex = s2("ex", [P, NT, NE])
        esum = s2("esum", [P, NT])
        wts = s2("wts", [P, 2, NT])
        iota_s = s2("iota_s", [1, SLOTS])
        iota_k = s2("iota_k", [1, NDK])
        yflat = yout[0:1].rearrange("p k c -> p (k c)")
        scmp = yflat[:, 0:SLOTS * NE].rearrange("p (s e) -> p s e", s=SLOTS)
        skcmp = yflat[:, 0:NDK * SLOTS].rearrange("p (k s) -> p k s", k=NDK)
        se = s2("se", [1, SLOTS + 1])
        schg = s2("schg", [1, SLOTS])
        srank = s2("srank", [1, SLOTS])
        dk = s2("dk", [1, NDK])
        chg_i = s2("chg_i", [1, SLOTS], I32)
        rank_i = s2("rank_i", [1, SLOTS], I32)
        dk_i = s2("dk_i", [1, NDK], I32)
        q2 = ExitStack()
        psT = ps_in(q2, "psT", [P, KH, P])
        psG = [ps_in(q2, f"psG{k}", [P, 512]) for k in range(2)]
        psU = [ps_in(q2, f"psU{k}", [P, 512]) for k in range(2)]
        psHT = ps_in(q2, "psHT", [P, 4, P])
        psY = [ps_in(q2, f"psY{k}", [P, H]) for k in range(2)]
        q2.close()
        p2.close()

        wait_carrier = sem("wait_carrier")
        consts_in = sem("consts_in")
        x_in = sem("x_in")
        ctx_loaded = sem("ctx_loaded")
        ident_made = sem("ident_made")
        consts_made = sem("consts_made")
        wt_full = sem("wt_full")
        wt_read = sem("wt_read")
        a_exp = sem("a_exp")
        a_ready = sem("a_ready")
        tg_ready = sem("tg_ready")
        zeroed = sem("zeroed")
        misc_full = [sem("misc_full0"), sem("misc_full1")]
        misc_read = [sem("misc_read0"), sem("misc_read1")]
        post_full = [sem("post_full0"), sem("post_full1")]
        post_read = [sem("post_read0"), sem("post_read1")]
        conv_tap = sem("conv_tap")
        ln1_var = sem("ln1_var")
        ln1_act = sem("ln1_act")
        ln1_dve = sem("ln1_dve")
        silu_done = sem("silu_done")
        c_stored = sem("c_stored")
        c_loaded = [sem("c_loaded0"), sem("c_loaded1")]
        sp_abs = sem("sp_abs")
        sp_exp = sem("sp_exp")
        sp_ln = sem("sp_ln")
        sp_dve = sem("sp_dve")
        du_ready = sem("du_ready")
        dbut_ready = sem("dbut_ready")
        dbut_last = sem("dbut_last")
        dut_ready = sem("dut_ready")
        da_ready = sem("da_ready")
        dbu_ready = sem("dbu_ready")
        scanned = sem("scanned")
        prod_ready = sem("prod_ready")
        prod_used = sem("prod_used")
        y_done = sem("y_done")
        y_taken = sem("y_taken")
        y3_ready = sem("y3_ready")
        x1_ready = sem("x1_ready")
        ln2_var = sem("ln2_var")
        ln2_act = sem("ln2_act")
        ln2_dve = sem("ln2_dve")
        p1_done = sem("p1_done")
        xn_made = sem("xn_made")
        xn_stored = [sem("xn_stored0"), sem("xn_stored1")]
        raw_loaded = sem("raw_loaded")
        w_hi = sem("w_hi")
        w_split = sem("w_split")
        xin_ready = [sem("xin_ready0"), sem("xin_ready1")]
        xT_done = sem("xT_done")
        xh_ready = sem("xh_ready")
        xl_ready = sem("xl_ready")
        g_done = sem("g_done")
        gu_done = sem("gu_done")
        sg_ready = sem("sg_ready")
        h_ready = sem("h_ready")
        hT_done = sem("hT_done")
        hh_ready = sem("hh_ready")
        hl_ready = sem("hl_ready")
        y_full = sem("y_full")
        y_read = sem("y_read")
        y_stored = [sem("y_stored0"), sem("y_stored1")]
        lg_ready = sem("lg_ready")
        gw_full = sem("gw_full")
        gw_hi = sem("gw_hi")
        gw_ready = sem("gw_ready")
        rt_top = sem("rt_top")
        rt_shift = sem("rt_shift")
        cnt_read = sem("cnt_read")
        p2_consts = sem("p2_consts")
        rt = sem("rt")
        rt_mask = sem("rt_mask")
        rt_count = sem("rt_count")
        rt_act = sem("rt_act")
        pos_ready = sem("pos_ready")
        table_ready = sem("table_ready")
        g_loaded = [sem(f"g_loaded{k}") for k in range(4)]
        scat = [sem(f"scat{k}") for k in range(4)]
        gathered = [sem("gathered0"), sem("gathered1")]
        f_first = sem("f_first")
        f_done = sem("f_done")
        out_stored = sem("out_stored")

        block = top.enter_context(nc.Block())

        def slot_of(n, j):
            return n % 2 * ND + j

        def mbase(bp):
            return bp * 8

        NCONST = 11

        @block.sync
        def _(sp):
            def load_ctx(bp):
                sp.dma_start(ctx_cur[:], ctx_in[bass.ds(bp, 1)].rearrange("a (t p) c -> p (a t) c", p=P)
                             ).then_inc(ctx_loaded, 16)

            load_ctx(0)
            for dst, src in (
                (win_raw, in_proj_w.rearrange("(j p) c -> p j c", p=P)),
                (xp_raw, x_proj_w),
                (dp_raw[:], dt_proj_w.rearrange("(j p) r -> p j r", p=P)),
                (cw[:], conv_w.rearrange("(j p) a k -> p j (a k)", p=P)),
                (Aneg[:], A_log.rearrange("(j p) n -> p j n", p=P)),
                (gate_raw[:], gate_w),
            ):
                sp.dma_start(dst, src).then_inc(consts_in, 16)
            with nc.allow_non_contiguous_dma(reason="four short columns"):
                for dst, src in ((cb, conv_b), (db, dt_proj_b), (Dv, D_in)):
                    sp.dma_start(dst[:], src.rearrange("(j p) -> p j", p=P)).then_inc(consts_in, 16)
            sp.dma_start(tg[:, 0:1], g_xattn.partition_broadcast(P)).then_inc(consts_in, 16)
            sp.dma_start(tg[:, 1:2], g_ffn.partition_broadcast(P)).then_inc(consts_in, 16)
            sp.dma_start(x_tok[:, 0:NL, :], x[0].rearrange("(t p) c -> p t c", p=P)).then_inc(x_in, 16)

            def store_c(bp):
                sp.wait_ge(misc_read[0], mbase(bp) + 5)
                sp.dma_start(c_rows[bass.ds(bp, 1)].rearrange("a n l -> n (a l)"),
                             xdbl[RK + NS:XR, :]).then_inc(c_stored, 16)

            def load_c(b, n):
                if n == 0:
                    sp.wait_ge(c_stored, 16 * (b + 1))
                sp.wait_ge(prod_ready, (b * NS + n + 1) * ND)
                src = c_rows[bass.ds(b, 1), n, :].rearrange("a l -> (a l)").partition_broadcast(P)
                sp.dma_start(cbc[:, n % 2, :], src).then_inc(c_loaded[n % 2], 16)

            store_c(0)
            load_c(0, 0)
            load_c(0, 1)
            sp.dma_start(x_tok[:, NL:, :], x[1:].rearrange("b (t p) c -> p (b t) c", p=P)).then_inc(x_in, 16)
            sp.wait_ge(consts_made, 3)
            with sp.Fori(0, NB - 1) as b:
                sp.wait_ge(misc_full[1], mbase(b) + 1)
                load_ctx(b + 1)
                for n in range(2, NS):
                    load_c(b, n)
                    if n == 11:
                        store_c(b + 1)
                    if n == 5:
                        sp.dma_start(slot_in[bass.ds(b * ZROWS, ZROWS), :].rearrange("(s p) c -> p s c", p=P),
                                     ztile[:].unsqueeze(1).broadcast_to([P, ZROWS // P, H])).then_inc(zeroed, 16)
                load_c(b + 1, 0)
                load_c(b + 1, 1)
            for n in range(2, NS):
                load_c(NB - 1, n)

            def load_shared(half):
                g0 = half * INTER
                gu = shared_gate_up.rearrange("(k p) c -> p k c", p=P)
                sp.dma_start(raw_gu[:, :, 0:INTER], gu[:, :, g0:g0 + INTER]).then_inc(raw_loaded, 16)
                sp.dma_start(raw_gu[:, :, INTER:], gu[:, :, g0 + 2 * INTER:g0 + 3 * INTER]).then_inc(raw_loaded, 16)
                sp.dma_start(raw_d[:, 0:2, :], shared_down[g0:g0 + 2 * P, :].rearrange("(k p) c -> p k c", p=P)
                             ).then_inc(raw_loaded, 16)
                sp.dma_start(raw_d[0:ILAST, 2, :], shared_down[g0 + 2 * P:g0 + INTER, :]).then_inc(raw_loaded, 16)

            def load_expert(e, cond=None):
                gu = w_gate_up[bass.ds(e, 1)].rearrange("a (k p) c -> p (a k) c", p=P)
                dn = w_down[bass.ds(e, 1)].rearrange("a i c -> (a i) c")
                for dst, src in ((raw_gu[:, 0:2, :], gu[:, 0:2, :]), (raw_gu[:, 2:4, :], gu[:, 2:4, :]),
                                 (raw_d[:, 0:2, :], dn[0:2 * P, :].rearrange("(k p) c -> p k c", p=P)),
                                 (raw_d[0:ILAST, 2, :], dn[2 * P:INTER, :])):
                    sp.dma_start(dst, src, cond=cond).then_inc(raw_loaded, 16)

            def load_tile(src, q, qq, wait=True):
                if wait:
                    sp.wait_ge(xT_done, q - 1)
                sp.dma_start(xin[:, qq % 2, :], src).then_inc(xin_ready[qq % 2], 16)

            def tile_rows(rows, t):
                return rows[bass.ds(t * P, P), :]

            def store_xn(t, k):
                sp.wait_ge(xn_made, t + 1)
                sp.dma_start(tile_rows(xn_rows, t), xin[:, k, :]).then_inc(xn_stored[k], 16)

            sp.wait_ge(p1_done, 1)
            load_shared(0)
            store_xn(0, 0)
            store_xn(1, 1)
            sp.wait_ge(w_split, 1)
            load_shared(1)
            with sp.Fori(1, NT // 2) as m:
                for k in range(2):
                    store_xn(m * 2 + k, k)
            for k in range(2):
                sp.wait_ge(xn_stored[k], 16 * (NT // 2))
            with sp.Fori(0, NB1 // 2) as m:
                for k in range(2):
                    load_tile(tile_rows(xn_rows, m * 2 + k), m * 2 + k + NT, k)
            Q0 = NT + NB1
            sp.wait_ge(table_ready, 3)
            sp.wait_ge(w_split, 2)
            e0 = sp.value_load(dk_i[0:1, 0:1], min_val=0, max_val=NE - 1)
            load_expert(e0)
            for k in range(4):
                sp.wait_ge(scat[k], 32 * (NT // 4))
            load_tile(tile_rows(slot_in, 0), Q0, 0)
            load_tile(tile_rows(slot_in, 1), Q0 + 1, 1)
            sp.wait_ge(w_split, 3)
            e1 = sp.value_load(dk_i[0:1, 1:2], min_val=0, max_val=NE - 1)
            load_expert(e1)

            def prefetch_expert(r):
                rank = sp.value_load(rank_i[0:1, bass.ds(r, 1)], min_val=0, max_val=NE)
                chg = sp.value_load(chg_i[0:1, bass.ds(r, 1)], min_val=0, max_val=1)
                e = sp.value_load(dk_i[0:1, bass.ds(rank + 2, 1)], min_val=0, max_val=NE - 1)
                sp.wait_ge(w_split, rank + 4)
                load_expert(e, cond=chg)

            with sp.Fori(0, SLOTS // 2 - 1) as m:
                for k in range(2):
                    r = m * 2 + k
                    load_tile(tile_rows(slot_in, r + 2), Q0 + r + 2, k)
                    prefetch_expert(r)
            for r in range(SLOTS - 2, SLOTS):
                load_tile(tile_rows(xn_rows, r + 2 - SLOTS + NB1), Q0 + r + 2, r % 2)
                prefetch_expert(r)
            Q1 = Q0 + SLOTS
            with sp.Fori(1, (NT - NB1) // 2) as m:
                for k in range(2):
                    load_tile(tile_rows(xn_rows, m * 2 + k + NB1), m * 2 + k + Q1, k)
            out_t = out.rearrange("b (t p) c -> p (b t) c", p=P)
            with sp.Fori(0, NB1) as m:
                for k in range(2):
                    t = m + k * NB1
                    sp.wait_ge(f_done, m * 2 + k + 1)
                    sp.dma_start(out_t[:, bass.ds(t, 1), :], x_tok[:, bass.ds(t, 1), :]).then_inc(out_stored, 16)
            sp.wait_ge(out_stored, 16 * NT)
            sp.wait_ge(raw_loaded, 64 * (4 + SLOTS))

        @block.gpsimd
        def _(pool):
            pool.memset(ident[:], 0.0).then_inc(ident_made, 1)
            pool.wait_ge(ident_made, 1)
            pool.affine_select(out=ident[:], in_=ident[:], compare_op=ALU.not_equal, fill=1.0, base=0,
                               pattern=[[-1, P]], channel_multiplier=1).then_inc(ident_made, 1)
            pool.memset(zb16[:], 0.0).then_inc(consts_made, 1)
            pool.memset(zmov[:], 0.0).then_inc(consts_made, 1)
            pool.memset(ztile[:], 0.0).then_inc(consts_made, 1)
            pool.sem_inc(prod_ready, RING)

            def products(b, n):
                pool.wait_ge(c_loaded[n % 2], 16 * (b * (NS // 2) + n // 2 + 1))
                for j in range(ND):
                    i = b * ITEMS + n * ND + j
                    pool.wait_ge(scanned, i + 1 + RING)
                    pool.wait_ge(prod_used, i + 1)
                    pool.tensor_tensor(prod[:, slot_of(n, j), :], hst[:, slot_of(n, j), :], cbc[:, n % 2, :],
                                       ALU.mult).then_inc(prod_ready, 1)

            with pool.Fori(0, NB) as b:
                for n in range(NS):
                    products(b, n)

            pool.wait_ge(p1_done, 1)
            pool.iota(iota_e[:], pattern=[[1, NE]], base=0, channel_multiplier=0,
                      allow_small_or_imprecise_dtypes=True).then_inc(p2_consts, 1)
            pool.iota(iota_s[:], pattern=[[1, SLOTS]], base=0, channel_multiplier=0,
                      allow_small_or_imprecise_dtypes=True).then_inc(p2_consts, 1)
            pool.iota(iota_k[:], pattern=[[1, NDK]], base=0, channel_multiplier=0,
                      allow_small_or_imprecise_dtypes=True).then_inc(p2_consts, 1)
            pool.memset(ones[:], 1.0).then_inc(p2_consts, 1)
            pool.memset(onesf[:], 1.0).then_inc(p2_consts, 1)
            pool.memset(upper[:], 1.0).then_inc(p2_consts, 1)
            pool.memset(hbuf[:], 0.0).then_inc(p2_consts, 1)
            pool.wait_ge(p2_consts, 7)
            pool.affine_select(out=upper[:], in_=upper[:], compare_op=ALU.is_gt, fill=0.0, base=0,
                               pattern=[[1, P]], channel_multiplier=-1).then_inc(p2_consts, 1)

            def load_g(t):
                k = t % 4
                if t >= 4:
                    pool.wait_ge(scat[k], 32 * (t // 4))
                pool.dma_start(gbuf[:, k, :], xn_rows[t * P:(t + 1) * P, :]).then_inc(g_loaded[k], 16)

            for k in range(2):
                pool.wait_ge(xn_stored[k], 16 * (NT // 2))
            for t in range(4):
                load_g(t)
            pool.wait_ge(pos_ready, 1)
            pool.wait_ge(zeroed, 16 * (NB - 1))
            for t in range(NT):
                k = t % 4
                pool.wait_ge(g_loaded[k], 16 * (t // 4 + 1))
                for c in range(2):
                    pool.indirect_dma_start(
                        slot_in, bass.IndirectOffsetOnAxis(ap=posi[:, c, t:t + 1].bitcast(U32), axis=0),
                        gbuf[:, k, :], None).then_inc(scat[k], 16)
                if t + 4 < NT:
                    load_g(t + 4)

            Q0 = NT + NB1
            with pool.Fori(0, SLOTS // 2) as m:
                for k in range(2):
                    pool.wait_ge(y_read, Q0 + m * 2 + k + 1 + 2)
                    pool.dma_start(slot_out[bass.ds((m * 2 + k) * P, P), :],
                                   yout[:, k, :]).then_inc(y_stored[k], 16)
            pool.wait_ge(y_stored[0], 16 * (SLOTS // 2))
            pool.wait_ge(y_stored[1], 16 * (SLOTS // 2))
            for i in range(NT):
                t = (i % 2) * NB1 + i // 2
                if i >= 2:
                    pool.wait_ge(f_done, i - 1)
                else:
                    for k in (0, 1):
                        pool.wait_ge(scat[2 * i + k], 32 * (NT // 4))
                for c in range(2):
                    pool.indirect_dma_start(
                        gbuf[:, 2 * (i % 2) + c, :], None, slot_out,
                        bass.IndirectOffsetOnAxis(ap=posi[:, c, t:t + 1].bitcast(U32), axis=0),
                    ).then_inc(gathered[i % 2], 16)

        @block.tensor
        def _(pe):
            mm, tr = nc.tensor.matmul, nc.tensor.transpose
            pe.wait_ge(ident_made, 2)
            pe.wait_ge(consts_made, 3)
            pe.wait_ge(consts_in, 16 * NCONST)
            for k in range(NK):
                for j in range(ND):
                    last = tr(mp[k][:, j * P:(j + 1) * P], win_raw[:, j, k * P:(k + 1) * P], ident[:])
                last.then_inc(wt_full, 1)
            for j in range(ND):
                last = tr(dbu_ps[0][:, j * XR:(j + 1) * XR], xp_raw[:, j * P:(j + 1) * P], ident[0:XR, 0:XR])
            last.then_inc(wt_full, 1)
            for j in range(ND):
                last = tr(dbu_ps[1][0:RK, j * P:(j + 1) * P], dp_raw[:, j, :], ident[:])
            last.then_inc(wt_full, 1)
            pe.wait_ge(wt_read, 4)
            pe.sem_inc(dbu_ready, 2 * ND)
            pe.sem_inc(prod_used, RING)

            def ctx_transposes(bp):
                pe.wait_ge(ctx_loaded, 16 * (bp + 1))
                for k in range(NK):
                    pe.wait_ge(misc_read[k], mbase(bp) + 1)
                    for t in range(NL):
                        last = tr(mp[k][:, t * P:(t + 1) * P], ctx_cur[:, t, k * P:(k + 1) * P], ident[:])
                    last.then_inc(misc_full[k], 1)

            def in_proj(bp, j):
                u = 1 + j // 2
                pe.wait_ge(misc_read[j % 2], mbase(bp) + u + 1)
                if j == 0:
                    pe.wait_ge(misc_read[1], mbase(bp) + 2)
                for k in range(NK):
                    last = mm(mp[j % 2][:], winT[:, k, j * P:(j + 1) * P], ctxT[:, k, :],
                              start=k == 0, stop=k == NK - 1)
                last.then_inc(misc_full[j % 2], 1)

            def x_proj(bp):
                pe.wait_ge(misc_read[0], mbase(bp) + 4)
                pe.wait_ge(silu_done, bp * 2 * ND + ND)
                for j in range(ND):
                    last = mm(mp[0][0:XR, :], xpT[:, j, :],
                              xs[:, bass.ds(bp % 2, 1), j, :].rearrange("p a l -> p (a l)"),
                              start=j == 0, stop=j == ND - 1)
                last.then_inc(misc_full[0], 1)

            def b_transposes(bp):
                pe.wait_ge(misc_read[0], mbase(bp) + 5)
                pe.wait_ge(misc_read[1], mbase(bp) + 4)
                pe.sem_inc(wait_carrier, 1)
                for t in range(NL):
                    last = tr(mp[1][:, t * XR:(t + 1) * XR], xdbl[:, t * P:(t + 1) * P], ident[0:XR, 0:XR])
                last.then_inc(misc_full[1], 1)

            def dt_proj(bp, j):
                pe.wait_ge(misc_read[0], mbase(bp) + 5 + j)
                mm(mp[0][:], dpT[:, j * P:(j + 1) * P], xdbl[0:RK, :], start=True,
                   stop=True).then_inc(misc_full[0], 1)

            def du_transposes(bp, j):
                pe.wait_ge(du_ready, bp * ND + j + 1)
                pe.wait_ge(misc_read[1], mbase(bp) + 5 + j)
                for t in range(NL):
                    last = tr(mp[1][:, t * P:(t + 1) * P], du[:, j % 2, t * P:(t + 1) * P], ident[:])
                last.then_inc(misc_full[1], 1)

            def step(b, n, j):
                i = b * ITEMS + n * ND + j
                if j == 0:
                    pe.wait_ge(dbut_ready, b * NS + n + 1)
                    pe.wait_ge(dbut_last, b * NS + n + 1)
                pe.wait_ge(scanned, i - 1 + RING)
                for t in range(NL):
                    last = tr(dbu_ps[j % 2][:, t * P:(t + 1) * P], dbuT[:, n % 2, t, j * P:(j + 1) * P], ident[:])
                last.then_inc(dbu_ready, 1)

            def open_y(b, j):
                pe.wait_ge(y_taken, b * ND + j + 1)
                mm(y_ps[j][:], zb16[:], zmov[:], start=True, stop=False)

            def close_y(b, j):
                mm(y_ps[j][:], zb16[:], zmov[:], start=False, stop=True).then_inc(y_done, 1)

            def add_y(b, n, j):
                i = b * ITEMS + n * ND + j
                pe.wait_ge(prod_ready, i + 1 + RING)
                mm(y_ps[j][:], ident[:], prod[:, slot_of(n, j), :], start=False, stop=False).then_inc(prod_used, 1)

            def y_transpose(b, t, prepared):
                pe.wait_ge(y3_ready, (b + 1) * ND)
                if t < 2:
                    pe.wait_ge(misc_read[t], mbase(prepared) + 1)
                else:
                    pe.wait_ge(post_read[t % 2], b * 2 + 1)
                for j in range(ND):
                    last = tr(mp[t % 2][:, j * P:(j + 1) * P], y3[:, j, t * P:(t + 1) * P], ident[:])
                last.then_inc(post_full[t % 2], 1)

            def pieces(bp, n, j):
                if (n, j) == (3, 1):
                    ctx_transposes(bp)
                elif 4 <= n < 8 and j == 0:
                    in_proj(bp, n - 4)
                elif (n, j) == (9, 1):
                    x_proj(bp)
                elif (n, j) == (10, 0):
                    b_transposes(bp)
                elif 10 <= n < 14 and j == 1:
                    dt_proj(bp, n - 10)
                elif 11 <= n < 15 and j == 3:
                    du_transposes(bp, n - 11)

            def first_steps(b, before=None):
                for j in range(ND):
                    step(b, 0, j)
                    if before is not None:
                        add_y(before, NS - 1, j)
                        close_y(before, j)
                for j in range(ND):
                    step(b, 1, j)
                    open_y(b, j)
                    add_y(b, 0, j)
                    if before is not None and j >= 2:
                        y_transpose(before, 2 * j - 4, before + 2)
                        y_transpose(before, 2 * j - 3, before + 2)

            pe.wait_ge(misc_read[0], 1)
            for n in range(2, NS):
                for j in range(ND):
                    pieces(0, n, j)
            first_steps(0)
            with pe.Fori(0, NB - 1) as b:
                for n in range(2, NS):
                    for j in range(ND):
                        step(b, n, j)
                        add_y(b, n - 1, j)
                        pieces(b + 1, n, j)
                first_steps(b + 1, before=b)
            for n in range(2, NS):
                for j in range(ND):
                    step(NB - 1, n, j)
                    add_y(NB - 1, n - 1, j)
            for j in range(ND):
                add_y(NB - 1, NS - 1, j)
                close_y(NB - 1, j)
            for t in range(NL):
                y_transpose(NB - 1, t, NB)

            pe.wait_ge(p1_done, 1)
            for k in range(KH):
                last = tr(psHT[:, k, 0:NE], gate_raw[:, k * P:(k + 1) * P], ident[0:NE, 0:NE])
            last.then_inc(gw_full, 1)

            def transpose_x(q, k, made=False):
                if made:
                    pe.wait_ge(xn_made, q + 1)
                else:
                    pe.wait_ge(xin_ready[k], 16 * (((q - NT) >> 1) + 1))
                pe.wait_ge(xl_ready, q + 1)
                for c in range(KH):
                    last = tr(psT[:, c, :], xin[:, k, c * P:(c + 1) * P], ident[:])
                last.then_inc(xT_done, 1)

            def half_product(ps, w0, k, buf):
                n = 0
                for c in range(KH):
                    for a, w in ((xh, wgu_h), (xh, wgu_l), (xl, wgu_h)):
                        last = mm(ps[:, 0:INTER], a[:, k, c, :], w_at(w, buf)[:, c, w0:w0 + INTER],
                                  start=n == 0, stop=n == 3 * KH - 1)
                        n += 1
                return last

            def w_at(w, buf):
                if isinstance(buf, int):
                    return w[:, buf]
                return w[:, bass.ds(buf, 1)].rearrange("p a k c -> p (a k) c")

            def transpose_h(q, k):
                pe.wait_ge(h_ready, q + 1 + 2)
                pe.wait_ge(hl_ready, q + 2)
                for c in range(3):
                    last = tr(psHT[:, c, :], hbuf[:, k, c * P:(c + 1) * P], ident[:])
                last.then_inc(hT_done, 1)

            def down(q, k, buf):
                pe.wait_ge(hl_ready, q + 1 + 2)
                pe.wait_ge(y_read, q + 1)
                n = 0
                for c in range(3):
                    rows = P if c < 2 else ILAST
                    for a, w in ((hh, wd_h), (hh, wd_l), (hl, wd_h)):
                        last = mm(psY[k][:], a[0:rows, k, c, :], w_at(w, buf)[0:rows, c, :],
                                  start=n == 0, stop=n == 8)
                        n += 1
                last.then_inc(y_full, 1)

            def slot(q, k, buf, prev_buf, router=False, first=False, last_slot=False, last_made=False):
                pe.wait_ge(xl_ready, q + 2)
                pe.wait_ge(h_ready, q + 1)
                half_product(psG[k], 0, k, buf).then_inc(g_done, 1)
                if router:
                    n = 0
                    for c in range(KH):
                        for a, w in ((xh, gw_h), (xh, gw_l), (xl, gw_h)):
                            mm(psG[k][:, INTER:INTER + NE], a[:, k, c, :], w[:, c, :],
                               start=n == 0, stop=n == 3 * KH - 1)
                            n += 1
                if not first:
                    transpose_h(q - 1, 1 - k)
                if not last_slot:
                    transpose_x(q + 1, 1 - k, made=router and not last_made)
                half_product(psU[k], INTER, k, buf).then_inc(gu_done, 1)
                if not first:
                    down(q - 1, 1 - k, prev_buf)

            transpose_x(0, 0, made=True)
            pe.wait_ge(w_split, 1)
            pe.wait_ge(gw_ready, 1)
            slot(0, 0, 1, 1, router=True, first=True)
            slot(1, 1, 1, 1, router=True)
            with pe.Fori(1, NT // 2 - 1) as m:
                for k in range(2):
                    slot(m * 2 + k, k, 1, 1, router=True)
            slot(NT - 2, 0, 1, 1, router=True)
            slot(NT - 1, 1, 1, 1, router=True, last_made=True)
            pe.wait_ge(w_split, 2)
            slot(NT, 0, 2, 1)
            slot(NT + 1, 1, 2, 2)
            pe.wait_ge(rt_mask, 1)
            pe.wait_ge(hl_ready, NT + 1 + 2)
            counts = psHT[:].rearrange("p c n -> p (c n)")
            marks = msum[:].rearrange("p t e -> p (t e)")
            mm(counts[:, 0:NT * NE], upper[:], marks, start=True, stop=True)
            mm(counts[:, NT * NE:], ones[:], marks, start=True, stop=True).then_inc(rt_count, 1)
            pe.wait_ge(cnt_read, 1)
            with pe.Fori(1, NB1 // 2) as m:
                for k in range(2):
                    slot(m * 2 + k + NT, k, 2, 2)

            def routed_slot(r, k, first=False):
                pe.sem_inc(wait_carrier, 1)
                rank = pe.value_load(rank_i[0:1, bass.ds(r, 1)], min_val=0, max_val=NE)
                pe.wait_ge(w_split, rank + 3)
                if first:
                    slot(r + Q0, k, rank % 2, 2)
                else:
                    pe.sem_inc(wait_carrier, 1)
                    before = pe.value_load(rank_i[0:1, bass.ds(r - 1, 1)], min_val=0, max_val=NE)
                    slot(r + Q0, k, rank % 2, before % 2)

            Q0 = NT + NB1
            pe.wait_ge(table_ready, 3)
            routed_slot(0, 0, first=True)
            routed_slot(1, 1)
            with pe.Fori(1, SLOTS // 2) as m:
                for k in range(2):
                    routed_slot(m * 2 + k, k)
            Q1 = Q0 + SLOTS
            pe.sem_inc(wait_carrier, 1)
            before = pe.value_load(rank_i[0:1, SLOTS - 1:SLOTS], min_val=0, max_val=NE)
            slot(Q1, 0, 2, before % 2)
            slot(Q1 + 1, 1, 2, 2)
            with pe.Fori(1, (NT - NB1) // 2 - 1) as m:
                for k in range(2):
                    slot(m * 2 + k + Q1, k, 2, 2)
            QE = Q1 + NT - NB1
            slot(QE - 2, 0, 2, 2)
            slot(QE - 1, 1, 2, 2, last_slot=True)
            transpose_h(QE - 1, 1)
            down(QE - 1, 1, 2)

        @block.scalar
        def _(act):
            def par(buf, b):
                return buf[:, bass.ds(b % 2, 1)].rearrange("p a j l -> p (a j) l")

            act.wait_ge(consts_in, 16 * NCONST)
            nc.scalar.activation(Aneg[:], Aneg[:], ACT.Exp).then_inc(a_exp, 1)
            nc.scalar.activation(tg[:], tg[:], ACT.Tanh).then_inc(tg_ready, 1)
            act.wait_ge(a_exp, 1)
            nc.scalar.mul(Aneg[:], Aneg[:], -1.0).then_inc(a_ready, 1)
            act.wait_ge(a_ready, 1)
            nc.scalar.preload_act_table_set("natural_log_exp_and_others")

            def ln_seed(rs, ready, done, count):
                act.wait_ge(ready, count)
                nc.scalar.activation(rs[:, 1, :], rs[:, 0, :], ACT.Ln).then_inc(done, 1)
                act.wait_ge(done, count * 2 - 1)
                nc.scalar.activation(rs[:, 2, :], rs[:, 1, :], ACT.Exp, scale=-0.5).then_inc(done, 1)

            def silus(bp):
                act.wait_ge(conv_tap, (bp + 1) * ND * TAPS)
                for j in range(ND):
                    nc.scalar.activation(par(xs, bp)[:, j, :], par(xs, bp)[:, j, :], ACT.Silu
                                         ).then_inc(silu_done, 1)
                act.wait_ge(ln1_dve, (bp + 1) * 12)
                act.sem_inc(wait_carrier, 1)
                for j in range(ND):
                    nc.scalar.activation(par(zs, bp)[:, j, :],
                                         x_tok[:, bass.ds(bp * NL + j, 1), :].rearrange("p a c -> p (a c)"),
                                         ACT.Silu, bias=rs1[:, 4, j:j + 1],
                                         scale=rs1[:, 3, j:j + 1]).then_inc(silu_done, 1)
                nc.scalar.preload_act_table_set("natural_log_exp_and_others")

            def softplus_parts(bp, j):
                if j > 0 or not isinstance(bp, int):
                    act.wait_ge(du_ready, bp * ND + j)
                act.wait_ge(misc_full[0], mbase(bp) + 5 + j)
                nc.scalar.activation(sp_a, mp[0][:], ACT.Abs, bias=db[:, j:j + 1]).then_inc(sp_abs, 1)
                act.wait_ge(sp_abs, bp * ND + j + 1)
                nc.scalar.activation(sp_u, sp_a, ACT.Exp, scale=-1.0).then_inc(sp_exp, 1)
                act.wait_ge(sp_exp, bp * ND + j + 1)
                nc.scalar.activation(sp_l, sp_u, ACT.Ln, bias=1.0).then_inc(sp_ln, 1)

            def du_to_time(bp, j):
                act.wait_ge(misc_full[1], mbase(bp) + 5 + j)
                nc.scalar.copy(par(duT, bp)[:, :, j * P:(j + 1) * P],
                               mp[1][:].rearrange("p (t d) -> p t d", t=NL)).then_inc(dut_ready, 1)
                act.wait_ge(dut_ready, bp * ND + j + 1)
                act.sem_inc(misc_read[1], 1)

            def decay(b, n, j):
                act.wait_ge(scanned, b * ITEMS + n * ND + j + 1)
                act.sem_inc(wait_carrier, 1)
                nc.scalar.activation(dA[:, slot_of(n, j), :], par(dts, b)[:, j, :], ACT.Exp,
                                     scale=Aneg[:, j, n:n + 1]).then_inc(da_ready, 1)

            def input_terms(b, n):
                if n == 0:
                    act.wait_ge(dut_ready, (b + 1) * ND)
                    act.sem_inc(wait_carrier, 1)
                act.wait_ge(dbu_ready, (b * NS + n + 1) * ND)
                for t in range(NL - 1):
                    last = nc.scalar.activation(dbuT[:, n % 2, t, :], par(duT, b)[:, t, :], ACT.Copy,
                                                scale=par(BT, b)[:, t, RK + n:RK + n + 1])
                last.then_inc(dbut_ready, 1)

            def step(b, n, bp=None):
                for j in range(ND):
                    if (n, j) == (0, 0):
                        act.wait_ge(du_ready, (b + 1) * ND)
                        act.sem_inc(wait_carrier, 1)
                    decay(b, n, j)
                    if j == 2:
                        input_terms(b, n)
                    if bp is not None:
                        pieces(bp, n, j)

            def pieces(bp, n, j):
                if (n, j) == (6, 3):
                    ln_seed(rs1, ln1_var, ln1_act, bp + 1)
                elif (n, j) == (9, 3):
                    silus(bp)
                elif 12 <= n < 16 and j == 1:
                    softplus_parts(bp, n - 12)
                if 13 <= n < 16 and j == 3:
                    du_to_time(bp, n - 13)
                if (n, j) == (0, 1):
                    du_to_time(bp, 3)

            for n in range(2, NS):
                for j in range(ND):
                    pieces(0, n, j)
            step(0, 0, 0)
            step(0, 1)
            with act.Fori(0, NB - 1) as b:
                for n in range(2, NS):
                    step(b, n, b + 1)
                step(b + 1, 0, b + 1)
                step(b + 1, 1)
            for n in range(2, NS):
                step(NB - 1, n)
            ln_seed(rs2, ln2_var, ln2_act, 1)

            act.wait_ge(p1_done, 1)
            act.wait_ge(gw_full, 1)
            nc.scalar.copy(gw_h[:], psHT[:, :, 0:NE]).then_inc(gw_hi, 1)

            def split_hi(loaded, dst):
                act.wait_ge(raw_loaded, loaded)
                for c in range(KH):
                    nc.scalar.copy(dst(wgu_h)[:, c, :], raw_gu[:, c, :]).then_inc(w_hi, 1)
                for c in range(3):
                    rows = P if c < 2 else ILAST
                    nc.scalar.copy(dst(wd_h)[0:rows, c, :], raw_d[0:rows, c, :]).then_inc(w_hi, 1)

            def slot(q, k, first=False, last_slot=False):
                if not first:
                    act.wait_ge(hT_done, q)
                    nc.scalar.copy(hh[:, 1 - k, :, :], psHT[:, 0:3, :]).then_inc(hh_ready, 1)
                if not last_slot:
                    act.wait_ge(xT_done, q + 2)
                    nc.scalar.copy(xh[:, 1 - k, :, :], psT[:]).then_inc(xh_ready, 1)
                act.wait_ge(g_done, q + 1)
                nc.scalar.activation(sg[:, k, :], psG[k][:, 0:INTER], ACT.Silu).then_inc(sg_ready, 1)

            def static(buf):
                return lambda w: w[:, buf]

            split_hi(64, static(1))
            act.wait_ge(xT_done, 1)
            nc.scalar.copy(xh[:, 0, :, :], psT[:]).then_inc(xh_ready, 1)
            slot(0, 0, first=True)
            slot(1, 1)
            split_hi(128, static(2))
            with act.Fori(1, NT // 2) as m:
                for k in range(2):
                    slot(m * 2 + k, k)
            slot(NT, 0)
            slot(NT + 1, 1)
            act.wait_ge(rt_shift, 1)
            nc.scalar.activation(ex[:], ex[:], ACT.Exp).then_inc(rt_act, 1)
            with act.Fori(1, NB1 // 2) as m:
                for k in range(2):
                    slot(m * 2 + k + NT, k)
            split_hi(192, static(0))
            Q0 = NT + NB1
            act.wait_ge(table_ready, 3)

            def routed_slot(r, k):
                slot(r + Q0, k)
                chg = act.value_load(chg_i[0:1, bass.ds(r, 1)], min_val=0, max_val=1)
                rank = act.value_load(rank_i[0:1, bass.ds(r, 1)], min_val=0, max_val=NE)
                buf = (rank + 1) % 2
                with act.If(chg):
                    act.wait_ge(y_full, r + Q0)
                    split_hi(256 + 64 * r, lambda w: w[:, bass.ds(buf, 1)].rearrange("p a k c -> p (a k) c"))

            with act.Fori(0, SLOTS // 2) as m:
                for k in range(2):
                    routed_slot(m * 2 + k, k)
            Q1 = Q0 + SLOTS
            with act.Fori(0, (NT - NB1) // 2 - 1) as m:
                for k in range(2):
                    slot(m * 2 + k + Q1, k)
            QE = Q1 + NT - NB1
            slot(QE - 2, 0)
            slot(QE - 1, 1, last_slot=True)
            act.wait_ge(hT_done, QE)
            nc.scalar.copy(hh[:, 1, :, :], psHT[:, 0:3, :]).then_inc(hh_ready, 1)

        @block.vector
        def _(dve):
            V = nc.vector

            def par(buf, b):
                return buf[:, bass.ds(b % 2, 1)].rearrange("p a j l -> p (a j) l")

            dve.wait_ge(wt_full, 4)
            for k in range(NK):
                V.tensor_copy(winT[:, k, :], mp[k][:]).then_inc(wt_read, 1)
            V.tensor_copy(xpT[:].rearrange("p j e -> p (j e)"), dbu_ps[0][:, 0:ND * XR]).then_inc(wt_read, 1)
            V.tensor_copy(dpT[:], dbu_ps[1][0:RK, :]).then_inc(wt_read, 1)
            for k in range(2):
                dve.sem_inc(misc_read[k], 1)
            dve.sem_inc(scanned, RING)
            dve.sem_inc(y_taken, ND)
            dve.wait_ge(x_in, 16)
            dve.wait_ge(consts_in, 16 * NCONST)

            def tile_of(b, j):
                return x_tok[:, bass.ds(b * NL + j, 1), :].rearrange("p a c -> p (a c)")

            def ln_refine(rs, n, c0, steps):
                V.tensor_tensor(rs[:, 1, :], rs[:, 2, :], rs[:, 2, :], ALU.mult).then_inc(steps, 1)
                dve.wait_ge(steps, c0 + 1)
                V.scalar_tensor_tensor(rs[:, 3, :], rs[:, 1, :], -0.5, rs[:, 0, :], ALU.mult,
                                       ALU.mult).then_inc(steps, 1)
                dve.wait_ge(steps, c0 + 2)
                V.scalar_tensor_tensor(rs[:, 3, :], rs[:, 3, :], 1.5, rs[:, 2, :], ALU.add,
                                       ALU.mult).then_inc(steps, 1)
                dve.wait_ge(steps, c0 + 3)

            def z_stats(bp, j):
                V.bn_stats(st1[:, j, :], tile_of(bp, j)).then_inc(ln1_dve, 1)

            def z_var(bp):
                dve.wait_ge(ln1_dve, bp * 12 + ND)
                dve.sem_inc(wait_carrier, 1)
                for j in range(ND):
                    V.bn_aggr(mv1[:, j, :], st1[:, j, :]).then_inc(ln1_dve, 1)
                dve.wait_ge(ln1_dve, bp * 12 + 2 * ND)
                V.tensor_scalar(rs1[:, 0, :], mv1[:, :, 1], EPS, None, ALU.add).then_inc(ln1_var, 1)

            def z_scale(bp):
                dve.wait_ge(ln1_act, (bp + 1) * 2)
                ln_refine(rs1, ND, bp * 12 + 8, ln1_dve)
                V.scalar_tensor_tensor(rs1[:, 4, :], mv1[:, :, 0], -1.0, rs1[:, 3, :], ALU.mult,
                                       ALU.mult).then_inc(ln1_dve, 1)

            def ctx_to_sbuf(bp, k):
                dve.wait_ge(misc_full[k], mbase(bp) + 1)
                V.tensor_copy(ctxT[:, k, :], mp[k][:]).then_inc(misc_read[k], 1)

            def conv(bp, j, s):
                k, u = j % 2, 1 + j // 2
                xj = par(xs, bp)[:, j, :]
                c0 = (bp * ND + j) * TAPS
                if s == 0:
                    dve.wait_ge(misc_full[k], mbase(bp) + u + 1)
                    V.tensor_scalar(xj, mp[k][:], cw[:, j, TAPS - 1:TAPS], cb[:, j:j + 1], ALU.mult,
                                    ALU.add).then_inc(conv_tap, 1)
                    return
                dve.wait_ge(conv_tap, c0 + s)
                V.scalar_tensor_tensor(xj[:, s:], mp[k][:, 0:L - s], cw[:, j, TAPS - 1 - s:TAPS - s],
                                       xj[:, s:], ALU.mult, ALU.add).then_inc(conv_tap, 1)
                if s == TAPS - 1:
                    dve.wait_ge(conv_tap, c0 + TAPS)
                    dve.sem_inc(misc_read[k], 1)

            def x_proj_to_sbuf(bp):
                if not (isinstance(bp, int) and bp == 0):
                    dve.wait_ge(c_stored, 16 * bp)
                dve.wait_ge(misc_full[0], mbase(bp) + 4)
                V.tensor_copy(xdbl[:], mp[0][0:XR, :]).then_inc(misc_read[0], 1)

            def b_to_sbuf(bp):
                dve.wait_ge(misc_full[1], mbase(bp) + 4)
                V.tensor_copy(par(BT, bp).rearrange("p t e -> p (t e)"),
                              mp[1][:, 0:NL * XR]).then_inc(misc_read[1], 1)

            def softplus_in(bp, j):
                dve.wait_ge(misc_full[0], mbase(bp) + 5 + j)
                dve.wait_ge(sp_abs, bp * ND + j + 1)
                V.tensor_scalar(sp_r, mp[0][:], db[:, j:j + 1], 0.0, ALU.add,
                                ALU.max).then_inc(misc_read[0], 1)

            def softplus_out(bp, j, part):
                c0 = (bp * ND + j) * 4
                if part == 0:
                    dve.wait_ge(sp_ln, bp * ND + j + 1)
                    V.tensor_scalar(sp_t[:], sp_u, 1.0, -1.0, ALU.add, ALU.add).then_inc(sp_dve, 1)
                    dve.wait_ge(misc_read[0], mbase(bp) + 6 + j)
                    V.tensor_tensor(sp_r, sp_r, sp_l, ALU.add).then_inc(sp_dve, 1)
                elif part == 1:
                    dve.wait_ge(sp_dve, c0 + 2)
                    V.tensor_tensor(sp_t[:], sp_t[:], sp_u, ALU.subtract).then_inc(sp_dve, 1)
                    dve.wait_ge(sp_dve, c0 + 3)
                    V.tensor_tensor(par(dts, bp)[:, j, :], sp_r, sp_t[:], ALU.subtract).then_inc(sp_dve, 1)
                else:
                    dve.wait_ge(sp_dve, c0 + 4)
                    dve.wait_ge(silu_done, bp * 2 * ND + j + 1)
                    V.tensor_tensor(du[:, j % 2, :], par(dts, bp)[:, j, :], par(xs, bp)[:, j, :],
                                    ALU.mult).then_inc(du_ready, 1)

            def scan(b, n, j):
                i = b * ITEMS + n * ND + j
                dve.wait_ge(da_ready, i + 1)
                dve.wait_ge(dbu_ready, i + 1 + 2 * ND)
                dve.wait_ge(prod_ready, i + 1)
                V.tensor_tensor_scan(hst[:, slot_of(n, j), :], dA[:, slot_of(n, j), :], dbu_ps[j % 2][:], 0.0,
                                     ALU.mult, ALU.add).then_inc(scanned, 1)

            def input_terms(b, n):
                if n == 0:
                    dve.wait_ge(dut_ready, (b + 1) * ND)
                dve.wait_ge(dbu_ready, (b * NS + n + 1) * ND)
                dve.sem_inc(wait_carrier, 1)
                t = NL - 1
                V.tensor_scalar(dbuT[:, n % 2, t, :], par(duT, b)[:, t, :], par(BT, b)[:, t, RK + n:RK + n + 1],
                                None, ALU.mult).then_inc(dbut_last, 1)

            def add_du(b, j):
                dve.wait_ge(y_done, b * ND + j + 1)
                V.scalar_tensor_tensor(y3[:, j, :], par(xs, b)[:, j, :], Dv[:, j:j + 1], y_ps[j][:],
                                       ALU.mult, ALU.add).then_inc(y_taken, 1)

            def gate(b, j):
                dve.wait_ge(y_taken, b * ND + j + 1 + ND)
                V.scalar_tensor_tensor(y3[:, j, :], y3[:, j, :], tg[:, 0:1], par(zs, b)[:, j, :],
                                       ALU.mult, ALU.mult).then_inc(y3_ready, 1)

            def residual(b, t):
                dve.wait_ge(post_full[t % 2], b * 2 + t // 2 + 1)
                V.tensor_tensor(tile_of(b, t), tile_of(b, t), mp[t % 2][:], ALU.add).then_inc(x1_ready, 1)
                dve.wait_ge(x1_ready, b * NL + t + 1)
                dve.sem_inc(post_read[t % 2], 1)

            def x1_stats(b, t):
                V.bn_stats(st2[:, bass.ds(b * NL + t, 1), :].rearrange("p a c -> p (a c)"),
                           tile_of(b, t)).then_inc(ln2_dve, 1)

            def post(b, n, j):
                if n == 0:
                    if j >= 1:
                        add_du(b, j - 1)
                    if j >= 2:
                        gate(b, j - 2)
                else:
                    if j == 0:
                        add_du(b, 3)
                        gate(b, 2)
                    elif j == 1:
                        gate(b, 3)
                    else:
                        residual(b, j - 2)

            def rest_of_post(b):
                residual(b, 2)
                residual(b, 3)
                for t in range(NL):
                    x1_stats(b, t)

            def pieces(bp, n, j):
                if n in (2, 3):
                    if j >= 2:
                        z_stats(bp, (n - 2) * 2 + j - 2)
                    if n == 3 and j >= 2:
                        ctx_to_sbuf(bp, j - 2)
                if (n, j) == (4, 0):
                    z_var(bp)
                if 4 <= n < 8 and j >= 1:
                    conv(bp, n - 4, j - 1)
                if 5 <= n < 9 and j == 0:
                    conv(bp, n - 5, 3)
                if (n, j) == (6, 2):
                    z_scale(bp)
                if (n, j) == (9, 2):
                    x_proj_to_sbuf(bp)
                if (n, j) == (10, 1):
                    b_to_sbuf(bp)
                if 11 <= n < 15 and j < 3:
                    softplus_out(bp, n - 11, j)
                if 10 <= n < 14 and j == 3:
                    softplus_in(bp, n - 10)

            def item(b, n, j, last=False):
                scan(b, n, j)
                if j == 1 and not last:
                    if n < NS - 1:
                        input_terms(b, n + 1)
                    else:
                        input_terms(b + 1, 0)

            dve.wait_ge(a_ready, 1)
            dve.wait_ge(tg_ready, 1)
            for n in range(2, NS):
                for j in range(ND):
                    pieces(0, n, j)
            input_terms(0, 0)
            for n in range(2):
                for j in range(ND):
                    item(0, n, j)
            dve.wait_ge(x_in, 32)
            with dve.Fori(0, NB - 1) as b:
                for n in range(2, NS):
                    for j in range(ND):
                        item(b, n, j)
                        pieces(b + 1, n, j)
                for n in range(2):
                    for j in range(ND):
                        item(b + 1, n, j)
                        post(b, n, j)
                rest_of_post(b)
            for n in range(2, NS):
                for j in range(ND):
                    item(NB - 1, n, j, last=n == NS - 1)
            for j in range(ND):
                add_du(NB - 1, j)
                gate(NB - 1, j)
            for t in range(NL):
                residual(NB - 1, t)
                x1_stats(NB - 1, t)
            dve.wait_ge(ln2_dve, NT)
            dve.sem_inc(wait_carrier, 1)
            for t in range(NT):
                V.bn_aggr(mv2[:, t, :], st2[:, t, :]).then_inc(ln2_dve, 1)
            dve.wait_ge(ln2_dve, 2 * NT)
            V.tensor_scalar(rs2[:, 0, :], mv2[:, :, 1], EPS, None, ALU.add).then_inc(ln2_var, 1)
            dve.wait_ge(ln2_act, 2)
            ln_refine(rs2, NT, 2 * NT, ln2_dve)
            dve.sem_inc(p1_done, 1)

            def normalise(t, k):
                if not isinstance(t, int) or t >= 2:
                    dve.wait_ge(xT_done, t - 1)
                    dve.wait_ge(xn_stored[k], 16 * (t >> 1))
                    dve.sem_inc(wait_carrier, 1)
                V.tensor_scalar(xin[:, k, :], x_tok[:, bass.ds(t, 1), :].rearrange("p a c -> p (a c)"),
                                mv2[:, bass.ds(t, 1), 0], rs2[:, 3, bass.ds(t, 1)],
                                ALU.subtract, ALU.mult).then_inc(xn_made, 1)

            normalise(0, 0)
            normalise(1, 1)

            dve.sem_inc(xl_ready, 1)
            dve.sem_inc(h_ready, 2)
            dve.sem_inc(hl_ready, 2)
            dve.sem_inc(y_read, 2)
            dve.wait_ge(p2_consts, 8)
            dve.wait_ge(gw_hi, 1)
            V.tensor_tensor(gw_l[:], psHT[:, :, 0:NE], gw_h[:].bitcast(F32), ALU.subtract).then_inc(gw_ready, 1)

            def split_lo(ordinal, dst):
                for c in range(KH):
                    dve.wait_ge(w_hi, ordinal * 7 + c + 1)
                    V.tensor_tensor(dst(wgu_l)[:, c, :], raw_gu[:, c, :], dst(wgu_h)[:, c, :].bitcast(F32),
                                    ALU.subtract)
                for c in range(3):
                    rows = P if c < 2 else ILAST
                    dve.wait_ge(w_hi, ordinal * 7 + KH + c + 1)
                    ins = V.tensor_tensor(dst(wd_l)[0:rows, c, :], raw_d[0:rows, c, :],
                                          dst(wd_h)[0:rows, c, :].bitcast(F32), ALU.subtract)
                ins.then_inc(w_split, 1)

            def static(buf):
                return lambda w: w[:, buf]

            def h_lo(q, k):
                dve.wait_ge(hT_done, q + 1)
                dve.wait_ge(hh_ready, q + 1)
                V.tensor_tensor(hl[:, k, :, :], psHT[:, 0:3, :], hh[:, k, :, :].bitcast(F32),
                                ALU.subtract).then_inc(hl_ready, 1)

            def x_lo(q, k):
                dve.wait_ge(xT_done, q + 1)
                dve.wait_ge(xh_ready, q + 1)
                V.tensor_tensor(xl[:, k, :, :], psT[:], xh[:, k, :, :].bitcast(F32),
                                ALU.subtract).then_inc(xl_ready, 1)

            def token_tile(t):
                return x_tok[:, bass.ds(t, 1), :].rearrange("p a c -> p (a c)")

            def result_to(q, k, kind, t):
                dve.wait_ge(y_full, q + 1)
                if kind == "shared":
                    ins = V.scalar_tensor_tensor(token_tile(t), psY[k][:], tg[:, 1:2], token_tile(t),
                                                 ALU.mult, ALU.add)
                else:
                    if not isinstance(t, int) or t >= 2:
                        dve.wait_ge(y_stored[k], 16 * (t >> 1))
                    ins = V.tensor_copy(yout[:, k, :], psY[k][:])
                ins.then_inc(y_read, 1)

            def slot(q, k, kind, t, router=False, first=False, last_slot=False, make=False):
                if not first:
                    h_lo(q - 1, 1 - k)
                if not last_slot:
                    x_lo(q + 1, 1 - k)
                dve.wait_ge(sg_ready, q + 1)
                dve.wait_ge(gu_done, q + 1)
                V.tensor_tensor(hbuf[:, k, 0:INTER], sg[:, k, :], psU[k][:, 0:INTER], ALU.mult
                                ).then_inc(h_ready, 1)
                if router:
                    V.tensor_copy(lg[:, bass.ds(q, 1), :].rearrange("p a e -> p (a e)"),
                                  psG[k][:, INTER:INTER + NE]).then_inc(lg_ready, 1)
                if not first:
                    result_to(q - 1, 1 - k, kind, t)
                if make:
                    normalise(q + 2, k)

            steps = [0]

            def link(ins):
                steps[0] += 1
                ins.then_inc(rt, 1)
                dve.wait_ge(rt, steps[0])

            split_lo(0, static(1))
            x_lo(0, 0)
            slot(0, 0, "shared", 0, router=True, first=True, make=True)
            slot(1, 1, "shared", 0, router=True, make=True)
            split_lo(1, static(2))
            with dve.Fori(1, NT // 2 - 1) as m:
                for k in range(2):
                    slot(m * 2 + k, k, "shared", m * 2 + k - 1, router=True, make=True)
            for k in range(2):
                slot(NT - 2 + k, k, "shared", NT - 3 + k, router=True)
            slot(NT, 0, "shared", NT - 1)

            dve.wait_ge(lg_ready, NT)
            for t in range(NT):
                V.max(top8[:, t, :], lg[:, t, :]).then_inc(rt_top, 1)
            for t in range(NT):
                dve.wait_ge(rt_top, t + 1)
                V.max_index(idx8[:, t, :], top8[:, t, :], lg[:, t, :]).then_inc(rt_top, 1)
            dve.wait_ge(rt_top, 2 * NT)
            link(V.tensor_copy(e12[:], idx8[:, :, 0:2].rearrange("p t c -> p c t")))
            iota_b = iota_e[:].unsqueeze(1).broadcast_to([P, NT, NE])
            for c in range(2):
                ins = V.tensor_tensor(oh[:, c], iota_b, e12[:, c].unsqueeze(2).broadcast_to([P, NT, NE]),
                                      ALU.is_equal)
                link(ins)
            V.tensor_tensor(msum[:], oh[:, 0], oh[:, 1], ALU.add).then_inc(rt_mask, 1)
            V.tensor_tensor(ex[:], lg[:], top8[:, :, 0:1].broadcast_to([P, NT, NE]),
                            ALU.subtract).then_inc(rt_shift, 1)
            slot(NT + 1, 1, "shared", 0)
            dve.wait_ge(rt_count, 1)
            counts = psHT[:].rearrange("p c n -> p (c n)")
            link(V.tensor_copy(zpos[:].rearrange("p t e -> p (t e)"), counts[:, 0:NT * NE]))
            V.tensor_copy(cnt[:], counts[:, NT * NE:].rearrange("p (t e) -> p e t", t=NT)).then_inc(cnt_read, 1)
            dve.wait_ge(cnt_read, 1)
            flat = lambda a: a[:].rearrange("p e t -> p (e t)")
            link(V.tensor_tensor_scan(flat(cinc), onesf[:], flat(cnt), 0.0, ALU.mult, ALU.add))
            link(V.tensor_tensor(cexc[:], cinc[:], cnt[:], ALU.subtract))
            CE, TL, TE, ADJ, TMP = range(5)
            link(V.tensor_tensor(ce[:, CE], cinc[:, :, NT - 1], cexc[:, :, 0], ALU.subtract))
            link(V.tensor_scalar(cei[:, 0], ce[:, CE], float(P - 1), None, ALU.add))
            link(V.tensor_scalar(cei[:, 1], cei[:, 0], 7, None, ALU.logical_shift_right))
            link(V.tensor_copy(ce[:, TL], cei[:, 1]))
            link(V.tensor_tensor_scan(ce[:, TE], onesf[:, 0:NE], ce[:, TL], 0.0, ALU.mult, ALU.add))
            link(V.tensor_tensor(ce[:, TMP], ce[:, TE], ce[:, TL], ALU.subtract))
            link(V.scalar_tensor_tensor(ce[:, ADJ], ce[:, TMP], float(P), cexc[:, :, 0], ALU.mult,
                                        ALU.subtract))
            link(V.tensor_tensor(zpos[:], zpos[:], cexc[:].rearrange("p e t -> p t e"), ALU.add))
            link(V.tensor_tensor(zpos[:], zpos[:], ce[:, ADJ].unsqueeze(1).broadcast_to([P, NT, NE]), ALU.add))
            for c in range(2):
                link(V.tensor_tensor(ztmp[:], zpos[:], oh[:, c], ALU.mult))
                link(V.tensor_reduce(posf[:, c], ztmp[:], AX.X, ALU.add))
            V.tensor_copy(posi[:], posf[:]).then_inc(pos_ready, 1)
            link(V.memset(se[:, 0:1], -1.0))
            link(V.tensor_tensor(scmp, iota_s[:].unsqueeze(2).broadcast_to([1, SLOTS, NE]),
                                 ce[0:1, TE].unsqueeze(1).broadcast_to([1, SLOTS, NE]), ALU.is_ge))
            link(V.tensor_reduce(se[:, 1:], scmp, AX.X, ALU.add))
            link(V.tensor_scalar(se[:, 1:], se[:, 1:], float(NE - 1), None, ALU.min))
            link(V.tensor_tensor(schg[:], se[:, 1:], se[:, 0:SLOTS], ALU.not_equal))
            link(V.tensor_tensor_scan(srank[:], onesf[0:1, 0:SLOTS], schg[:], -1.0, ALU.mult, ALU.add))
            V.tensor_copy(chg_i[:], schg[:]).then_inc(table_ready, 1)
            V.tensor_copy(rank_i[:], srank[:]).then_inc(table_ready, 1)
            link(V.tensor_tensor(se[:, 1:], se[:, 1:], schg[:], ALU.mult))
            link(V.tensor_tensor(skcmp, iota_k[:].unsqueeze(2).broadcast_to([1, NDK, SLOTS]),
                                 srank[:].unsqueeze(1).broadcast_to([1, NDK, SLOTS]), ALU.is_equal))
            link(V.tensor_tensor(skcmp, skcmp, se[:, 1:].unsqueeze(1).broadcast_to([1, NDK, SLOTS]),
                                 ALU.mult))
            link(V.tensor_reduce(dk[:], skcmp, AX.X, ALU.add))
            V.tensor_copy(dk_i[:], dk[:]).then_inc(table_ready, 1)
            dve.wait_ge(rt_act, 1)
            link(V.tensor_reduce(esum[:], ex[:], AX.X, ALU.add))
            link(V.reciprocal(esum[:], esum[:]))
            link(V.tensor_scalar(esum[:], esum[:], tg[:, 1:2], None, ALU.mult))
            for c in range(2):
                link(V.tensor_tensor(ztmp[:], ex[:], oh[:, c], ALU.mult))
                link(V.tensor_reduce(wts[:, c], ztmp[:], AX.X, ALU.add))
                link(V.tensor_tensor(wts[:, c], wts[:, c], esum[:], ALU.mult))

            with dve.Fori(1, NB1 // 2) as m:
                for k in range(2):
                    slot(m * 2 + k + NT, k, "shared", m * 2 + k - 1)
            split_lo(2, static(0))
            Q0 = NT + NB1

            def routed_slot(r, k, kind="routed"):
                slot(r + Q0, k, kind, r - 1 if kind == "routed" else NB1 - 1)
                chg = dve.value_load(chg_i[0:1, bass.ds(r, 1)], min_val=0, max_val=1)
                rank = dve.value_load(rank_i[0:1, bass.ds(r, 1)], min_val=0, max_val=NE)
                buf = (rank + 1) % 2
                with dve.If(chg):
                    split_lo(rank + 3, lambda w: w[:, bass.ds(buf, 1)].rearrange("p a k c -> p (a k) c"))

            routed_slot(0, 0, "shared")
            routed_slot(1, 1)
            with dve.Fori(1, SLOTS // 2) as m:
                for k in range(2):
                    routed_slot(m * 2 + k, k)
            Q1 = Q0 + SLOTS

            def finish(i, t):
                k = i % 2 if isinstance(i, int) else i[1]
                i = i if isinstance(i, int) else i[0]
                dve.wait_ge(gathered[k], 32 * ((i >> 1) + 1))
                for c in range(2):
                    ins = V.scalar_tensor_tensor(token_tile(t), gbuf[:, 2 * k + c, :],
                                                 wts[:, c, bass.ds(t, 1)], token_tile(t), ALU.mult, ALU.add)
                    if c == 0:
                        ins.then_inc(f_first, 1)
                        dve.wait_ge(f_first, i + 1)
                ins.then_inc(f_done, 1)

            slot(Q1, 0, "routed", SLOTS - 1)
            slot(Q1 + 1, 1, "shared", NB1)
            with dve.Fori(1, (NT - NB1) // 2 - 1) as m:
                for k in range(2):
                    slot(m * 2 + k + Q1, k, "shared", m * 2 + k + NB1 - 1)
                    finish((m * 4 + 2 * k - 4, 0), m * 2 + k - 2)
                    finish((m * 4 + 2 * k - 3, 1), m * 2 + k - 2 + NB1)
            QE = Q1 + NT - NB1
            for k in range(2):
                slot(QE - 2 + k, k, "shared", NT - 3 + k, last_slot=k == 1)
                i = 2 * (NB1 - 4 + k)
                finish(i, NB1 - 4 + k)
                finish(i + 1, 2 * NB1 - 4 + k)
            h_lo(QE - 1, 1)
            result_to(QE - 1, 1, "shared", NT - 1)
            for i in range(2 * NB1 - 4, 2 * NB1):
                finish(i, (i % 2) * NB1 + i // 2)


_INS = ['x', 'ctx_1024', 'g_xattn', 'g_ffn', 'L0_xattn_in_proj_w', 'L0_xattn_conv_w', 'L0_xattn_conv_b',
        'L0_xattn_x_proj_w', 'L0_xattn_dt_proj_w', 'L0_xattn_dt_proj_b', 'L0_xattn_A_log', 'L0_xattn_D',
        'L0_ffn_gate_w', 'L0_ffn_w_gate_up', 'L0_ffn_w_down', 'L0_ffn_shared_gate_up', 'L0_ffn_shared_down']
_OUTS = [((4, 512, 512), 'float32')]


def kernel(**inputs):
    import numpy as _np
    import concourse.bacc as _bacc
    from concourse import mybir as _mybir
    from concourse.bass_utils import run_bass_kernel_spmd as _run

    nc = _bacc.Bacc("TRN2", target_bir_lowering=False, num_devices=1)
    arrays, args = {}, []
    for name in _INS:
        a = _np.ascontiguousarray(inputs[name])
        arrays[f"in_{name}_dram"] = a
        args.append(nc.dram_tensor(f"in_{name}_dram", a.shape, _mybir.dt.from_np(a.dtype), kind="ExternalInput").ap())
    for i, (shape, dtype) in enumerate(_OUTS):
        dt = _mybir.dt.from_np(_np.dtype(dtype))
        args.append(nc.dram_tensor(f"out_{i}_dram", shape, dt, kind="ExternalOutput").ap())
    flamingo_block(nc, *args)
    r = _run(nc, [arrays], core_ids=[0])
    return r.results[0]["out_0_dram"]
```

```python
from contextlib import ExitStack

import concourse.bass as bass
from concourse import mybir

F32 = mybir.dt.float32
F32R = mybir.dt.float32r
BF16 = mybir.dt.bfloat16
I32 = mybir.dt.int32
U32 = mybir.dt.uint32
ALU = mybir.AluOpType
ACT = mybir.ActivationFunctionType
AX = mybir.AxisListType

P = 128
EPS = 1e-5


def flamingo_block(nc, x, ctx_in, g_xattn, g_ffn, in_proj_w, conv_w, conv_b, x_proj_w, dt_proj_w,
                   dt_proj_b, A_log, D_in, gate_w, w_gate_up, w_down, shared_gate_up, shared_down, out):
    NB, L, D = x.shape
    DM = ctx_in.shape[2]
    NS = A_log.shape[1]
    RK = dt_proj_w.shape[1]
    XR = RK + 2 * NS
    TAPS = conv_w.shape[2]
    ND, NL, NK = D // P, L // P, DM // P
    H = D
    NE = gate_w.shape[0]
    INTER = w_down.shape[1]
    assert L == D and ND == NL == 4 and NK == 2 and NS == 16 and RK == 16 and TAPS == 4
    assert shared_down.shape[0] == 2 * INTER
    T = NB * L
    NT = T // P
    KH = H // P
    IPAD = 3 * P
    ILAST = INTER - 2 * P
    SLOTS = 2 * T // P + NE
    NDK = NE + 3
    ITEMS = NS * ND
    RING = 2 * ND
    ZROWS = SLOTS * P // (NB - 1)
    NB1 = NT // 2

    xn_rows = nc.dram_tensor("xn_rows", [T, H], F32).ap()
    slot_in = nc.dram_tensor("slot_in", [SLOTS * P, H], F32).ap()
    slot_out = nc.dram_tensor("slot_out", [SLOTS * P, H], F32).ap()
    c_rows = nc.dram_tensor("c_rows", [NB, NS, L], F32).ap()

    with ExitStack() as top:
        def sem(name):
            return top.enter_context(nc.semaphore(name))

        def sb_in(stack, name, shape, dt=F32):
            return stack.enter_context(nc.sbuf_tensor(name, shape, dt))

        def ps_in(stack, name, shape, dt=F32):
            return stack.enter_context(nc.psum_tensor(name, shape, dt))

        x_tok = sb_in(top, "x_tok", [P, NT, H])
        ident = sb_in(top, "ident", [P, P])
        tg = sb_in(top, "tg", [P, 2])
        gate_raw = sb_in(top, "gate_raw", [NE, H])
        st2 = sb_in(top, "st2", [P, NT, 6])
        mv2 = sb_in(top, "mv2", [P, NT, 2])
        rs2 = sb_in(top, "rs2", [P, 4, NT])

        p1 = ExitStack()
        s1 = lambda name, shape, dt=F32: sb_in(p1, name, shape, dt)
        ctx_cur = s1("ctx_cur", [P, NL, DM])
        ctxT = s1("ctxT", [P, NK, L])
        winT = s1("winT", [P, NK, D])
        xpT = s1("xpT", [P, ND, XR])
        dp_raw = s1("dp_raw", [P, ND, RK])
        dpT = s1("dpT", [RK, D])
        xdbl = s1("xdbl", [XR, L])
        sp_t = s1("sp_t", [P, L])
        du = s1("du", [P, 2, L])
        by_parity = s1("by_parity", [P, 2, 4, ND, L])
        xs, dts, duT, zs = (by_parity[:, :, k] for k in range(4))
        cw = s1("cw", [P, ND, TAPS])
        cb = s1("cb", [P, ND])
        db = s1("db", [P, ND])
        Dv = s1("Dv", [P, ND])
        Aneg = s1("Aneg", [P, ND, NS])
        BT = s1("BT", [P, 2, NL, XR])
        y3 = s1("y3", [P, ND, L])
        sp_a, sp_r, sp_u, sp_l = (y3[:, j, :] for j in range(ND))
        dbuT = s1("dbuT", [P, 2, NL, D])
        dA = s1("dA", [P, RING, L])
        win_raw = dA[:, 0:2, :].rearrange("p a (k c) -> p (a k) c", c=DM)
        xp_raw = dA[0:XR, 2, :]
        hst = s1("hst", [P, RING, L])
        prod = s1("prod", [P, RING, L])
        cbc = s1("cbc", [P, 2, L])
        zb16 = s1("zb16", [P, P], BF16)
        zmov = s1("zmov", [P, L], BF16)
        ztile = s1("ztile", [P, H])
        st1 = s1("st1", [P, ND, 6])
        mv1 = s1("mv1", [P, ND, 2])
        rs1 = s1("rs1", [P, 5, ND])
        q1 = ExitStack()
        y_ps = [ps_in(q1, f"y_ps{j}", [P, L]) for j in range(ND)]
        dbu_ps = [ps_in(q1, f"dbu_ps{k}", [P, L]) for k in range(2)]
        mp = [ps_in(q1, f"mp{k}", [P, L]) for k in range(2)]
        q1.close()
        p1.close()

        p2 = ExitStack()
        s2 = lambda name, shape, dt=F32: sb_in(p2, name, shape, dt)
        raw_gu = s2("raw_gu", [P, KH, 2 * INTER])
        raw_d = s2("raw_d", [P, 3, H])
        GU_W = 2 * INTER + NE
        GU_N, D_N = KH * GU_W, 3 * H
        weights = s2("weights", [P, 3, 2 * (GU_N + D_N)], F32R)
        wgu_h, wgu_l = (weights[:, :, k * GU_N:(k + 1) * GU_N].rearrange("p b (k c) -> p b k c", k=KH)
                        for k in range(2))
        wd_h, wd_l = (weights[:, :, 2 * GU_N + k * D_N:2 * GU_N + (k + 1) * D_N]
                      .rearrange("p b (k c) -> p b k c", k=3) for k in range(2))
        xin = s2("xin", [P, 2, H])
        xh = s2("xh", [P, 2, KH, P], F32R)
        xl = s2("xl", [P, 2, KH, P], F32R)
        sg = s2("sg", [P, 2, INTER])
        hbuf = s2("hbuf", [P, 2, IPAD])
        hh = s2("hh", [P, 2, 3, P], F32R)
        hl = s2("hl", [P, 2, 3, P], F32R)
        yout = s2("yout", [P, 2, H])
        gbuf = s2("gbuf", [P, 4, H])
        gw_h, gw_l = (w[:, 0, :, 2 * INTER:] for w in (wgu_h, wgu_l))
        lg = s2("lg", [P, NT, NE])
        top8 = s2("top8", [P, NT, 8])
        idx8 = s2("idx8", [P, NT, 8], U32)
        e12 = s2("e12", [P, 2, NT])
        iota_e = s2("iota_e", [P, NE])
        oh = s2("oh", [P, 2, NT, NE])
        msum = s2("msum", [P, NT, NE], BF16)
        upper = s2("upper", [P, P], BF16)
        ones = s2("ones", [P, P], BF16)
        onesf = s2("onesf", [P, NT * NE])
        cnt = s2("cnt", [P, NE, NT])
        cinc = s2("cinc", [P, NE, NT])
        cexc = s2("cexc", [P, NE, NT])
        ce = s2("ce", [P, 6, NE])
        cei = s2("cei", [P, 2, NE], I32)
        zpos = s2("zpos", [P, NT, NE])
        ztmp = s2("ztmp", [P, NT, NE])
        posf = s2("posf", [P, 2, NT])
        posi = s2("posi", [P, 2, NT], I32)
        ex = s2("ex", [P, NT, NE])
        esum = s2("esum", [P, NT])
        wts = s2("wts", [P, 2, NT])
        iota_s = s2("iota_s", [1, SLOTS])
        iota_k = s2("iota_k", [1, NDK])
        yflat = yout[0:1].rearrange("p k c -> p (k c)")
        scmp = yflat[:, 0:SLOTS * NE].rearrange("p (s e) -> p s e", s=SLOTS)
        skcmp = yflat[:, 0:NDK * SLOTS].rearrange("p (k s) -> p k s", k=NDK)
        se = s2("se", [1, SLOTS + 1])
        schg = s2("schg", [1, SLOTS])
        srank = s2("srank", [1, SLOTS])
        dk = s2("dk", [1, NDK])
        chg_i = s2("chg_i", [1, SLOTS], I32)
        rank_i = s2("rank_i", [1, SLOTS], I32)
        used_i = s2("used_i", [1, SLOTS], I32)
        dk_i = s2("dk_i", [1, NDK], I32)
        q2 = ExitStack()
        psT = ps_in(q2, "psT", [P, KH, P])
        psG = [ps_in(q2, f"psG{k}", [P, 512]) for k in range(2)]
        psU = [ps_in(q2, f"psU{k}", [P, 512]) for k in range(2)]
        psHT = ps_in(q2, "psHT", [P, 4, P])
        psY = [ps_in(q2, f"psY{k}", [P, H]) for k in range(2)]
        q2.close()
        p2.close()

        wait_carrier = sem("wait_carrier")
        consts_in = sem("consts_in")
        x_in = sem("x_in")
        ctx_loaded = sem("ctx_loaded")
        ident_made = sem("ident_made")
        consts_made = sem("consts_made")
        wt_full = sem("wt_full")
        wt_read = sem("wt_read")
        a_exp = sem("a_exp")
        a_ready = sem("a_ready")
        tg_ready = sem("tg_ready")
        zeroed = sem("zeroed")
        misc_full = [sem("misc_full0"), sem("misc_full1")]
        misc_read = [sem("misc_read0"), sem("misc_read1")]
        post_full = [sem("post_full0"), sem("post_full1")]
        post_read = [sem("post_read0"), sem("post_read1")]
        conv_tap = sem("conv_tap")
        ln1_var = sem("ln1_var")
        ln1_act = sem("ln1_act")
        ln1_dve = sem("ln1_dve")
        silu_done = sem("silu_done")
        c_stored = sem("c_stored")
        c_loaded = [sem("c_loaded0"), sem("c_loaded1")]
        sp_abs = sem("sp_abs")
        sp_exp = sem("sp_exp")
        sp_ln = sem("sp_ln")
        sp_dve = sem("sp_dve")
        du_ready = sem("du_ready")
        dbut_ready = sem("dbut_ready")
        dbut_last = sem("dbut_last")
        dut_ready = sem("dut_ready")
        da_ready = sem("da_ready")
        dbu_ready = sem("dbu_ready")
        scanned = sem("scanned")
        prod_ready = sem("prod_ready")
        prod_used = sem("prod_used")
        y_done = sem("y_done")
        y_taken = sem("y_taken")
        y3_ready = sem("y3_ready")
        x1_ready = sem("x1_ready")
        ln2_var = sem("ln2_var")
        ln2_act = sem("ln2_act")
        ln2_dve = sem("ln2_dve")
        p1_done = sem("p1_done")
        xn_made = sem("xn_made")
        xn_stored = [sem("xn_stored0"), sem("xn_stored1")]
        raw_gu_loaded = sem("raw_gu_loaded")
        raw_d_loaded = sem("raw_d_loaded")
        gu_hi = sem("gu_hi")
        d_hi = sem("d_hi")
        gu_split = sem("gu_split")
        gu_split_last = sem("gu_split_last")
        d_split = sem("d_split")
        slot_x_ready = [sem(f"slot_x_ready{k}") for k in range(4)]
        xin_ready = [sem("xin_ready0"), sem("xin_ready1")]
        xT_done = sem("xT_done")
        xh_ready = sem("xh_ready")
        xl_ready = sem("xl_ready")
        g_done = sem("g_done")
        gu_done = sem("gu_done")
        sg_ready = sem("sg_ready")
        h_ready = sem("h_ready")
        hT_done = sem("hT_done")
        hh_ready = sem("hh_ready")
        hl_ready = sem("hl_ready")
        y_full = sem("y_full")
        y_read = sem("y_read")
        y_stored = [sem("y_stored0"), sem("y_stored1")]
        lg_ready = sem("lg_ready")
        gw_full = sem("gw_full")
        gw_hi = sem("gw_hi")
        gw_ready = sem("gw_ready")
        rt_top = sem("rt_top")
        rt_shift = sem("rt_shift")
        cnt_read = sem("cnt_read")
        p2_consts = sem("p2_consts")
        rt = sem("rt")
        rt_mask = sem("rt_mask")
        rt_count = sem("rt_count")
        rt_act = sem("rt_act")
        pos_ready = sem("pos_ready")
        table_ready = sem("table_ready")
        g_loaded = [sem(f"g_loaded{k}") for k in range(4)]
        scat = [sem(f"scat{k}") for k in range(4)]
        gathered = [sem("gathered0"), sem("gathered1")]
        f_first = sem("f_first")
        f_done = sem("f_done")
        out_stored = sem("out_stored")

        block = top.enter_context(nc.Block())

        def slot_of(n, j):
            return n % 2 * ND + j

        def mbase(bp):
            return bp * 8

        NCONST = 11

        @block.sync
        def _(sp):
            def load_ctx(bp):
                sp.dma_start(ctx_cur[:], ctx_in[bass.ds(bp, 1)].rearrange("a (t p) c -> p (a t) c", p=P)
                             ).then_inc(ctx_loaded, 16)

            load_ctx(0)
            for dst, src in (
                (win_raw, in_proj_w.rearrange("(j p) c -> p j c", p=P)),
                (xp_raw, x_proj_w),
                (dp_raw[:], dt_proj_w.rearrange("(j p) r -> p j r", p=P)),
                (cw[:], conv_w.rearrange("(j p) a k -> p j (a k)", p=P)),
                (Aneg[:], A_log.rearrange("(j p) n -> p j n", p=P)),
                (gate_raw[:], gate_w),
            ):
                sp.dma_start(dst, src).then_inc(consts_in, 16)
            with nc.allow_non_contiguous_dma(reason="four short columns"):
                for dst, src in ((cb, conv_b), (db, dt_proj_b), (Dv, D_in)):
                    sp.dma_start(dst[:], src.rearrange("(j p) -> p j", p=P)).then_inc(consts_in, 16)
            sp.dma_start(tg[:, 0:1], g_xattn.partition_broadcast(P)).then_inc(consts_in, 16)
            sp.dma_start(tg[:, 1:2], g_ffn.partition_broadcast(P)).then_inc(consts_in, 16)
            sp.dma_start(x_tok[:, 0:NL, :], x[0].rearrange("(t p) c -> p t c", p=P)).then_inc(x_in, 16)

            def store_c(bp):
                sp.wait_ge(misc_read[0], mbase(bp) + 5)
                sp.dma_start(c_rows[bass.ds(bp, 1)].rearrange("a n l -> n (a l)"),
                             xdbl[RK + NS:XR, :]).then_inc(c_stored, 16)

            def load_c(b, n):
                if n == 0:
                    sp.wait_ge(c_stored, 16 * (b + 1))
                sp.wait_ge(prod_ready, (b * NS + n + 1) * ND)
                src = c_rows[bass.ds(b, 1), n, :].rearrange("a l -> (a l)").partition_broadcast(P)
                sp.dma_start(cbc[:, n % 2, :], src).then_inc(c_loaded[n % 2], 16)

            store_c(0)
            load_c(0, 0)
            load_c(0, 1)
            sp.dma_start(x_tok[:, NL:, :], x[1:].rearrange("b (t p) c -> p (b t) c", p=P)).then_inc(x_in, 16)
            sp.wait_ge(consts_made, 3)
            with sp.Fori(0, NB - 1) as b:
                sp.wait_ge(misc_full[1], mbase(b) + 1)
                load_ctx(b + 1)
                for n in range(2, NS):
                    load_c(b, n)
                    if n == 11:
                        store_c(b + 1)
                    if n == 5:
                        sp.dma_start(slot_in[bass.ds(b * ZROWS, ZROWS), :].rearrange("(s p) c -> p s c", p=P),
                                     ztile[:].unsqueeze(1).broadcast_to([P, ZROWS // P, H])).then_inc(zeroed, 16)
                load_c(b + 1, 0)
                load_c(b + 1, 1)
            def load_shared(half):
                g0 = half * INTER
                gu = shared_gate_up.rearrange("(k p) c -> p k c", p=P)
                sp.dma_start(raw_gu[:, :, 0:INTER], gu[:, :, g0:g0 + INTER]).then_inc(raw_gu_loaded, 16)
                sp.dma_start(raw_gu[:, :, INTER:], gu[:, :, g0 + 2 * INTER:g0 + 3 * INTER]
                             ).then_inc(raw_gu_loaded, 16)
                sp.dma_start(raw_d[:, 0:2, :], shared_down[g0:g0 + 2 * P, :].rearrange("(k p) c -> p k c", p=P)
                             ).then_inc(raw_d_loaded, 16)
                sp.dma_start(raw_d[0:ILAST, 2, :], shared_down[g0 + 2 * P:g0 + INTER, :]
                             ).then_inc(raw_d_loaded, 16)

            sp.wait_ge(dut_ready, NB * ND)
            sp.wait_ge(c_stored, 16 * NB)
            load_shared(0)
            for n in range(2, NS):
                load_c(NB - 1, n)

            def load_expert_gu(e, cond=None):
                gu = w_gate_up[bass.ds(e, 1)].rearrange("a (k p) c -> p (a k) c", p=P)
                for dst, src in ((raw_gu[:, 0:2, :], gu[:, 0:2, :]), (raw_gu[:, 2:4, :], gu[:, 2:4, :])):
                    sp.dma_start(dst, src, cond=cond).then_inc(raw_gu_loaded, 16)

            def load_expert_d(e, cond=None):
                dn = w_down[bass.ds(e, 1)].rearrange("a i c -> (a i) c")
                for dst, src in ((raw_d[:, 0:2, :], dn[0:2 * P, :].rearrange("(k p) c -> p k c", p=P)),
                                 (raw_d[0:ILAST, 2, :], dn[2 * P:INTER, :])):
                    sp.dma_start(dst, src, cond=cond).then_inc(raw_d_loaded, 16)

            def load_tile(src, q, qq, wait=True):
                if wait:
                    sp.wait_ge(xT_done, q - 1)
                sp.dma_start(xin[:, qq % 2, :], src).then_inc(xin_ready[qq % 2], 16)

            def tile_rows(rows, t):
                return rows[bass.ds(t * P, P), :]

            def store_xn(t, k):
                sp.wait_ge(xn_made, t + 1)
                sp.dma_start(tile_rows(xn_rows, t), xin[:, k, :]).then_inc(xn_stored[k], 16)

            store_xn(0, 0)
            store_xn(1, 1)
            sp.wait_ge(gu_split, 1)
            sp.wait_ge(d_split, 1)
            load_shared(1)
            with sp.Fori(1, NT // 2) as m:
                for k in range(2):
                    store_xn(m * 2 + k, k)
            for k in range(2):
                sp.wait_ge(xn_stored[k], 16 * (NT // 2))
            for n in range(3):
                load_tile(tile_rows(xn_rows, n), n + NT, n % 2)

            def load_g(t):
                k = t % 4
                if t >= 4:
                    sp.wait_ge(scat[k], 32 * (t // 4))
                sp.dma_start(gbuf[:, k, :], tile_rows(xn_rows, t)).then_inc(g_loaded[k], 16)

            for t in range(NT // 2):
                load_g(t)
            Q0 = NT + NB1
            sp.wait_ge(table_ready, 4)
            sp.wait_ge(gu_split, 2)
            sp.wait_ge(d_split, 2)
            e0 = sp.value_load(dk_i[0:1, 0:1], min_val=0, max_val=NE - 1)
            load_expert_gu(e0)
            load_expert_d(e0)
            for t in range(NT // 2, NT):
                load_g(t)

            def load_slot(r, k4):
                sp.dma_start(gbuf[:, k4, :], tile_rows(slot_in, r)).then_inc(slot_x_ready[k4], 16)

            for k in range(4):
                sp.wait_ge(scat[k], 32 * (NT // 4))
            for r in range(4):
                load_slot(r, r)
            e1 = sp.value_load(dk_i[0:1, 1:2], min_val=0, max_val=NE - 1)
            sp.wait_ge(gu_split, 3)
            load_expert_gu(e1)
            sp.wait_ge(d_split, 3)
            load_expert_d(e1)

            def prefetch_expert(r):
                rank = sp.value_load(rank_i[0:1, bass.ds(r, 1)], min_val=0, max_val=NE)
                chg = sp.value_load(chg_i[0:1, bass.ds(r, 1)], min_val=0, max_val=1)
                e = sp.value_load(dk_i[0:1, bass.ds(rank + 2, 1)], min_val=0, max_val=NE - 1)
                sp.wait_ge(gu_split, rank + 4)
                sp.wait_ge(gu_split_last, rank + 2)
                load_expert_gu(e, cond=chg)
                sp.wait_ge(d_split, rank + 4)
                load_expert_d(e, cond=chg)

            with sp.Fori(0, SLOTS // 4 - 1) as m:
                for k in range(4):
                    r = m * 4 + k
                    sp.wait_ge(xT_done, Q0 + r + 1)
                    load_slot(r + 4, k)
                    prefetch_expert(r)
            for r in range(SLOTS - 4, SLOTS):
                if r < SLOTS - 2:
                    t = r - (SLOTS - 4)
                    load_tile(tile_rows(xn_rows, t + NB1), Q0 + 2, t)
                prefetch_expert(r)
            Q1 = Q0 + SLOTS
            with sp.Fori(1, (NT - NB1) // 2) as m:
                for k in range(2):
                    load_tile(tile_rows(xn_rows, m * 2 + k + NB1), m * 2 + k + Q1, k)
            out_t = out.rearrange("b (t p) c -> p (b t) c", p=P)
            with sp.Fori(0, NB1) as m:
                for k in range(2):
                    t = m + k * NB1
                    sp.wait_ge(f_done, m * 2 + k + 1)
                    sp.dma_start(out_t[:, bass.ds(t, 1), :], x_tok[:, bass.ds(t, 1), :]).then_inc(out_stored, 16)
            sp.wait_ge(out_stored, 16 * NT)
            sp.wait_ge(raw_gu_loaded, 32 * (4 + SLOTS))
            sp.wait_ge(raw_d_loaded, 32 * (4 + SLOTS))

        @block.gpsimd
        def _(pool):
            pool.memset(ident[:], 0.0).then_inc(ident_made, 1)
            pool.wait_ge(ident_made, 1)
            pool.affine_select(out=ident[:], in_=ident[:], compare_op=ALU.not_equal, fill=1.0, base=0,
                               pattern=[[-1, P]], channel_multiplier=1).then_inc(ident_made, 1)
            pool.memset(zb16[:], 0.0).then_inc(consts_made, 1)
            pool.memset(zmov[:], 0.0).then_inc(consts_made, 1)
            pool.memset(ztile[:], 0.0).then_inc(consts_made, 1)
            pool.sem_inc(prod_ready, RING)

            def products(b, n):
                pool.wait_ge(c_loaded[n % 2], 16 * (b * (NS // 2) + n // 2 + 1))
                for j in range(ND):
                    i = b * ITEMS + n * ND + j
                    pool.wait_ge(scanned, i + 1 + RING)
                    pool.wait_ge(prod_used, i + 1)
                    pool.tensor_tensor(prod[:, slot_of(n, j), :], hst[:, slot_of(n, j), :], cbc[:, n % 2, :],
                                       ALU.mult).then_inc(prod_ready, 1)

            with pool.Fori(0, NB) as b:
                for n in range(NS):
                    products(b, n)

            pool.wait_ge(p1_done, 1)
            pool.iota(iota_e[:], pattern=[[1, NE]], base=0, channel_multiplier=0,
                      allow_small_or_imprecise_dtypes=True).then_inc(p2_consts, 1)
            pool.iota(iota_s[:], pattern=[[1, SLOTS]], base=0, channel_multiplier=0,
                      allow_small_or_imprecise_dtypes=True).then_inc(p2_consts, 1)
            pool.iota(iota_k[:], pattern=[[1, NDK]], base=0, channel_multiplier=0,
                      allow_small_or_imprecise_dtypes=True).then_inc(p2_consts, 1)
            pool.memset(ones[:], 1.0).then_inc(p2_consts, 1)
            pool.memset(onesf[:], 1.0).then_inc(p2_consts, 1)
            pool.memset(upper[:], 1.0).then_inc(p2_consts, 1)
            pool.memset(hbuf[:], 0.0).then_inc(p2_consts, 1)
            pool.wait_ge(p2_consts, 7)
            pool.affine_select(out=upper[:], in_=upper[:], compare_op=ALU.is_gt, fill=0.0, base=0,
                               pattern=[[1, P]], channel_multiplier=-1).then_inc(p2_consts, 1)

            pool.wait_ge(pos_ready, 1)
            pool.wait_ge(zeroed, 16 * (NB - 1))
            for t in range(NT):
                k = t % 4
                pool.wait_ge(g_loaded[k], 16 * (t // 4 + 1))
                for c in range(2):
                    pool.indirect_dma_start(
                        slot_in, bass.IndirectOffsetOnAxis(ap=posi[:, c, t:t + 1].bitcast(U32), axis=0),
                        gbuf[:, k, :], None).then_inc(scat[k], 16)

            Q0 = NT + NB1
            pool.wait_ge(table_ready, 4)
            pool.sem_inc(gu_split_last, 1)

            def rest_lo(r):
                chg = pool.value_load(chg_i[0:1, bass.ds(r, 1)], min_val=0, max_val=1)
                rank = pool.value_load(rank_i[0:1, bass.ds(r, 1)], min_val=0, max_val=NE)
                buf = (rank + 1) % 2
                with pool.If(chg):
                    c = KH - 1
                    pool.wait_ge(gu_hi, (rank + 3) * KH + c + 1)
                    pool.tensor_tensor(
                        wgu_l[:, bass.ds(buf, 1), c, 0:2 * INTER].rearrange("p a c -> p (a c)"), raw_gu[:, c, :],
                        wgu_h[:, bass.ds(buf, 1), c, 0:2 * INTER].rearrange("p a c -> p (a c)").bitcast(F32),
                        ALU.subtract).then_inc(gu_split_last, 1)
                    for c in range(3):
                        rows = P if c < 2 else ILAST
                        pool.wait_ge(d_hi, (rank + 3) * 3 + c + 1)
                        ins = pool.tensor_tensor(
                            wd_l[0:rows, bass.ds(buf, 1), c, :].rearrange("p a c -> p (a c)"), raw_d[0:rows, c, :],
                            wd_h[0:rows, bass.ds(buf, 1), c, :].rearrange("p a c -> p (a c)").bitcast(F32),
                            ALU.subtract)
                    ins.then_inc(d_split, 1)

            with pool.Fori(0, SLOTS // 2) as m:
                for k in range(2):
                    rest_lo(m * 2 + k)
                    pool.wait_ge(y_read, Q0 + m * 2 + k + 1 + 2)
                    pool.dma_start(slot_out[bass.ds((m * 2 + k) * P, P), :],
                                   yout[:, k, :]).then_inc(y_stored[k], 16)
            pool.wait_ge(y_stored[0], 16 * (SLOTS // 2))
            pool.wait_ge(y_stored[1], 16 * (SLOTS // 2))
            for i in range(NT):
                t = (i % 2) * NB1 + i // 2
                if i >= 2:
                    pool.wait_ge(f_done, i - 1)
                for c in range(2):
                    pool.indirect_dma_start(
                        gbuf[:, 2 * (i % 2) + c, :], None, slot_out,
                        bass.IndirectOffsetOnAxis(ap=posi[:, c, t:t + 1].bitcast(U32), axis=0),
                    ).then_inc(gathered[i % 2], 16)

        @block.tensor
        def _(pe):
            mm, tr = nc.tensor.matmul, nc.tensor.transpose
            pe.wait_ge(ident_made, 2)
            pe.wait_ge(consts_made, 3)
            pe.wait_ge(consts_in, 16 * NCONST)
            for k in range(NK):
                for j in range(ND):
                    last = tr(mp[k][:, j * P:(j + 1) * P], win_raw[:, j, k * P:(k + 1) * P], ident[:])
                last.then_inc(wt_full, 1)
            for j in range(ND):
                last = tr(dbu_ps[0][:, j * XR:(j + 1) * XR], xp_raw[:, j * P:(j + 1) * P], ident[0:XR, 0:XR])
            last.then_inc(wt_full, 1)
            for j in range(ND):
                last = tr(dbu_ps[1][0:RK, j * P:(j + 1) * P], dp_raw[:, j, :], ident[:])
            last.then_inc(wt_full, 1)
            pe.wait_ge(wt_read, 4)
            pe.sem_inc(dbu_ready, 2 * ND)
            pe.sem_inc(prod_used, RING)

            def ctx_transposes(bp):
                pe.wait_ge(ctx_loaded, 16 * (bp + 1))
                for k in range(NK):
                    pe.wait_ge(misc_read[k], mbase(bp) + 1)
                    for t in range(NL):
                        last = tr(mp[k][:, t * P:(t + 1) * P], ctx_cur[:, t, k * P:(k + 1) * P], ident[:])
                    last.then_inc(misc_full[k], 1)

            def in_proj(bp, j):
                u = 1 + j // 2
                pe.wait_ge(misc_read[j % 2], mbase(bp) + u + 1)
                if j == 0:
                    pe.wait_ge(misc_read[1], mbase(bp) + 2)
                for k in range(NK):
                    last = mm(mp[j % 2][:], winT[:, k, j * P:(j + 1) * P], ctxT[:, k, :],
                              start=k == 0, stop=k == NK - 1)
                last.then_inc(misc_full[j % 2], 1)

            def x_proj(bp):
                pe.wait_ge(misc_read[0], mbase(bp) + 4)
                pe.wait_ge(silu_done, bp * 2 * ND + ND)
                for j in range(ND):
                    last = mm(mp[0][0:XR, :], xpT[:, j, :],
                              xs[:, bass.ds(bp % 2, 1), j, :].rearrange("p a l -> p (a l)"),
                              start=j == 0, stop=j == ND - 1)
                last.then_inc(misc_full[0], 1)

            def b_transposes(bp):
                pe.wait_ge(misc_read[0], mbase(bp) + 5)
                pe.wait_ge(misc_read[1], mbase(bp) + 4)
                pe.sem_inc(wait_carrier, 1)
                for t in range(NL):
                    last = tr(mp[1][:, t * XR:(t + 1) * XR], xdbl[:, t * P:(t + 1) * P], ident[0:XR, 0:XR])
                last.then_inc(misc_full[1], 1)

            def dt_proj(bp, j):
                pe.wait_ge(misc_read[0], mbase(bp) + 5 + j)
                mm(mp[0][:], dpT[:, j * P:(j + 1) * P], xdbl[0:RK, :], start=True,
                   stop=True).then_inc(misc_full[0], 1)

            def du_transposes(bp, j):
                pe.wait_ge(du_ready, bp * ND + j + 1)
                pe.wait_ge(misc_read[1], mbase(bp) + 5 + j)
                for t in range(NL):
                    last = tr(mp[1][:, t * P:(t + 1) * P], du[:, j % 2, t * P:(t + 1) * P], ident[:])
                last.then_inc(misc_full[1], 1)

            def step(b, n, j):
                i = b * ITEMS + n * ND + j
                if j == 0:
                    pe.wait_ge(dbut_ready, b * NS + n + 1)
                    pe.wait_ge(dbut_last, b * NS + n + 1)
                pe.wait_ge(scanned, i - 1 + RING)
                for t in range(NL):
                    last = tr(dbu_ps[j % 2][:, t * P:(t + 1) * P], dbuT[:, n % 2, t, j * P:(j + 1) * P], ident[:])
                last.then_inc(dbu_ready, 1)

            def open_y(b, j):
                pe.wait_ge(y_taken, b * ND + j + 1)
                mm(y_ps[j][:], zb16[:], zmov[:], start=True, stop=False)

            def close_y(b, j):
                mm(y_ps[j][:], zb16[:], zmov[:], start=False, stop=True).then_inc(y_done, 1)

            def add_y(b, n, j):
                i = b * ITEMS + n * ND + j
                pe.wait_ge(prod_ready, i + 1 + RING)
                mm(y_ps[j][:], ident[:], prod[:, slot_of(n, j), :], start=False, stop=False).then_inc(prod_used, 1)

            def y_transpose(b, t, prepared):
                pe.wait_ge(y3_ready, (b + 1) * ND)
                if t < 2:
                    pe.wait_ge(misc_read[t], mbase(prepared) + 1)
                else:
                    pe.wait_ge(post_read[t % 2], b * 2 + 1)
                for j in range(ND):
                    last = tr(mp[t % 2][:, j * P:(j + 1) * P], y3[:, j, t * P:(t + 1) * P], ident[:])
                last.then_inc(post_full[t % 2], 1)

            def pieces(bp, n, j):
                if (n, j) == (3, 1):
                    ctx_transposes(bp)
                elif 4 <= n < 8 and j == 0:
                    in_proj(bp, n - 4)
                elif (n, j) == (9, 1):
                    x_proj(bp)
                elif (n, j) == (10, 0):
                    b_transposes(bp)
                elif 10 <= n < 14 and j == 1:
                    dt_proj(bp, n - 10)
                elif 11 <= n < 15 and j == 3:
                    du_transposes(bp, n - 11)

            def first_steps(b, before=None):
                for j in range(ND):
                    step(b, 0, j)
                    if before is not None:
                        add_y(before, NS - 1, j)
                        close_y(before, j)
                for j in range(ND):
                    step(b, 1, j)
                    open_y(b, j)
                    add_y(b, 0, j)
                    if before is not None and j >= 2:
                        y_transpose(before, 2 * j - 4, before + 2)
                        y_transpose(before, 2 * j - 3, before + 2)

            pe.wait_ge(misc_read[0], 1)
            for n in range(2, NS):
                for j in range(ND):
                    pieces(0, n, j)
            first_steps(0)
            with pe.Fori(0, NB - 1) as b:
                for n in range(2, NS):
                    for j in range(ND):
                        step(b, n, j)
                        add_y(b, n - 1, j)
                        pieces(b + 1, n, j)
                first_steps(b + 1, before=b)
            for n in range(2, NS):
                for j in range(ND):
                    step(NB - 1, n, j)
                    add_y(NB - 1, n - 1, j)
            for j in range(ND):
                add_y(NB - 1, NS - 1, j)
                close_y(NB - 1, j)
            for t in range(NL):
                y_transpose(NB - 1, t, NB)

            pe.wait_ge(p1_done, 1)
            for k in range(KH):
                last = tr(psHT[:, k, 0:NE], gate_raw[:, k * P:(k + 1) * P], ident[0:NE, 0:NE])
            last.then_inc(gw_full, 1)

            def made(t, k):
                return xn_made, t + 1, xin[:, k]

            def loaded(n, k):
                return xin_ready[k], 16 * ((n >> 1) + 1), xin[:, k]

            def routed_rows(r, k4):
                return slot_x_ready[k4], 16 * ((r >> 2) + 1), gbuf[:, k4]

            def transpose_x(q, k, source):
                ready, count, rows = source
                pe.wait_ge(ready, count)
                pe.wait_ge(xl_ready, q + 1)
                for c in range(KH):
                    last = tr(psT[:, c, :], rows[:, c * P:(c + 1) * P], ident[:])
                last.then_inc(xT_done, 1)

            def half_product(ps, w0, k, buf, width=INTER):
                n = 0
                for c in range(KH):
                    for a, w in ((xh, wgu_h), (xh, wgu_l), (xl, wgu_h)):
                        last = mm(ps[:, 0:width], a[:, k, c, :], w_at(w, buf)[:, c, w0:w0 + width],
                                  start=n == 0, stop=n == 3 * KH - 1)
                        n += 1
                return last

            def w_at(w, buf):
                if isinstance(buf, int):
                    return w[:, buf]
                return w[:, bass.ds(buf, 1)].rearrange("p a k c -> p (a k) c")

            def transpose_h(q, k):
                pe.wait_ge(h_ready, q + 1 + 2)
                pe.wait_ge(hl_ready, q + 2)
                for c in range(3):
                    last = tr(psHT[:, c, :], hbuf[:, k, c * P:(c + 1) * P], ident[:])
                last.then_inc(hT_done, 1)

            def if_used(used, products, done):
                if used is None:
                    products().then_inc(done, 1)
                    return
                with pe.If(used):
                    products().then_inc(done, 1)
                with pe.Else():
                    pe.sem_inc(done, 1)

            def down(q, k, buf, used):
                pe.wait_ge(hl_ready, q + 1 + 2)
                pe.wait_ge(y_read, q + 1)

                def products():
                    n = 0
                    for c in range(3):
                        rows = P if c < 2 else ILAST
                        for a, w in ((hh, wd_h), (hh, wd_l), (hl, wd_h)):
                            last = mm(psY[k][:], a[0:rows, k, c, :], w_at(w, buf)[0:rows, c, :],
                                      start=n == 0, stop=n == 8)
                            n += 1
                    return last

                if_used(used, products, y_full)

            def slot(q, k, buf, prev_buf, source, router=False, first=False, prev_rank=None, before_down=None,
                     used=None, prev_used=None):
                pe.wait_ge(xl_ready, q + 2)
                pe.wait_ge(h_ready, q + 1)
                if_used(used, lambda: half_product(psG[k], 0, k, buf), g_done)
                if not first:
                    transpose_h(q - 1, 1 - k)
                if source is not None:
                    transpose_x(q + 1, 1 - k, source)
                width = INTER + NE if router else INTER
                if_used(used, lambda: half_product(psU[k], INTER, k, buf, width), gu_done)
                if before_down is not None:
                    before_down()
                if not first:
                    if prev_rank is not None:
                        pe.wait_ge(d_split, prev_rank + 3)
                    down(q - 1, 1 - k, prev_buf, prev_used)

            transpose_x(0, 0, made(0, 0))
            pe.wait_ge(gu_split, 1)
            pe.wait_ge(d_split, 1)
            pe.wait_ge(gw_ready, 1)
            slot(0, 0, 0, 0, made(1, 1), router=True, first=True)
            slot(1, 1, 0, 0, made(2, 0), router=True)
            with pe.Fori(1, NT // 2 - 1) as m:
                for k in range(2):
                    slot(m * 2 + k, k, 0, 0, made(m * 2 + k + 1, 1 - k), router=True)
            slot(NT - 2, 0, 0, 0, made(NT - 1, 1), router=True)
            slot(NT - 1, 1, 0, 0, loaded(0, 0), router=True)
            pe.wait_ge(gu_split, 2)
            pe.wait_ge(d_split, 2)
            slot(NT, 0, 2, 0, loaded(1, 1))
            slot(NT + 1, 1, 2, 2, loaded(2, 0))
            pe.wait_ge(rt_mask, 1)
            pe.wait_ge(hl_ready, NT + 1 + 2)
            counts = psHT[:].rearrange("p c n -> p (c n)")
            marks = msum[:].rearrange("p t e -> p (t e)")
            mm(counts[:, 0:NT * NE], upper[:], marks, start=True, stop=True)
            mm(counts[:, NT * NE:], ones[:], marks, start=True, stop=True).then_inc(rt_count, 1)
            pe.wait_ge(cnt_read, 1)
            with pe.Fori(1, NB1 // 2 - 1) as m:
                for k in range(2):
                    slot(m * 2 + k + NT, k, 2, 2, loaded(m * 2 + k + 1, 1 - k))
            Q0 = NT + NB1
            slot(Q0 - 2, 0, 2, 2, loaded(NB1 - 1, 1))
            slot(Q0 - 1, 1, 2, 2, routed_rows(0, 0))

            def read_rank(r):
                pe.sem_inc(wait_carrier, 1)
                return pe.value_load(rank_i[0:1, bass.ds(r, 1)], min_val=0, max_val=NE)

            def read_used(r):
                return pe.value_load(used_i[0:1, bass.ds(r, 1)], min_val=0, max_val=1)

            def routed_slots(r0, n, source, before=None, before_used=None, full=True):
                ranks = [before, read_rank(r0)]
                used = [before_used, None if full else read_used(r0)]

                def read_next():
                    ranks.append(read_rank(r0 + i + 1))
                    used.append(None if full else read_used(r0 + i + 1))

                for i in range(n):
                    before, rank = ranks[i], ranks[i + 1]
                    pe.wait_ge(gu_split, rank + 3)
                    pe.wait_ge(gu_split_last, rank + 1)
                    slot(r0 + i + Q0, i % 2, rank % 2, 2 if before is None else before % 2, source(i),
                         prev_rank=before, before_down=read_next if i < n - 1 else None,
                         used=used[i + 1], prev_used=used[i])
                return ranks[n], used[n]

            def loop_source(m):
                return lambda i: routed_rows(m * 4 + i + 1, (i + 1) % 4)

            FULL = 2 * T // P
            pe.wait_ge(table_ready, 4)
            routed_slots(0, 4, lambda i: routed_rows(i + 1, (i + 1) % 4))
            with pe.Fori(1, FULL // 4) as m:
                routed_slots(m * 4, 4, loop_source(m), before=read_rank(m * 4 - 1))
            with pe.Fori(FULL // 4, SLOTS // 4 - 1) as m:
                routed_slots(m * 4, 4, loop_source(m), before=read_rank(m * 4 - 1),
                             before_used=read_used(m * 4 - 1), full=False)
            R1 = SLOTS - 4
            before, before_used = routed_slots(
                R1, 4, lambda i: routed_rows(R1 + i + 1, i + 1) if i < 3 else loaded(NB1, 0),
                before=read_rank(R1 - 1), before_used=read_used(R1 - 1), full=False)
            Q1 = Q0 + SLOTS
            slot(Q1, 0, 2, before % 2, loaded(NB1 + 1, 1), prev_rank=before, prev_used=before_used)
            slot(Q1 + 1, 1, 2, 2, loaded(NB1 + 2, 0))
            with pe.Fori(1, (NT - NB1) // 2 - 1) as m:
                for k in range(2):
                    slot(m * 2 + k + Q1, k, 2, 2, loaded(m * 2 + k + 1 + NB1, 1 - k))
            QE = Q1 + NT - NB1
            slot(QE - 2, 0, 2, 2, loaded(NT - 1, 1))
            slot(QE - 1, 1, 2, 2, None)
            transpose_h(QE - 1, 1)
            down(QE - 1, 1, 2, None)

        @block.scalar
        def _(act):
            def par(buf, b):
                return buf[:, bass.ds(b % 2, 1)].rearrange("p a j l -> p (a j) l")

            act.wait_ge(consts_in, 16 * NCONST)
            nc.scalar.activation(Aneg[:], Aneg[:], ACT.Exp).then_inc(a_exp, 1)
            nc.scalar.activation(tg[:], tg[:], ACT.Tanh).then_inc(tg_ready, 1)
            act.wait_ge(a_exp, 1)
            nc.scalar.mul(Aneg[:], Aneg[:], -1.0).then_inc(a_ready, 1)
            act.wait_ge(a_ready, 1)
            nc.scalar.preload_act_table_set("natural_log_exp_and_others")

            def ln_seed(rs, ready, done, count):
                act.wait_ge(ready, count)
                nc.scalar.activation(rs[:, 1, :], rs[:, 0, :], ACT.Ln).then_inc(done, 1)
                act.wait_ge(done, count * 2 - 1)
                nc.scalar.activation(rs[:, 2, :], rs[:, 1, :], ACT.Exp, scale=-0.5).then_inc(done, 1)

            def silus(bp):
                act.wait_ge(conv_tap, (bp + 1) * ND * TAPS)
                for j in range(ND):
                    nc.scalar.activation(par(xs, bp)[:, j, :], par(xs, bp)[:, j, :], ACT.Silu
                                         ).then_inc(silu_done, 1)
                act.wait_ge(ln1_dve, (bp + 1) * 12)
                act.sem_inc(wait_carrier, 1)
                for j in range(ND):
                    nc.scalar.activation(par(zs, bp)[:, j, :],
                                         x_tok[:, bass.ds(bp * NL + j, 1), :].rearrange("p a c -> p (a c)"),
                                         ACT.Silu, bias=rs1[:, 4, j:j + 1],
                                         scale=rs1[:, 3, j:j + 1]).then_inc(silu_done, 1)
                nc.scalar.preload_act_table_set("natural_log_exp_and_others")

            def softplus_parts(bp, j):
                if j > 0 or not isinstance(bp, int):
                    act.wait_ge(du_ready, bp * ND + j)
                act.wait_ge(misc_full[0], mbase(bp) + 5 + j)
                nc.scalar.activation(sp_a, mp[0][:], ACT.Abs, bias=db[:, j:j + 1]).then_inc(sp_abs, 1)
                act.wait_ge(sp_abs, bp * ND + j + 1)
                nc.scalar.activation(sp_u, sp_a, ACT.Exp, scale=-1.0).then_inc(sp_exp, 1)
                act.wait_ge(sp_exp, bp * ND + j + 1)
                nc.scalar.activation(sp_l, sp_u, ACT.Ln, bias=1.0).then_inc(sp_ln, 1)

            def du_to_time(bp, j):
                act.wait_ge(misc_full[1], mbase(bp) + 5 + j)
                nc.scalar.copy(par(duT, bp)[:, :, j * P:(j + 1) * P],
                               mp[1][:].rearrange("p (t d) -> p t d", t=NL)).then_inc(dut_ready, 1)
                act.wait_ge(dut_ready, bp * ND + j + 1)
                act.sem_inc(misc_read[1], 1)

            def decay(b, n, j):
                act.wait_ge(scanned, b * ITEMS + n * ND + j + 1)
                act.sem_inc(wait_carrier, 1)
                nc.scalar.activation(dA[:, slot_of(n, j), :], par(dts, b)[:, j, :], ACT.Exp,
                                     scale=Aneg[:, j, n:n + 1]).then_inc(da_ready, 1)

            def input_terms(b, n):
                if n == 0:
                    act.wait_ge(dut_ready, (b + 1) * ND)
                    act.sem_inc(wait_carrier, 1)
                act.wait_ge(dbu_ready, (b * NS + n + 1) * ND)
                for t in range(NL - 1):
                    last = nc.scalar.activation(dbuT[:, n % 2, t, :], par(duT, b)[:, t, :], ACT.Copy,
                                                scale=par(BT, b)[:, t, RK + n:RK + n + 1])
                last.then_inc(dbut_ready, 1)

            def step(b, n, bp=None):
                for j in range(ND):
                    if (n, j) == (0, 0):
                        act.wait_ge(du_ready, (b + 1) * ND)
                        act.sem_inc(wait_carrier, 1)
                    decay(b, n, j)
                    if j == 2:
                        input_terms(b, n)
                    if bp is not None:
                        pieces(bp, n, j)

            def pieces(bp, n, j):
                if (n, j) == (6, 3):
                    ln_seed(rs1, ln1_var, ln1_act, bp + 1)
                elif (n, j) == (9, 3):
                    silus(bp)
                elif 12 <= n < 16 and j == 1:
                    softplus_parts(bp, n - 12)
                if 13 <= n < 16 and j == 3:
                    du_to_time(bp, n - 13)
                if (n, j) == (0, 1):
                    du_to_time(bp, 3)

            for n in range(2, NS):
                for j in range(ND):
                    pieces(0, n, j)
            step(0, 0, 0)
            step(0, 1)
            with act.Fori(0, NB - 1) as b:
                for n in range(2, NS):
                    step(b, n, b + 1)
                step(b + 1, 0, b + 1)
                step(b + 1, 1)
            def gu_chunk_hi(c, dst):
                nc.scalar.copy(dst(wgu_h)[:, c, 0:2 * INTER], raw_gu[:, c, :]).then_inc(gu_hi, 1)

            def d_chunk_hi(c, dst):
                rows = P if c < 2 else ILAST
                nc.scalar.copy(dst(wd_h)[0:rows, c, :], raw_d[0:rows, c, :]).then_inc(d_hi, 1)

            def split_gu_hi(loaded, dst):
                act.wait_ge(raw_gu_loaded, loaded)
                for c in range(KH):
                    gu_chunk_hi(c, dst)

            def split_d_hi(loaded, dst):
                act.wait_ge(raw_d_loaded, loaded)
                for c in range(3):
                    d_chunk_hi(c, dst)

            def split_hi(loaded, dst):
                split_gu_hi(loaded, dst)
                split_d_hi(loaded, dst)

            def static(buf):
                return lambda w: w[:, buf]

            for n in range(2, NS):
                step(NB - 1, n)
                if n == 4:
                    act.wait_ge(y3_ready, (NB - 1) * ND)
                    act.wait_ge(raw_gu_loaded, 32)
                    act.wait_ge(raw_d_loaded, 32)
                if 4 <= n < 8:
                    gu_chunk_hi(n - 4, static(0))
                elif 8 <= n < 11:
                    d_chunk_hi(n - 8, static(0))
            ln_seed(rs2, ln2_var, ln2_act, 1)

            act.wait_ge(p1_done, 1)
            act.wait_ge(gw_full, 1)
            nc.scalar.copy(gw_h, psHT[:, :, 0:NE]).then_inc(gw_hi, 1)

            def slot(q, k, first=False, last_slot=False, load=None):
                if not first:
                    act.wait_ge(hT_done, q)
                    nc.scalar.copy(hh[:, 1 - k, :, :], psHT[:, 0:3, :]).then_inc(hh_ready, 1)
                if not last_slot:
                    act.wait_ge(xT_done, q + 2)
                    nc.scalar.copy(xh[:, 1 - k, :, :], psT[:]).then_inc(xh_ready, 1)
                if load is not None:
                    act.dma_start(xin[:, 1 - k, :], xn_rows[bass.ds(load * P, P), :]).then_inc(xin_ready[1 - k], 16)
                act.wait_ge(g_done, q + 1)
                nc.scalar.activation(sg[:, k, :], psG[k][:, 0:INTER], ACT.Silu).then_inc(sg_ready, 1)

            act.wait_ge(xT_done, 1)
            nc.scalar.copy(xh[:, 0, :, :], psT[:]).then_inc(xh_ready, 1)
            slot(0, 0, first=True)
            slot(1, 1)
            split_hi(64, static(2))
            with act.Fori(1, NT // 2) as m:
                for k in range(2):
                    slot(m * 2 + k, k)
            slot(NT, 0, load=3)
            slot(NT + 1, 1, load=4)
            act.wait_ge(rt_shift, 1)
            nc.scalar.activation(ex[:], ex[:], ACT.Exp).then_inc(rt_act, 1)
            for n in range(2, NB1 - 2):
                slot(NT + n, n % 2, load=n + 3 if n + 3 < NB1 else None)
            Q0 = NT + NB1
            slot(Q0 - 2, 0)
            split_hi(96, static(0))
            slot(Q0 - 1, 1)
            act.wait_ge(table_ready, 4)

            def to_buffer(r):
                chg = act.value_load(chg_i[0:1, bass.ds(r, 1)], min_val=0, max_val=1)
                rank = act.value_load(rank_i[0:1, bass.ds(r, 1)], min_val=0, max_val=NE)
                buf = (rank + 1) % 2
                return chg, lambda w: w[:, bass.ds(buf, 1)].rearrange("p a k c -> p (a k) c")

            def down_hi(r):
                chg, dst = to_buffer(r)
                with act.If(chg):
                    split_d_hi(128 + 32 * r, dst)

            def routed_slot(r, k, first=False):
                slot(r + Q0, k)
                if not first:
                    down_hi(r - 1)
                chg, dst = to_buffer(r)
                with act.If(chg):
                    act.wait_ge(y_full, r + Q0)
                    split_gu_hi(128 + 32 * r, dst)

            routed_slot(0, 0, first=True)
            routed_slot(1, 1)
            with act.Fori(1, SLOTS // 2) as m:
                for k in range(2):
                    routed_slot(m * 2 + k, k)
            down_hi(SLOTS - 1)
            Q1 = Q0 + SLOTS
            with act.Fori(0, (NT - NB1) // 2 - 1) as m:
                for k in range(2):
                    slot(m * 2 + k + Q1, k)
            QE = Q1 + NT - NB1
            slot(QE - 2, 0)
            slot(QE - 1, 1, last_slot=True)
            act.wait_ge(hT_done, QE)
            nc.scalar.copy(hh[:, 1, :, :], psHT[:, 0:3, :]).then_inc(hh_ready, 1)

        @block.vector
        def _(dve):
            V = nc.vector

            def par(buf, b):
                return buf[:, bass.ds(b % 2, 1)].rearrange("p a j l -> p (a j) l")

            dve.wait_ge(wt_full, 4)
            for k in range(NK):
                V.tensor_copy(winT[:, k, :], mp[k][:]).then_inc(wt_read, 1)
            V.tensor_copy(xpT[:].rearrange("p j e -> p (j e)"), dbu_ps[0][:, 0:ND * XR]).then_inc(wt_read, 1)
            V.tensor_copy(dpT[:], dbu_ps[1][0:RK, :]).then_inc(wt_read, 1)
            for k in range(2):
                dve.sem_inc(misc_read[k], 1)
            dve.sem_inc(scanned, RING)
            dve.sem_inc(y_taken, ND)
            dve.wait_ge(x_in, 16)
            dve.wait_ge(consts_in, 16 * NCONST)

            def tile_of(b, j):
                return x_tok[:, bass.ds(b * NL + j, 1), :].rearrange("p a c -> p (a c)")

            def ln_refine(rs, n, c0, steps):
                V.tensor_tensor(rs[:, 1, :], rs[:, 2, :], rs[:, 2, :], ALU.mult).then_inc(steps, 1)
                dve.wait_ge(steps, c0 + 1)
                V.scalar_tensor_tensor(rs[:, 3, :], rs[:, 1, :], -0.5, rs[:, 0, :], ALU.mult,
                                       ALU.mult).then_inc(steps, 1)
                dve.wait_ge(steps, c0 + 2)
                V.scalar_tensor_tensor(rs[:, 3, :], rs[:, 3, :], 1.5, rs[:, 2, :], ALU.add,
                                       ALU.mult).then_inc(steps, 1)
                dve.wait_ge(steps, c0 + 3)

            def z_stats(bp, j):
                V.bn_stats(st1[:, j, :], tile_of(bp, j)).then_inc(ln1_dve, 1)

            def z_var(bp):
                dve.wait_ge(ln1_dve, bp * 12 + ND)
                dve.sem_inc(wait_carrier, 1)
                for j in range(ND):
                    V.bn_aggr(mv1[:, j, :], st1[:, j, :]).then_inc(ln1_dve, 1)
                dve.wait_ge(ln1_dve, bp * 12 + 2 * ND)
                V.tensor_scalar(rs1[:, 0, :], mv1[:, :, 1], EPS, None, ALU.add).then_inc(ln1_var, 1)

            def z_scale(bp):
                dve.wait_ge(ln1_act, (bp + 1) * 2)
                ln_refine(rs1, ND, bp * 12 + 8, ln1_dve)
                V.scalar_tensor_tensor(rs1[:, 4, :], mv1[:, :, 0], -1.0, rs1[:, 3, :], ALU.mult,
                                       ALU.mult).then_inc(ln1_dve, 1)

            def ctx_to_sbuf(bp, k):
                dve.wait_ge(misc_full[k], mbase(bp) + 1)
                V.tensor_copy(ctxT[:, k, :], mp[k][:]).then_inc(misc_read[k], 1)

            def conv(bp, j, s):
                k, u = j % 2, 1 + j // 2
                xj = par(xs, bp)[:, j, :]
                c0 = (bp * ND + j) * TAPS
                if s == 0:
                    dve.wait_ge(misc_full[k], mbase(bp) + u + 1)
                    V.tensor_scalar(xj, mp[k][:], cw[:, j, TAPS - 1:TAPS], cb[:, j:j + 1], ALU.mult,
                                    ALU.add).then_inc(conv_tap, 1)
                    return
                dve.wait_ge(conv_tap, c0 + s)
                V.scalar_tensor_tensor(xj[:, s:], mp[k][:, 0:L - s], cw[:, j, TAPS - 1 - s:TAPS - s],
                                       xj[:, s:], ALU.mult, ALU.add).then_inc(conv_tap, 1)
                if s == TAPS - 1:
                    dve.wait_ge(conv_tap, c0 + TAPS)
                    dve.sem_inc(misc_read[k], 1)

            def x_proj_to_sbuf(bp):
                if not (isinstance(bp, int) and bp == 0):
                    dve.wait_ge(c_stored, 16 * bp)
                dve.wait_ge(misc_full[0], mbase(bp) + 4)
                V.tensor_copy(xdbl[:], mp[0][0:XR, :]).then_inc(misc_read[0], 1)

            def b_to_sbuf(bp):
                dve.wait_ge(misc_full[1], mbase(bp) + 4)
                V.tensor_copy(par(BT, bp).rearrange("p t e -> p (t e)"),
                              mp[1][:, 0:NL * XR]).then_inc(misc_read[1], 1)

            def softplus_in(bp, j):
                dve.wait_ge(misc_full[0], mbase(bp) + 5 + j)
                dve.wait_ge(sp_abs, bp * ND + j + 1)
                V.tensor_scalar(sp_r, mp[0][:], db[:, j:j + 1], 0.0, ALU.add,
                                ALU.max).then_inc(misc_read[0], 1)

            def softplus_out(bp, j, part):
                c0 = (bp * ND + j) * 4
                if part == 0:
                    dve.wait_ge(sp_ln, bp * ND + j + 1)
                    V.tensor_scalar(sp_t[:], sp_u, 1.0, -1.0, ALU.add, ALU.add).then_inc(sp_dve, 1)
                    dve.wait_ge(misc_read[0], mbase(bp) + 6 + j)
                    V.tensor_tensor(sp_r, sp_r, sp_l, ALU.add).then_inc(sp_dve, 1)
                elif part == 1:
                    dve.wait_ge(sp_dve, c0 + 2)
                    V.tensor_tensor(sp_t[:], sp_t[:], sp_u, ALU.subtract).then_inc(sp_dve, 1)
                    dve.wait_ge(sp_dve, c0 + 3)
                    V.tensor_tensor(par(dts, bp)[:, j, :], sp_r, sp_t[:], ALU.subtract).then_inc(sp_dve, 1)
                else:
                    dve.wait_ge(sp_dve, c0 + 4)
                    dve.wait_ge(silu_done, bp * 2 * ND + j + 1)
                    V.tensor_tensor(du[:, j % 2, :], par(dts, bp)[:, j, :], par(xs, bp)[:, j, :],
                                    ALU.mult).then_inc(du_ready, 1)

            def scan(b, n, j):
                i = b * ITEMS + n * ND + j
                dve.wait_ge(da_ready, i + 1)
                dve.wait_ge(dbu_ready, i + 1 + 2 * ND)
                dve.wait_ge(prod_ready, i + 1)
                V.tensor_tensor_scan(hst[:, slot_of(n, j), :], dA[:, slot_of(n, j), :], dbu_ps[j % 2][:], 0.0,
                                     ALU.mult, ALU.add).then_inc(scanned, 1)

            def input_terms(b, n):
                if n == 0:
                    dve.wait_ge(dut_ready, (b + 1) * ND)
                dve.wait_ge(dbu_ready, (b * NS + n + 1) * ND)
                dve.sem_inc(wait_carrier, 1)
                t = NL - 1
                V.tensor_scalar(dbuT[:, n % 2, t, :], par(duT, b)[:, t, :], par(BT, b)[:, t, RK + n:RK + n + 1],
                                None, ALU.mult).then_inc(dbut_last, 1)

            def add_du(b, j):
                dve.wait_ge(y_done, b * ND + j + 1)
                V.scalar_tensor_tensor(y3[:, j, :], par(xs, b)[:, j, :], Dv[:, j:j + 1], y_ps[j][:],
                                       ALU.mult, ALU.add).then_inc(y_taken, 1)

            def gate(b, j):
                dve.wait_ge(y_taken, b * ND + j + 1 + ND)
                V.scalar_tensor_tensor(y3[:, j, :], y3[:, j, :], tg[:, 0:1], par(zs, b)[:, j, :],
                                       ALU.mult, ALU.mult).then_inc(y3_ready, 1)

            def residual(b, t):
                dve.wait_ge(post_full[t % 2], b * 2 + t // 2 + 1)
                V.tensor_tensor(tile_of(b, t), tile_of(b, t), mp[t % 2][:], ALU.add).then_inc(x1_ready, 1)
                dve.wait_ge(x1_ready, b * NL + t + 1)
                dve.sem_inc(post_read[t % 2], 1)

            def x1_stats(b, t):
                V.bn_stats(st2[:, bass.ds(b * NL + t, 1), :].rearrange("p a c -> p (a c)"),
                           tile_of(b, t)).then_inc(ln2_dve, 1)

            def post(b, n, j):
                if n == 0:
                    if j >= 1:
                        add_du(b, j - 1)
                    if j >= 2:
                        gate(b, j - 2)
                else:
                    if j == 0:
                        add_du(b, 3)
                        gate(b, 2)
                    elif j == 1:
                        gate(b, 3)
                    else:
                        residual(b, j - 2)

            def rest_of_post(b):
                residual(b, 2)
                residual(b, 3)
                for t in range(NL):
                    x1_stats(b, t)

            def pieces(bp, n, j):
                if n in (2, 3):
                    if j >= 2:
                        z_stats(bp, (n - 2) * 2 + j - 2)
                    if n == 3 and j >= 2:
                        ctx_to_sbuf(bp, j - 2)
                if (n, j) == (4, 0):
                    z_var(bp)
                if 4 <= n < 8 and j >= 1:
                    conv(bp, n - 4, j - 1)
                if 5 <= n < 9 and j == 0:
                    conv(bp, n - 5, 3)
                if (n, j) == (6, 2):
                    z_scale(bp)
                if (n, j) == (9, 2):
                    x_proj_to_sbuf(bp)
                if (n, j) == (10, 1):
                    b_to_sbuf(bp)
                if 11 <= n < 15 and j < 3:
                    softplus_out(bp, n - 11, j)
                if 10 <= n < 14 and j == 3:
                    softplus_in(bp, n - 10)

            def item(b, n, j, last=False):
                scan(b, n, j)
                if j == 1 and not last:
                    if n < NS - 1:
                        input_terms(b, n + 1)
                    else:
                        input_terms(b + 1, 0)

            dve.wait_ge(a_ready, 1)
            dve.wait_ge(tg_ready, 1)
            for n in range(2, NS):
                for j in range(ND):
                    pieces(0, n, j)
            input_terms(0, 0)
            for n in range(2):
                for j in range(ND):
                    item(0, n, j)
            dve.wait_ge(x_in, 32)
            with dve.Fori(0, NB - 1) as b:
                for n in range(2, NS):
                    for j in range(ND):
                        item(b, n, j)
                        pieces(b + 1, n, j)
                for n in range(2):
                    for j in range(ND):
                        item(b + 1, n, j)
                        post(b, n, j)
                rest_of_post(b)
            def static(buf):
                return lambda w: w[:, buf]

            def gu_chunk_lo(ordinal, c, dst):
                dve.wait_ge(gu_hi, ordinal * KH + c + 1)
                return V.tensor_tensor(dst(wgu_l)[:, c, 0:2 * INTER], raw_gu[:, c, :],
                                       dst(wgu_h)[:, c, 0:2 * INTER].bitcast(F32), ALU.subtract)

            def d_chunk_lo(ordinal, c, dst):
                rows = P if c < 2 else ILAST
                dve.wait_ge(d_hi, ordinal * 3 + c + 1)
                return V.tensor_tensor(dst(wd_l)[0:rows, c, :], raw_d[0:rows, c, :],
                                       dst(wd_h)[0:rows, c, :].bitcast(F32), ALU.subtract)

            def split_gu_lo(ordinal, dst, chunks=KH):
                for c in range(chunks):
                    ins = gu_chunk_lo(ordinal, c, dst)
                ins.then_inc(gu_split, 1)

            def split_lo(ordinal, dst):
                split_gu_lo(ordinal, dst)
                for c in range(3):
                    ins = d_chunk_lo(ordinal, c, dst)
                ins.then_inc(d_split, 1)

            for n in range(2, NS):
                for j in range(ND):
                    item(NB - 1, n, j, last=n == NS - 1)
                    if 8 <= n < 12 and j == 3:
                        ins = gu_chunk_lo(0, n - 8, static(0))
                        if n == 11:
                            ins.then_inc(gu_split, 1)
                    elif 12 <= n < 15 and j == 3:
                        ins = d_chunk_lo(0, n - 12, static(0))
                        if n == 14:
                            ins.then_inc(d_split, 1)
            for j in range(ND):
                add_du(NB - 1, j)
                gate(NB - 1, j)
            for t in range(NL):
                residual(NB - 1, t)
                x1_stats(NB - 1, t)
            dve.wait_ge(ln2_dve, NT)
            dve.sem_inc(wait_carrier, 1)
            for t in range(NT):
                V.bn_aggr(mv2[:, t, :], st2[:, t, :]).then_inc(ln2_dve, 1)
            dve.wait_ge(ln2_dve, 2 * NT)
            V.tensor_scalar(rs2[:, 0, :], mv2[:, :, 1], EPS, None, ALU.add).then_inc(ln2_var, 1)
            dve.wait_ge(ln2_act, 2)
            ln_refine(rs2, NT, 2 * NT, ln2_dve)
            dve.sem_inc(p1_done, 1)

            def normalise(t, k):
                if not isinstance(t, int) or t >= 2:
                    dve.wait_ge(xT_done, t - 1)
                    dve.wait_ge(xn_stored[k], 16 * (t >> 1))
                    dve.sem_inc(wait_carrier, 1)
                V.tensor_scalar(xin[:, k, :], x_tok[:, bass.ds(t, 1), :].rearrange("p a c -> p (a c)"),
                                mv2[:, bass.ds(t, 1), 0], rs2[:, 3, bass.ds(t, 1)],
                                ALU.subtract, ALU.mult).then_inc(xn_made, 1)

            normalise(0, 0)
            normalise(1, 1)

            dve.sem_inc(xl_ready, 1)
            dve.sem_inc(h_ready, 2)
            dve.sem_inc(hl_ready, 2)
            dve.sem_inc(y_read, 2)
            dve.wait_ge(p2_consts, 8)
            dve.wait_ge(gw_hi, 1)
            V.tensor_tensor(gw_l, psHT[:, :, 0:NE], gw_h.bitcast(F32), ALU.subtract).then_inc(gw_ready, 1)

            def h_lo(q, k):
                dve.wait_ge(hT_done, q + 1)
                dve.wait_ge(hh_ready, q + 1)
                V.tensor_tensor(hl[:, k, :, :], psHT[:, 0:3, :], hh[:, k, :, :].bitcast(F32),
                                ALU.subtract).then_inc(hl_ready, 1)

            def x_lo(q, k):
                dve.wait_ge(xT_done, q + 1)
                dve.wait_ge(xh_ready, q + 1)
                V.tensor_tensor(xl[:, k, :, :], psT[:], xh[:, k, :, :].bitcast(F32),
                                ALU.subtract).then_inc(xl_ready, 1)

            def token_tile(t):
                return x_tok[:, bass.ds(t, 1), :].rearrange("p a c -> p (a c)")

            def result_to(q, k, kind, t):
                dve.wait_ge(y_full, q + 1)
                if kind == "shared":
                    ins = V.scalar_tensor_tensor(token_tile(t), psY[k][:], tg[:, 1:2], token_tile(t),
                                                 ALU.mult, ALU.add)
                else:
                    if not isinstance(t, int) or t >= 2:
                        dve.wait_ge(y_stored[k], 16 * (t >> 1))
                    ins = V.tensor_copy(yout[:, k, :], psY[k][:])
                ins.then_inc(y_read, 1)

            def slot(q, k, kind, t, router=False, first=False, last_slot=False, make=False, before_result=None):
                if not first:
                    h_lo(q - 1, 1 - k)
                if not last_slot:
                    x_lo(q + 1, 1 - k)
                dve.wait_ge(sg_ready, q + 1)
                dve.wait_ge(gu_done, q + 1)
                if router:
                    V.tensor_copy(lg[:, bass.ds(q, 1), :].rearrange("p a e -> p (a e)"),
                                  psU[k][:, INTER:INTER + NE]).then_inc(lg_ready, 1)
                V.tensor_tensor(hbuf[:, k, 0:INTER], sg[:, k, :], psU[k][:, 0:INTER], ALU.mult
                                ).then_inc(h_ready, 1)
                if before_result is not None:
                    before_result()
                if not first:
                    result_to(q - 1, 1 - k, kind, t)
                if make:
                    normalise(q + 2, k)

            steps = [0]

            def link(ins):
                steps[0] += 1
                ins.then_inc(rt, 1)
                dve.wait_ge(rt, steps[0])

            x_lo(0, 0)
            slot(0, 0, "shared", 0, router=True, first=True, make=True)
            slot(1, 1, "shared", 0, router=True, make=True)
            split_lo(1, static(2))
            with dve.Fori(1, NT // 2 - 1) as m:
                for k in range(2):
                    slot(m * 2 + k, k, "shared", m * 2 + k - 1, router=True, make=True)
            for k in range(2):
                slot(NT - 2 + k, k, "shared", NT - 3 + k, router=True)
            slot(NT, 0, "shared", NT - 1)

            dve.wait_ge(lg_ready, NT)
            for t in range(NT):
                V.max(top8[:, t, :], lg[:, t, :]).then_inc(rt_top, 1)
            for t in range(NT):
                dve.wait_ge(rt_top, t + 1)
                V.max_index(idx8[:, t, :], top8[:, t, :], lg[:, t, :]).then_inc(rt_top, 1)
            dve.wait_ge(rt_top, 2 * NT)
            link(V.tensor_copy(e12[:], idx8[:, :, 0:2].rearrange("p t c -> p c t")))
            iota_b = iota_e[:].unsqueeze(1).broadcast_to([P, NT, NE])
            for c in range(2):
                ins = V.tensor_tensor(oh[:, c], iota_b, e12[:, c].unsqueeze(2).broadcast_to([P, NT, NE]),
                                      ALU.is_equal)
                link(ins)
            V.tensor_tensor(msum[:], oh[:, 0], oh[:, 1], ALU.add).then_inc(rt_mask, 1)
            V.tensor_tensor(ex[:], lg[:], top8[:, :, 0:1].broadcast_to([P, NT, NE]),
                            ALU.subtract).then_inc(rt_shift, 1)
            slot(NT + 1, 1, "shared", 0)
            dve.wait_ge(rt_count, 1)
            counts = psHT[:].rearrange("p c n -> p (c n)")
            link(V.tensor_copy(zpos[:].rearrange("p t e -> p (t e)"), counts[:, 0:NT * NE]))
            V.tensor_copy(cnt[:], counts[:, NT * NE:].rearrange("p (t e) -> p e t", t=NT)).then_inc(cnt_read, 1)
            dve.wait_ge(cnt_read, 1)
            flat = lambda a: a[:].rearrange("p e t -> p (e t)")
            link(V.tensor_tensor_scan(flat(cinc), onesf[:], flat(cnt), 0.0, ALU.mult, ALU.add))
            link(V.tensor_tensor(cexc[:], cinc[:], cnt[:], ALU.subtract))
            CE, TL, TE, ADJ, TMP = range(5)
            link(V.tensor_tensor(ce[:, CE], cinc[:, :, NT - 1], cexc[:, :, 0], ALU.subtract))
            link(V.tensor_scalar(cei[:, 0], ce[:, CE], float(P - 1), None, ALU.add))
            link(V.tensor_scalar(cei[:, 1], cei[:, 0], 7, None, ALU.logical_shift_right))
            link(V.tensor_copy(ce[:, TL], cei[:, 1]))
            link(V.tensor_tensor_scan(ce[:, TE], onesf[:, 0:NE], ce[:, TL], 0.0, ALU.mult, ALU.add))
            link(V.tensor_tensor(ce[:, TMP], ce[:, TE], ce[:, TL], ALU.subtract))
            link(V.scalar_tensor_tensor(ce[:, ADJ], ce[:, TMP], float(P), cexc[:, :, 0], ALU.mult,
                                        ALU.subtract))
            link(V.tensor_tensor(zpos[:], zpos[:], cexc[:].rearrange("p e t -> p t e"), ALU.add))
            link(V.tensor_tensor(zpos[:], zpos[:], ce[:, ADJ].unsqueeze(1).broadcast_to([P, NT, NE]), ALU.add))
            for c in range(2):
                link(V.tensor_tensor(ztmp[:], zpos[:], oh[:, c], ALU.mult))
                link(V.tensor_reduce(posf[:, c], ztmp[:], AX.X, ALU.add))
            V.tensor_copy(posi[:], posf[:]).then_inc(pos_ready, 1)
            link(V.memset(se[:, 0:1], -1.0))
            link(V.tensor_tensor(scmp, iota_s[:].unsqueeze(2).broadcast_to([1, SLOTS, NE]),
                                 ce[0:1, TE].unsqueeze(1).broadcast_to([1, SLOTS, NE]), ALU.is_ge))
            link(V.tensor_reduce(se[:, 1:], scmp, AX.X, ALU.add))
            link(V.tensor_scalar(se[:, 1:], se[:, 1:], float(NE - 1), None, ALU.min))
            V.tensor_scalar(used_i[:], iota_s[:], ce[0:1, TE, NE - 1:NE], None, ALU.is_lt).then_inc(table_ready, 1)
            link(V.tensor_tensor(schg[:], se[:, 1:], se[:, 0:SLOTS], ALU.not_equal))
            link(V.tensor_tensor_scan(srank[:], onesf[0:1, 0:SLOTS], schg[:], -1.0, ALU.mult, ALU.add))
            V.tensor_copy(chg_i[:], schg[:]).then_inc(table_ready, 1)
            V.tensor_copy(rank_i[:], srank[:]).then_inc(table_ready, 1)
            link(V.tensor_tensor(se[:, 1:], se[:, 1:], schg[:], ALU.mult))
            link(V.tensor_tensor(skcmp, iota_k[:].unsqueeze(2).broadcast_to([1, NDK, SLOTS]),
                                 srank[:].unsqueeze(1).broadcast_to([1, NDK, SLOTS]), ALU.is_equal))
            link(V.tensor_tensor(skcmp, skcmp, se[:, 1:].unsqueeze(1).broadcast_to([1, NDK, SLOTS]),
                                 ALU.mult))
            link(V.tensor_reduce(dk[:], skcmp, AX.X, ALU.add))
            V.tensor_copy(dk_i[:], dk[:]).then_inc(table_ready, 1)
            dve.wait_ge(rt_act, 1)
            link(V.tensor_reduce(esum[:], ex[:], AX.X, ALU.add))
            link(V.reciprocal(esum[:], esum[:]))
            link(V.tensor_scalar(esum[:], esum[:], tg[:, 1:2], None, ALU.mult))
            for c in range(2):
                link(V.tensor_tensor(ztmp[:], ex[:], oh[:, c], ALU.mult))
                link(V.tensor_reduce(wts[:, c], ztmp[:], AX.X, ALU.add))
                link(V.tensor_tensor(wts[:, c], wts[:, c], esum[:], ALU.mult))

            with dve.Fori(1, NB1 // 2 - 1) as m:
                for k in range(2):
                    slot(m * 2 + k + NT, k, "shared", m * 2 + k - 1)
            Q0 = NT + NB1
            slot(Q0 - 2, 0, "shared", NB1 - 3)
            split_lo(2, static(0))
            slot(Q0 - 1, 1, "shared", NB1 - 2)

            def routed_slot(r, k, kind="routed"):
                table = {}

                def read_tables():
                    table["chg"] = dve.value_load(chg_i[0:1, bass.ds(r, 1)], min_val=0, max_val=1)
                    table["rank"] = dve.value_load(rank_i[0:1, bass.ds(r, 1)], min_val=0, max_val=NE)

                slot(r + Q0, k, kind, r - 1 if kind == "routed" else NB1 - 1, before_result=read_tables)
                rank = table["rank"]
                buf = (rank + 1) % 2
                with dve.If(table["chg"]):
                    split_gu_lo(rank + 3, lambda w: w[:, bass.ds(buf, 1)].rearrange("p a k c -> p (a k) c"),
                                chunks=KH - 1)

            routed_slot(0, 0, "shared")
            routed_slot(1, 1)
            with dve.Fori(1, SLOTS // 2) as m:
                for k in range(2):
                    routed_slot(m * 2 + k, k)
            Q1 = Q0 + SLOTS

            def finish(i, t):
                i, k = i
                dve.wait_ge(gathered[k], 32 * ((i >> 1) + 1))
                for c in range(2):
                    ins = V.scalar_tensor_tensor(token_tile(t), gbuf[:, 2 * k + c, :],
                                                 wts[:, c, bass.ds(t, 1)], token_tile(t), ALU.mult, ALU.add)
                    if c == 0:
                        ins.then_inc(f_first, 1)
                        dve.wait_ge(f_first, i + 1)
                ins.then_inc(f_done, 1)

            def finish_pair(n, q):
                finish((n * 2, 0), n)
                dve.wait_ge(y_read, q + 1 + 2)
                finish((n * 2 + 1, 1), n + NB1)

            slot(Q1, 0, "routed", SLOTS - 1)
            slot(Q1 + 1, 1, "shared", NB1)
            finish_pair(0, Q1)
            with dve.Fori(1, (NT - NB1) // 2 - 1) as m:
                for k in range(2):
                    slot(m * 2 + k + Q1, k, "shared", m * 2 + k + NB1 - 1)
                    finish_pair(m * 2 + k - 1, m * 2 + k - 1 + Q1)
            QE = Q1 + NT - NB1
            for k in range(2):
                slot(QE - 2 + k, k, "shared", NT - 3 + k, last_slot=k == 1)
                finish_pair(NB1 - 3 + k, QE - 3 + k)
            h_lo(QE - 1, 1)
            finish((2 * NB1 - 2, 0), NB1 - 1)
            result_to(QE - 1, 1, "shared", NT - 1)
            dve.wait_ge(y_read, QE + 2)
            finish((2 * NB1 - 1, 1), NT - 1)


_INS = ['x', 'ctx_1024', 'g_xattn', 'g_ffn', 'L0_xattn_in_proj_w', 'L0_xattn_conv_w', 'L0_xattn_conv_b',
        'L0_xattn_x_proj_w', 'L0_xattn_dt_proj_w', 'L0_xattn_dt_proj_b', 'L0_xattn_A_log', 'L0_xattn_D',
        'L0_ffn_gate_w', 'L0_ffn_w_gate_up', 'L0_ffn_w_down', 'L0_ffn_shared_gate_up', 'L0_ffn_shared_down']
_OUTS = [((4, 512, 512), 'float32')]


def kernel(**inputs):
    import numpy as _np
    import concourse.bacc as _bacc
    from concourse import mybir as _mybir
    from concourse.bass_utils import run_bass_kernel_spmd as _run

    nc = _bacc.Bacc("TRN2", target_bir_lowering=False, num_devices=1)
    arrays, args = {}, []
    for name in _INS:
        a = _np.ascontiguousarray(inputs[name])
        arrays[f"in_{name}_dram"] = a
        args.append(nc.dram_tensor(f"in_{name}_dram", a.shape, _mybir.dt.from_np(a.dtype), kind="ExternalInput").ap())
    for i, (shape, dtype) in enumerate(_OUTS):
        dt = _mybir.dt.from_np(_np.dtype(dtype))
        args.append(nc.dram_tensor(f"out_{i}_dram", shape, dt, kind="ExternalOutput").ap())
    flamingo_block(nc, *args)
    r = _run(nc, [arrays], core_ids=[0])
    return r.results[0]["out_0_dram"]
```
